# Optimizing a Trainium2 kernel written in Bass

```python
import numpy as np
import jax
import jax.numpy as jnp

def _softmax(x, axis=-1):
    return jax.nn.softmax(x, axis=axis)

def _gelu(x):
    return jax.nn.gelu(x, approximate=True)

def _silu(x):
    return jax.nn.silu(x)

def _sigmoid(x):
    return jax.nn.sigmoid(x)

def _layernorm(x, axis=-1, eps=1e-05):
    m = jnp.mean(x, axis=axis, keepdims=True)
    v = jnp.var(x, axis=axis, keepdims=True)
    return (x - m) / jnp.sqrt(v + eps)

def _scatter_add(tgt, idx, src, axis=0):
    return tgt.at[idx].add(src)

def _segment_sum(src, seg, n):
    return jax.ops.segment_sum(src, seg, n)
kernel_name = 'mk_metaformer_d2_conv_nchw512_r4_e2f136'

def setup_inputs(seed: int=0):
    np.random.seed(seed)
    _w = jnp.asarray

    def _rec_inputs():
        import jax
        import jax.numpy as jnp
        _gk = jax.random.key(seed)
        x = -0.0002928 + 1 * jax.random.normal(jax.random.fold_in(_gk, 1), (8, 128, 32, 32), jnp.float32)
        return x
    x = _rec_inputs()

    def _L0_conv_setup():
        import jax, jax.numpy as jnp
        import numpy as np
        N_GROUPS = 32
        N_HEADS = 8
        GN_EPS = 1e-05
        key = jax.random.key(seed)
        k1, k2, k3 = jax.random.split(key, 3)
        B, C, H, W = (8, 128, 32, 32)
        x = jax.random.normal(k1, (B, C, H, W), dtype=jnp.float32)
        gn_w = jnp.ones((C,), dtype=jnp.float32)
        gn_b = jnp.zeros((C,), dtype=jnp.float32)
        qkv_w = jax.random.normal(k2, (3 * C, C), dtype=jnp.float32) * 0.02
        qkv_b = jnp.zeros((3 * C,), dtype=jnp.float32)
        proj_w = jax.random.normal(k3, (C, C), dtype=jnp.float32) * 0.02
        proj_b = jnp.zeros((C,), dtype=jnp.float32)
        return {'x': x, 'gn_w': gn_w, 'gn_b': gn_b, 'qkv_w': qkv_w, 'qkv_b': qkv_b, 'proj_w': proj_w, 'proj_b': proj_b}
    _L0_conv_all = _L0_conv_setup()
    _L0_conv_in = {k: v for k, v in _L0_conv_all.items() if k in ('gn_w', 'gn_b', 'qkv_w', 'qkv_b', 'proj_w', 'proj_b')}
    del _L0_conv_all

    def _L0_ffn_setup():
        import jax, jax.numpy as jnp
        import numpy as np
        B, S, D = (4, 512, 128)
        E, H, K = (8, 256, 2)

        def _moe_forward(x, router_w, router_b, w1, b1, wg, bg, wv, bv, w2, b2):
            b, s, d = x.shape
            xf = x.reshape(-1, d)
            T = xf.shape[0]
            scores = xf @ router_w + router_b
            probs = jax.nn.softmax(scores, axis=-1)
            topk_p, topk_i = jax.lax.top_k(probs, K)
            gates = jnp.zeros((T, E), xf.dtype).at[jnp.arange(T)[:, None], topk_i].set(topk_p)
            h = jnp.einsum('td,edh->teh', xf, w1) + b1[None]
            gated = jax.nn.silu(jnp.einsum('teh,ehf->tef', h, wg) + bg[None]) * (jnp.einsum('teh,ehf->tef', h, wv) + bv[None])
            y = jnp.einsum('tef,efd->ted', gated, w2) + b2[None]
            out = jnp.einsum('ted,te->td', y, gates)
            return out.reshape(b, s, d)
        key = jax.random.key(seed)
        ks = jax.random.split(key, 8)
        s_in = 0.02
        return {'x': jax.random.normal(ks[0], (B, S, D), jnp.float32), 'router_w': jax.random.normal(ks[1], (D, E), jnp.float32) * s_in, 'router_b': jnp.zeros((E,), jnp.float32), 'w1': jax.random.normal(ks[2], (E, D, H), jnp.float32) * s_in, 'b1': jnp.zeros((E, H), jnp.float32), 'wg': jax.random.normal(ks[3], (E, H, H), jnp.float32) * s_in, 'bg': jnp.zeros((E, H), jnp.float32), 'wv': jax.random.normal(ks[4], (E, H, H), jnp.float32) * s_in, 'bv': jnp.zeros((E, H), jnp.float32), 'w2': jax.random.normal(ks[5], (E, H, D), jnp.float32) * s_in, 'b2': jnp.zeros((E, D), jnp.float32)}
    _L0_ffn_all = _L0_ffn_setup()
    _L0_ffn_in = {k: v for k, v in _L0_ffn_all.items() if k in ('router_w', 'router_b', 'w1', 'b1', 'wg', 'bg', 'wv', 'bv', 'w2', 'b2')}
    del _L0_ffn_all

    def _L1_conv_setup():
        import jax, jax.numpy as jnp
        import numpy as np
        DIM = 16
        EPS = 1e-15
        BN_EPS = 1e-05

        def _conv(x, w, groups=1):
            return jax.lax.conv_general_dilated(x, w, window_strides=(1, 1), padding='SAME', feature_group_count=groups, dimension_numbers=('NCHW', 'OIHW', 'NCHW'))
        key = jax.random.key(seed)
        ks = jax.random.split(key, 5)
        B, Cin, H, W = (8, 128, 16, 16)
        total_dim = 128
        C3 = 3 * total_dim
        x = jax.random.normal(ks[0], (B, Cin, H, W), dtype=jnp.float32)
        w_qkv = jax.random.normal(ks[1], (C3, Cin, 1, 1), dtype=jnp.float32) * 0.02
        w_dw = jax.random.normal(ks[2], (C3, 1, 5, 5), dtype=jnp.float32) * 0.02
        w_pw = jax.random.normal(ks[3], (C3, C3 // (3 * DIM), 1, 1), dtype=jnp.float32) * 0.02
        w_proj = jax.random.normal(ks[4], (128, 2 * total_dim, 1, 1), dtype=jnp.float32) * 0.02
        bn_gamma = jnp.ones((128,), jnp.float32)
        bn_beta = jnp.zeros((128,), jnp.float32)
        bn_mean = jnp.zeros((128,), jnp.float32)
        bn_var = jnp.ones((128,), jnp.float32)
        return {'x': x, 'w_qkv': w_qkv, 'w_dw': w_dw, 'w_pw': w_pw, 'w_proj': w_proj, 'bn_gamma': bn_gamma, 'bn_beta': bn_beta, 'bn_mean': bn_mean, 'bn_var': bn_var}
    _L1_conv_all = _L1_conv_setup()
    _L1_conv_in = {k: v for k, v in _L1_conv_all.items() if k in ('w_qkv', 'w_dw', 'w_pw', 'w_proj', 'bn_gamma', 'bn_beta', 'bn_mean', 'bn_var')}
    del _L1_conv_all

    def _L1_ffn_setup():
        import jax, jax.numpy as jnp
        import numpy as np
        NUM_EXPERTS = 8
        TOP_K = 2
        LN_EPS = 1e-05

        def _layernorm(x, g, b):
            mu = jnp.mean(x, axis=-1, keepdims=True)
            var = jnp.mean(jnp.square(x - mu), axis=-1, keepdims=True)
            return (x - mu) * jax.lax.rsqrt(var + LN_EPS) * g + b
        key = jax.random.key(seed)
        ks = jax.random.split(key, 8)
        B, S, D, F, E = (8, 1024, 128, 512, NUM_EXPERTS)
        return {'x': jax.random.normal(ks[0], (B, S, D), dtype=jnp.float32), 'gate_w': jax.random.normal(ks[1], (D, E), dtype=jnp.float32) * 0.02, 'w1': jax.random.normal(ks[2], (E, D, F), dtype=jnp.float32) * 0.02, 'b1': jnp.zeros((E, F), dtype=jnp.float32), 'w2': jax.random.normal(ks[3], (E, F, D), dtype=jnp.float32) * 0.02, 'b2': jnp.zeros((E, D), dtype=jnp.float32), 'ln_g': jnp.ones((D,), dtype=jnp.float32), 'ln_b': jnp.zeros((D,), dtype=jnp.float32)}
    _L1_ffn_all = _L1_ffn_setup()
    _L1_ffn_in = {k: v for k, v in _L1_ffn_all.items() if k in ('gate_w', 'w1', 'b1', 'w2', 'b2', 'ln_g', 'ln_b')}
    del _L1_ffn_all
    return {'x': x, 'L0_conv_gn_w': _L0_conv_in['gn_w'], 'L0_conv_gn_b': _L0_conv_in['gn_b'], 'L0_conv_qkv_w': _L0_conv_in['qkv_w'], 'L0_conv_qkv_b': _L0_conv_in['qkv_b'], 'L0_conv_proj_w': _L0_conv_in['proj_w'], 'L0_conv_proj_b': _L0_conv_in['proj_b'], 'L0_ffn_router_w': _L0_ffn_in['router_w'], 'L0_ffn_router_b': _L0_ffn_in['router_b'], 'L0_ffn_w1': _L0_ffn_in['w1'], 'L0_ffn_b1': _L0_ffn_in['b1'], 'L0_ffn_wg': _L0_ffn_in['wg'], 'L0_ffn_bg': _L0_ffn_in['bg'], 'L0_ffn_wv': _L0_ffn_in['wv'], 'L0_ffn_bv': _L0_ffn_in['bv'], 'L0_ffn_w2': _L0_ffn_in['w2'], 'L0_ffn_b2': _L0_ffn_in['b2'], 'L1_conv_w_qkv': _L1_conv_in['w_qkv'], 'L1_conv_w_dw': _L1_conv_in['w_dw'], 'L1_conv_w_pw': _L1_conv_in['w_pw'], 'L1_conv_w_proj': _L1_conv_in['w_proj'], 'L1_conv_bn_gamma': _L1_conv_in['bn_gamma'], 'L1_conv_bn_beta': _L1_conv_in['bn_beta'], 'L1_conv_bn_mean': _L1_conv_in['bn_mean'], 'L1_conv_bn_var': _L1_conv_in['bn_var'], 'L1_ffn_gate_w': _L1_ffn_in['gate_w'], 'L1_ffn_w1': _L1_ffn_in['w1'], 'L1_ffn_b1': _L1_ffn_in['b1'], 'L1_ffn_w2': _L1_ffn_in['w2'], 'L1_ffn_b2': _L1_ffn_in['b2'], 'L1_ffn_ln_g': _L1_ffn_in['ln_g'], 'L1_ffn_ln_b': _L1_ffn_in['ln_b']}

def reference(x, L0_conv_gn_w, L0_conv_gn_b, L0_conv_qkv_w, L0_conv_qkv_b, L0_conv_proj_w, L0_conv_proj_b, L0_ffn_router_w, L0_ffn_router_b, L0_ffn_w1, L0_ffn_b1, L0_ffn_wg, L0_ffn_bg, L0_ffn_wv, L0_ffn_bv, L0_ffn_w2, L0_ffn_b2, L1_conv_w_qkv, L1_conv_w_dw, L1_conv_w_pw, L1_conv_w_proj, L1_conv_bn_gamma, L1_conv_bn_beta, L1_conv_bn_mean, L1_conv_bn_var, L1_ffn_gate_w, L1_ffn_w1, L1_ffn_b1, L1_ffn_w2, L1_ffn_b2, L1_ffn_ln_g, L1_ffn_ln_b):
    import jax
    import jax.numpy as jnp

    def _L0_conv_ref(x, gn_w, gn_b, qkv_w, qkv_b, proj_w, proj_b):
        import jax, jax.numpy as jnp
        import numpy as np
        N_GROUPS = 32
        N_HEADS = 8
        GN_EPS = 1e-05
        b, c, h, w = x.shape
        t = h * w
        xf = x.reshape(b, c, t)
        xg = xf.reshape(b, N_GROUPS, c // N_GROUPS * t)
        mean = jnp.mean(xg, axis=-1, keepdims=True)
        var = jnp.var(xg, axis=-1, keepdims=True)
        normed = ((xg - mean) * jax.lax.rsqrt(var + GN_EPS)).reshape(b, c, t)
        normed = normed * gn_w[None, :, None] + gn_b[None, :, None]
        qkv = jnp.einsum('oc,bct->bot', qkv_w, normed) + qkv_b[None, :, None]
        q, k, v = jnp.split(qkv, 3, axis=1)
        ch = c // N_HEADS
        scale = 1.0 / np.sqrt(np.sqrt(ch)).astype(np.float32)
        q = (q * scale).reshape(b * N_HEADS, ch, t)
        k = (k * scale).reshape(b * N_HEADS, ch, t)
        v = v.reshape(b * N_HEADS, ch, t)
        weight = jnp.einsum('bct,bcs->bts', q, k)
        weight = jax.nn.softmax(weight.astype(jnp.float32), axis=-1).astype(q.dtype)
        a = jnp.einsum('bts,bcs->bct', weight, v).reshape(b, c, t)
        out = jnp.einsum('oc,bct->bot', proj_w, xf + a) + proj_b[None, :, None]
        return out.reshape(b, -1, h, w)

    def _L0_ffn_ref(x, router_w, router_b, w1, b1, wg, bg, wv, bv, w2, b2):
        import jax, jax.numpy as jnp
        import numpy as np
        B, S, D = (4, 512, 128)
        E, H, K = (8, 256, 2)

        def _moe_forward(x, router_w, router_b, w1, b1, wg, bg, wv, bv, w2, b2):
            b, s, d = x.shape
            xf = x.reshape(-1, d)
            T = xf.shape[0]
            scores = xf @ router_w + router_b
            probs = jax.nn.softmax(scores, axis=-1)
            topk_p, topk_i = jax.lax.top_k(probs, K)
            gates = jnp.zeros((T, E), xf.dtype).at[jnp.arange(T)[:, None], topk_i].set(topk_p)
            h = jnp.einsum('td,edh->teh', xf, w1) + b1[None]
            gated = jax.nn.silu(jnp.einsum('teh,ehf->tef', h, wg) + bg[None]) * (jnp.einsum('teh,ehf->tef', h, wv) + bv[None])
            y = jnp.einsum('tef,efd->ted', gated, w2) + b2[None]
            out = jnp.einsum('ted,te->td', y, gates)
            return out.reshape(b, s, d)
        return _moe_forward(x, router_w, router_b, w1, b1, wg, bg, wv, bv, w2, b2)

    def _L1_conv_ref(x, w_qkv, w_dw, w_pw, w_proj, bn_gamma, bn_beta, bn_mean, bn_var):
        import jax, jax.numpy as jnp
        import numpy as np
        DIM = 16
        EPS = 1e-15
        BN_EPS = 1e-05

        def _conv(x, w, groups=1):
            return jax.lax.conv_general_dilated(x, w, window_strides=(1, 1), padding='SAME', feature_group_count=groups, dimension_numbers=('NCHW', 'OIHW', 'NCHW'))
        qkv = _conv(x, w_qkv)
        C3 = qkv.shape[1]
        agg = _conv(_conv(qkv, w_dw, groups=C3), w_pw, groups=3 * DIM)
        qkv = jnp.concatenate([qkv, agg], axis=1)
        B, _, H, W = qkv.shape
        S = H * W
        qkv = qkv.reshape(B, -1, 3 * DIM, S)
        q, k, v = jnp.split(qkv, 3, axis=2)
        q = jax.nn.relu(q)
        k = jax.nn.relu(k)
        v = jnp.concatenate([v, jnp.ones_like(v[:, :, :1])], axis=2)
        vk = jnp.einsum('bhds,bhes->bhde', v, k)
        out = jnp.einsum('bhde,bhes->bhds', vk, q)
        out = out[:, :, :-1] / (out[:, :, -1:] + EPS)
        out = out.reshape(B, -1, H, W)
        y = _conv(out, w_proj)
        inv = bn_gamma / jnp.sqrt(bn_var + BN_EPS)
        y = y * inv[:, None, None] + (bn_beta - bn_mean * inv)[:, None, None]
        return y

    def _L1_ffn_ref(x, gate_w, w1, b1, w2, b2, ln_g, ln_b):
        import jax, jax.numpy as jnp
        import numpy as np
        NUM_EXPERTS = 8
        TOP_K = 2
        LN_EPS = 1e-05

        def _layernorm(x, g, b):
            mu = jnp.mean(x, axis=-1, keepdims=True)
            var = jnp.mean(jnp.square(x - mu), axis=-1, keepdims=True)
            return (x - mu) * jax.lax.rsqrt(var + LN_EPS) * g + b
        B, S, D = x.shape
        E = gate_w.shape[1]
        x_norm = _layernorm(x, ln_g, ln_b)
        xf = x_norm.reshape(B * S, D)
        logits = xf @ gate_w
        probs = jax.nn.softmax(logits, axis=-1)
        dispatch_w, expert_idx = jax.lax.top_k(probs, TOP_K)
        combine = jnp.sum(jax.nn.one_hot(expert_idx, E, dtype=xf.dtype) * dispatch_w[..., None], axis=1)
        out = jnp.zeros_like(xf)
        for e in range(E):
            h = jax.nn.gelu(xf @ w1[e] + b1[e], approximate=False)
            y = h @ w2[e] + b2[e]
            out = out + combine[:, e:e + 1] * y
        return x + out.reshape(B, S, D)

    def _gn(v, G=32, eps=1e-05):
        B_, C_, H_, W_ = v.shape
        g = v.reshape(B_, G, C_ // G, H_, W_)
        m = jnp.mean(g, axis=(2, 3, 4), keepdims=True)
        s = jnp.var(g, axis=(2, 3, 4), keepdims=True)
        return ((g - m) / jnp.sqrt(s + eps)).reshape(v.shape)

    def _ln_c(v, eps=1e-06):
        m = jnp.mean(v, axis=1, keepdims=True)
        s = jnp.var(v, axis=1, keepdims=True)
        return (v - m) / jnp.sqrt(s + eps)

    def _ln_t(v, eps=1e-05):
        m = jnp.mean(v, axis=-1, keepdims=True)
        s = jnp.var(v, axis=-1, keepdims=True)
        return (v - m) / jnp.sqrt(s + eps)

    def _to_tokens(v):
        B_, C_, H_, W_ = v.shape
        return v.reshape(B_, C_, H_ * W_).transpose(0, 2, 1)

    def _from_tokens(t, like):
        B_, C_, H_, W_ = like.shape
        return t.transpose(0, 2, 1).reshape(B_, C_, H_, W_)
    x = x + _L0_conv_ref(_ln_c(x), L0_conv_gn_w, L0_conv_gn_b, L0_conv_qkv_w, L0_conv_qkv_b, L0_conv_proj_w, L0_conv_proj_b)
    t = _to_tokens(x)
    t = t + _L0_ffn_ref(_ln_t(t), L0_ffn_router_w, L0_ffn_router_b, L0_ffn_w1, L0_ffn_b1, L0_ffn_wg, L0_ffn_bg, L0_ffn_wv, L0_ffn_bv, L0_ffn_w2, L0_ffn_b2)
    x = _from_tokens(t, x)
    x = x + _L1_conv_ref(_ln_c(x), L1_conv_w_qkv, L1_conv_w_dw, L1_conv_w_pw, L1_conv_w_proj, L1_conv_bn_gamma, L1_conv_bn_beta, L1_conv_bn_mean, L1_conv_bn_var)
    t = _to_tokens(x)
    t = t + _L1_ffn_ref(_ln_t(t), L1_ffn_gate_w, L1_ffn_w1, L1_ffn_b1, L1_ffn_w2, L1_ffn_b2, L1_ffn_ln_g, L1_ffn_ln_b)
    x = _from_tokens(t, x)
    return x

_drawn_inputs = setup_inputs


def setup_inputs(seed=0):
    import zlib

    import numpy as np

    out = dict(_drawn_inputs(seed))
    spreads = {'L0_conv_gn_w': (1.0, 0.6),
     'L0_conv_gn_b': (0.0, 0.8),
     'L0_conv_qkv_b': (0.0, 0.314),
     'L0_conv_proj_b': (0.0, 0.1),
     'L0_ffn_router_b': (0.0, 0.704),
     'L0_ffn_b1': (0.0, 0.8),
     'L0_ffn_bg': (0.0, 0.8),
     'L0_ffn_bv': (0.0, 0.8),
     'L0_ffn_b2': (0.0, 2.0),
     'L1_conv_bn_gamma': (1.0, 0.6),
     'L1_conv_bn_beta': (0.0, 0.8),
     'L1_conv_bn_mean': (0.0, 0.751),
     'L1_conv_bn_var': (1.0, 0.6),
     'L1_ffn_b1': (0.0, 0.8),
     'L1_ffn_b2': (0.0, 2.0),
     'L1_ffn_ln_g': (1.0, 0.6),
     'L1_ffn_ln_b': (0.0, 0.8)}
    factors = {'L0_conv_qkv_w': 8.0,
     'L0_ffn_router_w': 3.007,
     'L0_ffn_w1': 8.0,
     'L0_ffn_wg': 8.0,
     'L0_ffn_wv': 8.0,
     'L0_ffn_w2': 8.0,
     'L1_conv_w_qkv': 8.0,
     'L1_conv_w_dw': 8.0,
     'L1_conv_w_pw': 8.0,
     'L1_conv_w_proj': 8.0,
     'L1_ffn_gate_w': 4.726,
     'L1_ffn_w1': 8.0,
     'L1_ffn_w2': 8.0}
    for name, (base, spread) in spreads.items():
        noise = np.random.default_rng([zlib.crc32(name.encode()), seed]).standard_normal(out[name].shape)
        drawn = base * np.exp(spread * noise) if base else spread * noise
        out[name] = jnp.asarray(drawn.astype(out[name].dtype))
    for name, factor in factors.items():
        out[name] = (out[name] * factor).astype(out[name].dtype)
    return out
```

```python
from contextlib import ExitStack

import numpy as np
import concourse.bass as bass
from concourse import mybir

F32 = mybir.dt.float32
BF16 = mybir.dt.bfloat16
ALU = mybir.AluOpType
ACT = mybir.ActivationFunctionType
AX = mybir.AxisListType

C = 128
B = 8
T = 1024
HALF = 512
HEADS = 8
CH = C // HEADS
VH = 2 * CH
TC = T // C
QK_SCALE = 0.5
Q_PARTS = (0, 0, 0, 1, 1, 2)
K_PARTS = (0, 1, 2, 0, 1, 0)
KB = len(Q_PARTS) * CH
KM = KB + 3


LN_EXP_TABLES = 6


def load_tables(nc, act, tables):
    act.add_instruction(mybir.InstLoadActFuncSet(name=nc.get_next_instruction_name(), ins=[], outs=[],
                                                 engine=mybir.EngineType.Activation, act_func_set_id=tables))


def split_in_three(eng, value, rest, parts, done, b, held=None):
    if held is not None:
        eng.sem_inc(held, 1)
    eng.tensor_copy(parts[:, 0], value).then_inc(done, 1)
    eng.wait_ge(done, b * 4 + 1)
    eng.tensor_tensor(rest, value, parts[:, 0], ALU.subtract).then_inc(done, 1)
    eng.wait_ge(done, b * 4 + 2)
    if held is not None:
        eng.sem_inc(held, 1)
    eng.tensor_copy(parts[:, 1], rest).then_inc(done, 1)
    eng.wait_ge(done, b * 4 + 3)
    eng.tensor_tensor(parts[:, 2], rest, parts[:, 1], ALU.subtract).then_inc(done, 1)


def normalize_and_project(nc, sb, sem, bank, w, X, XF, x_in, parts_dram, v_dram):
    xc = sb("xc", [C, T], F32)
    sq = sb("sq", [C, T], F32)
    rstd = sb("rstd", [C, T], F32)
    normed = sb("normed", [C, T], F32)
    qk = sb("qk", [C, 2, T], F32)
    rest = sb("rest", [C, 2, T], F32)
    parts = sb("parts", [C, 2, 3, T], BF16)
    vt = sb("vt", [C, TC * HEADS * VH], F32)
    bqk = sb("bqk", [C, 2], F32)
    bn = sb("bn", [C, 2, 6], F32)
    mv = sb("mv", [C, 3], F32)
    gmean = sb("gmean", [C, 1], F32)
    gvar = sb("gvar", [C, 1], F32)
    gmean2 = sb("gmean2", [C, 1], F32)
    glog = sb("glog", [C, 1], F32)
    grs = sb("grs", [C, 1], F32)
    ga = sb("ga", [C, 1], F32)
    gma = sb("gma", [C, 1], F32)
    gb = sb("gb", [C, 1], F32)
    x_loaded, bias_scaled = sem("x_loaded"), sem("bias_scaled")
    centred, xc_copied, squared, var_ready = sem("centred"), sem("xc_copied"), sem("squared"), sem("var_ready")
    ln_logged, rstd_ready, xf_ready = sem("ln_logged"), sem("rstd_ready"), sem("xf_ready")
    stats_part, stats_ready, group_ready = sem("stats_part"), sem("stats_ready"), sem("group_ready")
    gmean_ready, gvar_ready, g_logged, grs_ready = sem("gmean_ready"), sem("gvar_ready"), sem("g_logged"), sem("grs_ready")
    gab_ready, normed_ready, qk_ready, qk_biased = sem("gab_ready"), sem("normed_ready"), sem("qk_ready"), sem("qk_biased")
    q_split, k_split, stored = sem("q_split"), sem("k_split"), sem("stored")
    v_ready, v_copied, held, stats_held = sem("v_ready"), sem("v_copied"), sem("held"), sem("stats_held")

    with nc.Block() as block:
        @block.sync
        def _(sp):
            for b in range(B):
                sp.dma_start(X[:, b * T:(b + 1) * T], x_in[b]).then_inc(x_loaded, 16)
            with sp.Fori(0, B) as b:
                sp.wait_ge(q_split, b * 4 + 4)
                sp.wait_ge(k_split, b * 4 + 4)
                sp.dma_start(parts_dram[bass.ds(b, 1)].rearrange("o s w c t -> c (o s w) t"),
                             parts[:].rearrange("c s w t -> c (s w) t")).then_inc(stored, 16)
                sp.wait_ge(v_copied, b * 4 + 4)
                sp.dma_start(v_dram[bass.ds(b, 1)].rearrange("o c n -> c (o n)"), vt[:]).then_inc(stored, 16)
            sp.wait_ge(stored, 32 * B)

        @block.tensor
        def _(pe):
            pe.wait_ge(w.loaded, 16 * w.count)
            pe.wait_ge(x_loaded, 16 * B)
            with pe.Fori(0, B) as b:
                pe.wait_ge(qk_biased, b * 4)
                for n in range(2):
                    pe.matmul(bank[:, n, :], w["centre"], X[:, bass.ds(b * T + n * HALF, HALF)],
                              start=True, stop=True).then_inc(centred, 1)
                for n in range(2):
                    pe.wait_ge(squared, b * 2 + n + 1)
                    pe.matmul(bank[:, 2 + n, :], w["mean"], sq[:, n * HALF:(n + 1) * HALF],
                              start=True, stop=True).then_inc(var_ready, 1)
                pe.wait_ge(v_copied, b * 4)
                pe.wait_ge(stats_ready, b + 1)
                pe.matmul(bank[:, 4, 0:3], w["group"], mv[:], start=True, stop=True).then_inc(group_ready, 1)
                pe.wait_ge(normed_ready, b + 1)
                for s in range(2):
                    for n in range(2):
                        pe.matmul(bank[:, 2 * s + n, :], w["wqk"][:, s * C:(s + 1) * C],
                                  normed[:, n * HALF:(n + 1) * HALF], start=True, stop=True).then_inc(qk_ready, 1)
                for p in range(4):
                    for u in range(2):
                        c = 2 * p + u
                        ins = pe.matmul(bank[:, 4 + p, 256 * u:256 * u + 256], normed[:, c * C:(c + 1) * C],
                                        w["wv"], start=True, stop=True)
                    ins.then_inc(v_ready, 1)

        @block.scalar
        def _(act):
            act.wait_ge(w.loaded, 16 * w.count)
            act.activation(bqk[:], w["bqk"], ACT.Copy, scale=QK_SCALE).then_inc(bias_scaled, 1)
            act.wait_ge(bias_scaled, 1)
            with act.Fori(0, B) as b:
                act.wait_ge(var_ready, b * 2)
                for n in range(2):
                    act.wait_ge(xc_copied, b * 2 + n + 1)
                    act.activation(sq[:, n * HALF:(n + 1) * HALF], xc[:, n * HALF:(n + 1) * HALF], ACT.Square).then_inc(squared, 1)
                act.wait_ge(xf_ready, b * 2)
                for n in range(2):
                    act.wait_ge(var_ready, b * 2 + n + 1)
                    act.activation(rstd[:, n * HALF:(n + 1) * HALF], bank[:, 2 + n, :], ACT.Ln,
                                   bias=w["eps"][:, 0:1]).then_inc(ln_logged, 1)
                for n in range(2):
                    act.wait_ge(ln_logged, b * 2 + n + 1)
                    act.activation(rstd[:, n * HALF:(n + 1) * HALF], rstd[:, n * HALF:(n + 1) * HALF], ACT.Exp,
                                   scale=-0.5).then_inc(rstd_ready, 1)
                act.wait_ge(gvar_ready, b + 1)
                act.activation(glog[:], gvar[:], ACT.Ln, bias=w["eps"][:, 1:2]).then_inc(g_logged, 1)
                act.wait_ge(g_logged, b + 1)
                act.activation(grs[:], glog[:], ACT.Exp, scale=-0.5).then_inc(grs_ready, 1)
                act.wait_ge(q_split, b * 4)
                act.wait_ge(k_split, b * 4)
                for s in range(2):
                    for n in range(2):
                        act.wait_ge(qk_ready, b * 4 + 2 * s + n + 1)
                        act.activation(qk[:, s, n * HALF:(n + 1) * HALF], bank[:, 2 * s + n, :], ACT.Identity,
                                       bias=bqk[:, s:s + 1], scale=QK_SCALE).then_inc(qk_biased, 1)

        @block.vector
        def _(dve):
            dve.wait_ge(w.loaded, 16 * w.count)
            with dve.Fori(0, B) as b:
                for n in range(2):
                    dve.wait_ge(centred, b * 2 + n + 1)
                    dve.tensor_copy(xc[:, n * HALF:(n + 1) * HALF], bank[:, n, :]).then_inc(xc_copied, 1)
                for n in range(2):
                    dve.wait_ge(xc_copied, b * 2 + n + 1)
                    dve.wait_ge(rstd_ready, b * 2 + n + 1)
                    dve.tensor_tensor(XF[:, bass.ds(b * T + n * HALF, HALF)], xc[:, n * HALF:(n + 1) * HALF],
                                      rstd[:, n * HALF:(n + 1) * HALF], ALU.mult).then_inc(xf_ready, 1)
                for n in range(2):
                    dve.wait_ge(xf_ready, b * 2 + n + 1)
                    dve.sem_inc(stats_held, 1)
                    dve.bn_stats(bn[:, n, :], XF[:, bass.ds(b * T + n * HALF, HALF)]).then_inc(stats_part, 1)
                dve.wait_ge(stats_part, b * 3 + 2)
                dve.sem_inc(stats_held, 1)
                dve.bn_aggr(mv[:, 0:2], bn[:]).then_inc(stats_part, 1)
                dve.wait_ge(stats_part, b * 3 + 3)
                dve.scalar_tensor_tensor(out=mv[:, 2:3], in0=mv[:, 0:1], scalar=mv[:, 0:1], in1=mv[:, 1:2],
                                         op0=ALU.mult, op1=ALU.add).then_inc(stats_ready, 1)
                dve.wait_ge(group_ready, b + 1)
                dve.tensor_copy(gmean[:], bank[:, 4, 0:1]).then_inc(gmean_ready, 1)
                dve.wait_ge(gmean_ready, b * 2 + 1)
                dve.tensor_tensor(gmean2[:], gmean[:], gmean[:], ALU.mult).then_inc(gmean_ready, 1)
                dve.wait_ge(gmean_ready, b * 2 + 2)
                dve.tensor_tensor(gvar[:], bank[:, 4, 2:3], gmean2[:], ALU.subtract).then_inc(gvar_ready, 1)
                dve.wait_ge(grs_ready, b + 1)
                dve.tensor_tensor(ga[:], grs[:], w["gn"][:, 0:1], ALU.mult).then_inc(gab_ready, 1)
                dve.wait_ge(gab_ready, b * 3 + 1)
                dve.tensor_tensor(gma[:], gmean[:], ga[:], ALU.mult).then_inc(gab_ready, 1)
                dve.wait_ge(gab_ready, b * 3 + 2)
                dve.tensor_tensor(gb[:], w["gn"][:, 1:2], gma[:], ALU.subtract).then_inc(gab_ready, 1)
                dve.wait_ge(gab_ready, b * 3 + 3)
                dve.wait_ge(v_ready, b * 4)
                dve.tensor_scalar(normed[:], XF[:, bass.ds(b * T, T)], ga[:, 0:1], gb[:, 0:1],
                                  ALU.mult, ALU.add).then_inc(normed_ready, 1)
                dve.wait_ge(qk_biased, b * 4 + 2)
                dve.wait_ge(stored, b * 32)
                split_in_three(dve, qk[:, 0, :], rest[:, 0, :], parts[:, 0], q_split, b)
                for p in range(4):
                    dve.wait_ge(v_ready, b * 4 + p + 1)
                    dve.tensor_tensor(vt[:, p * HALF:(p + 1) * HALF], bank[:, 4 + p, :], w["bv"],
                                      ALU.add).then_inc(v_copied, 1)

        @block.gpsimd
        def _(pool):
            with pool.Fori(0, B) as b:
                pool.wait_ge(qk_biased, b * 4 + 4)
                pool.wait_ge(stored, b * 32)
                split_in_three(pool, qk[:, 1, :], rest[:, 1, :], parts[:, 1], k_split, b, held)


STEPS = 32
UNITS = 130
SLOTS = 4


def max_unit(u):
    if u in (64, 129):
        return None
    k = u - (u > 64)
    return k // 16, k // 2 % TC, k % 2


def attention(nc, sb, sem, bank, w, X, XF, parts_dram, v_dram):
    qs = sb("qs", [KM, 2, HEADS, T], BF16)
    ks = sb("ks", [KM, 2, HEADS, T], BF16)
    vt = sb("vt", [C, 2, TC, HEADS * VH], F32)
    P = sb("P", [C, SLOTS, 2 * HALF], F32)
    mx = sb("mx", [C, 64, 2], F32)
    nm = sb("nm", [C, 64], F32)
    nmT = sb("nmT", [32, C], F32)
    nm_rest = sb("nm_rest", [32, C], F32)
    nm_parts = sb("nm_parts", [32, 3, C], BF16)
    o = sb("o", [C, HALF], F32)
    den = sb("den", [C, HALF], F32)
    rden = sb("rden", [C, HALF], F32)
    a = sb("a", [C, 2, T], F32)
    ones_set, qk_loaded, rows_loaded = sem("ones_set"), sem("qk_loaded"), sem("rows_loaded")
    max_filled, max_freed, negated, rows_split = sem("max_filled"), sem("max_freed"), sem("negated"), sem("rows_split")
    scores_ready, probs_ready, pv_done = sem("scores_ready"), sem("probs_ready"), sem("pv_done")
    o_copied, den_ready, den_logged, rden_ready, a_ready = (
        sem("o_copied"), sem("den_ready"), sem("den_logged"), sem("rden_ready"), sem("a_ready"))
    proj_ready, image_done, held = sem("proj_ready"), sem("image_done"), sem("held")
    LOADS = len(Q_PARTS) + len(K_PARTS) + 1

    def over_images(eng, first, body):
        first()
        with eng.Fori(0, B // 2 - 1) as i:
            body(2 * i, 0, True)
            body(2 * i + 1, 1, True)
        body(B - 2, 0, True)
        body(B - 1, 1, False)

    def units_of(e):
        return range(e * UNITS // STEPS, (e + 1) * UNITS // STEPS)

    with nc.Block() as block:
        @block.sync
        def _(sp):
            def load(b, par):
                for r, (qp, kp) in enumerate(zip(Q_PARTS, K_PARTS)):
                    for s, part, stack in ((0, qp, qs), (1, kp, ks)):
                        src = parts_dram[bass.ds(b, 1), s, part].rearrange("o (h i) t -> i (o h) t", i=CH)
                        sp.dma_start(stack[r * CH:(r + 1) * CH, par], src).then_inc(qk_loaded, 16)
                sp.dma_start(vt[:, par].rearrange("c s n -> c (s n)"),
                             v_dram[bass.ds(b, 1)].rearrange("o c n -> c (o n)")).then_inc(qk_loaded, 16)

            def max_rows(b, par, g):
                sp.wait_ge(rows_split, b * 8 + 4 * g + 4)
                for part in range(3):
                    sp.dma_start(qs[KB + part:KB + part + 1, par, 4 * g:4 * g + 4, :]
                                 .rearrange("p h (c t) -> p (h c) t", t=C),
                                 nm_parts[:, part, :]).then_inc(rows_loaded, 16)

            def first():
                load(0, 0)
                max_rows(0, 0, 0)
                max_rows(0, 0, 1)

            def body(b, par, more):
                if more:
                    sp.wait_ge(pv_done, b * STEPS)
                    load(b + 1, 1 - par)
                    max_rows(b + 1, 1 - par, 0)
                    max_rows(b + 1, 1 - par, 1)

            over_images(sp, first, body)

        @block.tensor
        def _(pe):
            def take_max(b, par, u):
                slot = 5 + u % 3
                pe.wait_ge(max_freed, b * UNITS + (u - 2 if u >= 3 else 0))
                unit = max_unit(u)
                if unit is None:
                    g = u // 128
                    pe.wait_ge(negated, b * 2 + g + 1)
                    pe.transpose(bank[0:32, slot, 0:C], nm[:, 32 * g:32 * g + 32], w["ident"]).then_inc(max_filled, 1)
                    return
                h, c, half = unit
                pe.matmul(bank[:, slot, :], qs[0:KB, par, h, c * C:(c + 1) * C],
                          ks[0:KB, par, h, half * HALF:(half + 1) * HALF], start=True, stop=True).then_inc(max_filled, 1)

            def first():
                pe.wait_ge(w.loaded, 16 * w.count)
                pe.wait_ge(ones_set, 1)
                pe.wait_ge(qk_loaded, 16 * LOADS)
                for u in range(UNITS):
                    take_max(0, 0, u)

            def weigh(b, par, e):
                g, n, s = e // 16, e // 8 % 2, e % 8
                pe.wait_ge(probs_ready, b * 2 * STEPS + 2 * e + 2)
                if s == 0:
                    pe.wait_ge(o_copied, b * 4 + 2 * g + n)
                for j in range(4):
                    head = 4 * g + j
                    ins = pe.matmul(bank[32 * j:32 * j + 32, 4, :], vt[:, par, s, head * VH:(head + 1) * VH],
                                    P[:, (2 * e + j // 2) % SLOTS, j % 2 * HALF:(j % 2 + 1) * HALF],
                                    start=(s == 0), stop=(s == 7))
                ins.then_inc(pv_done, 1)

            def body(b, par, more):
                pe.wait_ge(image_done, b * 2)
                if more:
                    pe.wait_ge(qk_loaded, (b + 2) * 16 * LOADS)
                for e in range(STEPS):
                    g, n, s = e // 16, e // 8 % 2, e % 8
                    if e % 16 == 0:
                        pe.wait_ge(rows_loaded, b * 96 + 48 * g + 48)
                    units = list(units_of(e)) if more else []
                    for pair in range(2):
                        x = 2 * e + pair
                        pe.wait_ge(probs_ready, b * 2 * STEPS + max(x - 1, 0))
                        for u in range(2):
                            head = 4 * g + 2 * pair + u
                            ins = pe.matmul(bank[:, 2 * pair + u, :], ks[:, par, head, s * C:(s + 1) * C],
                                            qs[:, par, head, n * HALF:(n + 1) * HALF], start=True, stop=True)
                        ins.then_inc(scores_ready, 1)
                        for u in units[2 * pair:2 * pair + 2 + 3 * pair]:
                            take_max(b + 1, 1 - par, u)
                    if e:
                        weigh(b, par, e - 1)
                weigh(b, par, STEPS - 1)
                for n in range(2):
                    pe.matmul(bank[:, n, :], w["wproj"], XF[:, bass.ds(b * T + n * HALF, HALF)], start=True, stop=False)
                pe.wait_ge(a_ready, b * 4 + 4)
                for n in range(2):
                    for g in range(2):
                        ins = pe.matmul(bank[:, n, :], w["wproj_heads"][:, g * C:(g + 1) * C],
                                        a[:, g, n * HALF:(n + 1) * HALF], start=False, stop=(g == 1))
                    ins.then_inc(proj_ready, 1)

            over_images(pe, first, body)

        @block.scalar
        def _(act):
            def reciprocal(b, q):
                act.wait_ge(den_ready, b * 4 + q + 1)
                act.wait_ge(a_ready, b * 4 + q)
                act.activation(rden[:], den[:], ACT.Ln).then_inc(den_logged, 1)
                act.wait_ge(den_logged, b * 4 + q + 1)
                act.activation(rden[:], rden[:], ACT.Exp, scale=-1.0).then_inc(rden_ready, 1)

            def body(b, par, more):
                for e in range(STEPS):
                    act.wait_ge(pv_done, b * STEPS + max(e - 1, 0))
                    for pair in range(2):
                        x = 2 * e + pair
                        act.wait_ge(scores_ready, b * 2 * STEPS + x + 1)
                        act.activation(P[:, x % SLOTS, :], bank[:, 2 * pair:2 * pair + 2, :]
                                       .rearrange("p a t -> p (a t)"), ACT.Exp).then_inc(probs_ready, 1)
                    if e % 8 == 2 and e >= 8:
                        reciprocal(b, e // 8 - 1)
                reciprocal(b, 3)

            over_images(act, lambda: None, body)

        @block.vector
        def _(dve):
            def reduce(b, u):
                slot = 5 + u % 3
                unit = max_unit(u)
                dve.wait_ge(max_filled, b * UNITS + u + 1)
                if unit is not None:
                    h, c, half = unit
                    dve.tensor_reduce(mx[:, h * TC + c, half:half + 1], bank[:, slot, :], AX.X, ALU.max).then_inc(max_freed, 1)
                    if u in (63, 128):
                        g = u // 128
                        dve.wait_ge(max_freed, b * UNITS + u + 1)
                        dve.tensor_reduce(nm[:, 32 * g:32 * g + 32], mx[:, 32 * g:32 * g + 32, :], AX.X, ALU.max,
                                          negate=True).then_inc(negated, 1)
                    return
                g = u // 128
                dve.tensor_copy(nmT[:], bank[0:32, slot, 0:C]).then_inc(max_freed, 1)
                dve.wait_ge(max_freed, b * UNITS + u + 1)
                dve.wait_ge(rows_loaded, b * 96 + 48 * g)
                split_in_three(dve, nmT[:], nm_rest[:], nm_parts[:], rows_split, b * 2 + g)

            def first():
                for u in range(UNITS):
                    reduce(0, u)

            def quarter(b, q):
                dve.wait_ge(pv_done, b * STEPS + 8 * q + 8)
                dve.wait_ge(a_ready, b * 4 + q)
                dve.tensor_copy(o[:], bank[:, 4, :]).then_inc(o_copied, 1)
                dve.wait_ge(o_copied, b * 4 + q + 1)
                dve.wait_ge(den_logged, b * 4 + q)
                dve.sem_inc(held, 1)
                dve.stream_shuffle(den[:], o[:], [CH + i % CH for i in range(32)]).then_inc(den_ready, 1)

            def divide(b, q):
                dve.wait_ge(rden_ready, b * 4 + q + 1)
                if q == 0:
                    dve.wait_ge(image_done, b * 2)
                g, n = q // 2, q % 2
                dve.tensor_tensor(a[:, g, n * HALF:(n + 1) * HALF], o[:], rden[:], ALU.mult).then_inc(a_ready, 1)

            def body(b, par, more):
                for e in range(STEPS):
                    for u in units_of(e) if more else ():
                        reduce(b + 1, u)
                    if e % 8 == 1 and e >= 8:
                        quarter(b, e // 8 - 1)
                    if e % 8 == 4 and e >= 8:
                        divide(b, e // 8 - 1)
                quarter(b, 3)
                divide(b, 3)
                for n in range(2):
                    cols = X[:, bass.ds(b * T + n * HALF, HALF)]
                    dve.wait_ge(proj_ready, b * 2 + n + 1)
                    dve.scalar_tensor_tensor(out=cols, in0=bank[:, n, :], scalar=w["bproj"], in1=cols,
                                             op0=ALU.add, op1=ALU.add).then_inc(image_done, 1)

            over_images(dve, first, body)

        @block.gpsimd
        def _(pool):
            pool.memset(ks[KB:KM, :, :, :], 1.0).then_inc(ones_set, 1)


class Weights:

    def __init__(self, nc, sb, sem, drams):
        self.loaded, self.count = sem("weights_loaded"), len(drams)
        self.tiles = {name: sb(name, list(d.shape), F32) for name, d in drams.items()}
        ones, before = sb("ones", [C, C], BF16), sb("before", [C, C], BF16)
        self.ones, self.before = ones[:], before[:]
        cast = sem("constants_cast")
        with nc.Block() as block:
            @block.sync
            def _(sp):
                for name, d in drams.items():
                    sp.dma_start(self.tiles[name][:], d).then_inc(self.loaded, 16)

            @block.scalar
            def _(act):
                load_tables(nc, act, LN_EXP_TABLES)

            @block.vector
            def _(dve):
                dve.memset(ones[:], 1.0)
                dve.wait_ge(self.loaded, 16 * self.count)
                dve.tensor_copy(before[:], self["before_f"]).then_inc(cast, 1)
                dve.wait_ge(cast, 1)

    def __getitem__(self, name):
        return self.tiles[name][:]


E = 8
TOKENS = B * T
TILE = 512
Q = TILE // C
ROW = C + 2
REGION = TOKENS // TILE + 1
TILES = 40
RING = 4
IDLE = TILES - 2 * TOKENS // TILE
UNITS_XD = E * REGION + IDLE
BLANKS = E + IDLE
SPARE = 2 * TOKENS


def route(nc, sb, sem, bank, w, X, layer, xd_dram, table):
    second = layer == 1
    k = f"moe{layer}_"
    xc = sb("xc", [C, 2, TILE], F32)
    sq = sb("sq", [C, 2, TILE], F32)
    rs = sb("rs", [C, 2, TILE], F32)
    rs2 = sb("rs2", [C, 2, TILE], F32)
    xl = sb("xl", [C, 2, TILE], F32)
    xn = sb("xn", [C, 2, TILE], F32)
    rows = sb("rows", [C, 2, Q, 2, ROW], F32)
    places = sb("places", [C, 2, Q, 2], mybir.dt.uint32)
    small = {n: sb(n, [C, Q, E], F32) for n in
             ("logits", "shifted", "e", "p", "eq", "key", "best", "p2", "eq2", "key2", "second", "slot", "at")}
    per = {n: sb(n, [C, Q], F32) for n in ("lmax", "esum", "rsum", "g1", "k1", "g2", "k2")}
    per["place"] = sb("place", [C, Q, 2], F32)
    ids = sb("ids", [C, 2, Q, 2], F32)
    count = sb("count", [C, E], F32)
    blank = sb("blank", [C, BLANKS, Q * ROW], F32)
    mask = sb("mask", [C, Q, E], BF16)
    base = sb("base", [C, E], F32)
    count16 = sb("count16", [C, E, 16], F32)
    tiles = sb("tiles", [C, E], F32)
    ends = sb("ends", [C, E], F32)
    pad = sb("pad", [C, E], F32)
    passed = sb("passed", [C, TILES, E], F32)
    skip = sb("skip", [C, TILES, E], F32)
    ex = sb("ex", [C, TILES], F32)
    un = sb("un", [C, TILES], F32)
    base_i = sb("base_i", [C, E], mybir.dt.int32)
    centred, copied, squared, var_ready = sem("centred"), sem("copied"), sem("squared"), sem("var_ready")
    logged, rstd_ready, xn_ready, router_ready = sem("logged"), sem("rstd_ready"), sem("xn_ready"), sem("router_ready")
    turned, rows_ready, exp_ready, mask_ready = sem("turned"), sem("rows_ready"), sem("exp_ready"), sem("mask_ready")
    ranked, step, gates_ready, sent = sem("ranked"), sem("step"), sem("gates_ready"), [sem("sent0"), sem("sent1")]
    planned, blanks_sent, base_set, blank_ready = sem("planned"), sem("blanks_sent"), sem("base_set"), sem("blank_ready")
    fence, normed_once = sem("fence"), sem("normed_once")
    STEPS_TILE = 23

    with nc.Block() as block:
        @block.tensor
        def _(pe):
            with pe.Fori(0, TOKENS // TILE // 2) as i:
                for p in range(2):
                    pe.wait_ge(copied, 2 * i + p)
                    pe.matmul(bank[:, 4 * p, :], w["centre"], X[:, bass.ds((2 * i + p) * TILE, TILE)],
                              start=True, stop=True).then_inc(centred, 1)
                for p in range(2):
                    pe.wait_ge(squared, 2 * i + p + 1)
                    pe.matmul(bank[:, 4 * p + 1, :], w["mean"], sq[:, p, :], start=True, stop=True).then_inc(var_ready, 1)
                for p in range(2):
                    pe.wait_ge(xn_ready, 2 * i + p + 1)
                    for q in range(Q):
                        ins = pe.matmul(bank[:, 4 * p + 2, q * E:(q + 1) * E], xn[:, p, q * C:(q + 1) * C],
                                        w[k + "router"], start=True, stop=True)
                    ins.then_inc(router_ready, 1)
                    pe.wait_ge(rows_ready, 2 * i)
                    for q in range(Q):
                        ins = pe.transpose(bank[:, 4 * p + 3, q * C:(q + 1) * C], xn[:, p, q * C:(q + 1) * C], w["ident"])
                    ins.then_inc(turned, 1)
                for p in range(2):
                    pe.wait_ge(mask_ready, 2 * i + p + 1)
                    for q in range(Q + 1):
                        out = bank[:, 4 * p + 2, 64 + q * E:64 + (q + 1) * E]
                        for q2 in range(q):
                            ins = pe.matmul(out, w.ones, mask[:, q2, :], start=(q2 == 0), stop=(q == Q and q2 == q - 1))
                        if q < Q:
                            ins = pe.matmul(out, w.before, mask[:, q, :], start=(q == 0), stop=True)
                    ins.then_inc(ranked, 1)

        @block.scalar
        def _(act):
            load_tables(nc, act, LN_EXP_TABLES)
            with act.Fori(0, TOKENS // TILE // 2) as i:
                for p in range(2):
                    act.wait_ge(copied, 2 * i + p + 1)
                    act.activation(sq[:, p, :], xc[:, p, :], ACT.Square).then_inc(squared, 1)
                for p in range(2):
                    act.wait_ge(var_ready, 2 * i + p + 1)
                    act.wait_ge(xn_ready, 2 * i)
                    act.activation(rs[:, p, :], bank[:, 4 * p + 1, :], ACT.Ln, bias=w["eps"][:, 1:2]).then_inc(logged, 1)
                    if second:
                        act.activation(rs2[:, p, :], bank[:, 4 * p + 1, :], ACT.Ln, bias=w["eps"][:, 2:3],
                                       scale=1.0 + 1e-5).then_inc(logged, 1)
                m = 2 if second else 1
                for p in range(2):
                    act.wait_ge(logged, (2 * i + p + 1) * m)
                    act.activation(rs[:, p, :], rs[:, p, :], ACT.Exp, scale=-0.5).then_inc(rstd_ready, 1)
                    if second:
                        act.activation(rs2[:, p, :], rs2[:, p, :], ACT.Exp, scale=-0.5).then_inc(rstd_ready, 1)
                for p in range(2):
                    act.wait_ge(turned, 2 * i + p + 1)
                    act.wait_ge(sent[p], i * 16 * 2 * Q)
                    act.activation(rows[:, p, :, :, 0:C], bank[:, 4 * p + 3, :].rearrange("t (q c) -> t q c", q=Q)
                                   .unsqueeze(2).to_broadcast([C, Q, 2, C]), ACT.Copy).then_inc(rows_ready, 1)
                for p in range(2):
                    act.wait_ge(step, (2 * i + p) * STEPS_TILE + 3)
                    act.activation(small["e"][:], small["shifted"][:], ACT.Exp).then_inc(exp_ready, 1)

        @block.vector
        def _(dve):
            dve.tensor_copy(base[:], w["region"])
            dve.tensor_copy(ids[:].rearrange("t p q c -> t (p q c)"), w["row_ids"]).then_inc(base_set, 1)
            dve.wait_ge(base_set, 1)
            with dve.Fori(0, TOKENS // TILE // 2) as i:
                for p in range(2):
                    dve.wait_ge(centred, 2 * i + p + 1)
                    dve.tensor_copy(xc[:, p, :], bank[:, 4 * p, :]).then_inc(copied, 1)
                for p in range(2):
                    t = 2 * i + p
                    if not second:
                        dve.wait_ge(rstd_ready, t + 1)
                        dve.wait_ge(turned, 2 * i)
                        dve.tensor_tensor(xn[:, p, :], xc[:, p, :], rs[:, p, :], ALU.mult).then_inc(xn_ready, 1)
                        continue
                    dve.wait_ge(rstd_ready, 2 * t + 2)
                    dve.wait_ge(turned, 2 * i)
                    dve.tensor_tensor(xl[:, p, :], xc[:, p, :], rs[:, p, :], ALU.mult).then_inc(normed_once, 1)
                    dve.tensor_tensor(rs2[:, p, :], xc[:, p, :], rs2[:, p, :], ALU.mult).then_inc(normed_once, 1)
                    dve.wait_ge(normed_once, 2 * t + 1)
                    tokens = X[:, bass.ds(t * TILE, TILE)]
                    dve.tensor_tensor(tokens, tokens, xl[:, p, :], ALU.add)
                    dve.wait_ge(normed_once, 2 * t + 2)
                    dve.tensor_scalar(xn[:, p, :], rs2[:, p, :], w["ln"][:, 0:1], w["ln"][:, 1:2],
                                      ALU.mult, ALU.add).then_inc(xn_ready, 1)
                for p in range(2):
                    t = 2 * i + p
                    done = [0]
                    s, v = small, per
                    wide = lambda a: a[:].unsqueeze(2).to_broadcast([C, Q, E])

                    def then(ins):
                        ins.then_inc(step, 1)
                        done[0] += 1
                        dve.wait_ge(step, t * STEPS_TILE + done[0])

                    dve.wait_ge(router_ready, t + 1)
                    then(dve.tensor_tensor(s["logits"][:].rearrange("t q e -> t (q e)"), bank[:, 4 * p + 2, 0:Q * E],
                                           w[k + "router_bias"], ALU.add))
                    then(dve.tensor_reduce(v["lmax"][:], s["logits"][:], AX.X, ALU.max))
                    then(dve.tensor_tensor(s["shifted"][:], s["logits"][:], wide(v["lmax"]), ALU.subtract))
                    dve.wait_ge(exp_ready, t + 1)
                    then(dve.tensor_reduce(v["esum"][:], s["e"][:], AX.X, ALU.add))
                    then(dve.reciprocal(v["rsum"][:], v["esum"][:]))
                    then(dve.tensor_tensor(s["p"][:], s["e"][:], wide(v["rsum"]), ALU.mult))
                    for probs, gate, eq, key, kmax, hot in (("p", "g1", "eq", "key", "k1", "best"),
                                                            ("p2", "g2", "eq2", "key2", "k2", "second")):
                        if hot == "second":
                            then(dve.scalar_tensor_tensor(out=s["p2"][:], in0=s["best"][:], scalar=-2.0, in1=s["p"][:],
                                                          op0=ALU.mult, op1=ALU.add))
                        then(dve.tensor_reduce(v[gate][:], s[probs][:], AX.X, ALU.max))
                        then(dve.tensor_tensor(s[eq][:], s[probs][:], wide(v[gate]), ALU.is_equal))
                        then(dve.tensor_tensor(s[key][:].rearrange("t q e -> t (q e)"),
                                               s[eq][:].rearrange("t q e -> t (q e)"), w["firstness"], ALU.mult))
                        then(dve.tensor_reduce(v[kmax][:], s[key][:], AX.X, ALU.max))
                        then(dve.tensor_tensor(s[hot][:], s[key][:], wide(v[kmax]), ALU.is_equal))
                    dve.wait_ge(ranked, t)
                    dve.tensor_tensor(mask[:], s["best"][:], s["second"][:], ALU.add).then_inc(mask_ready, 1)
                    dve.wait_ge(rows_ready, t + 1)
                    dve.tensor_copy(rows[:, p, :, 0, C:C + 1], v["g1"][:].unsqueeze(2))
                    dve.tensor_copy(rows[:, p, :, 1, C:C + 1], v["g2"][:].unsqueeze(2))
                    dve.tensor_copy(rows[:, p, :, :, C + 1:C + 2], ids[:, p].unsqueeze(3))
                    then(dve.tensor_scalar(ids[:, p], ids[:, p], 2.0 * TILE, None, ALU.add))
                    dve.wait_ge(ranked, t + 1)
                    then(dve.tensor_tensor(s["slot"][:], bank[:, 4 * p + 2, 64:64 + Q * E].rearrange("t (q e) -> t q e", q=Q),
                                           base[:].unsqueeze(1).to_broadcast([C, Q, E]), ALU.add))
                    dve.tensor_tensor(base[:], base[:], bank[:, 4 * p + 2, 64 + Q * E:64 + (Q + 1) * E], ALU.add)
                    for c, hot in enumerate(("best", "second")):
                        then(dve.tensor_tensor(s["at"][:], s["slot"][:], s[hot][:], ALU.mult))
                        then(dve.tensor_reduce(v["place"][:, :, c:c + 1], s["at"][:], AX.X, ALU.add))
                    dve.tensor_copy(places[:, p], v["place"][:]).then_inc(gates_ready, 1)
                    assert done[0] == STEPS_TILE
            done = [0]

            def plan(ins):
                ins.then_inc(planned, 1)
                done[0] += 1
                dve.wait_ge(planned, done[0])

            dve.wait_ge(gates_ready, TOKENS // TILE)
            plan(dve.tensor_copy(base_i[:], base[:]))
            plan(dve.tensor_tensor(count[:], base[:], w["region"], ALU.subtract))
            plan(dve.tensor_tensor(count16[:], count[:].unsqueeze(2).to_broadcast([C, E, 16]),
                                   w["k_tile"].rearrange("t (e k) -> t e k", e=E), ALU.is_gt))
            plan(dve.tensor_reduce(tiles[:], count16[:], AX.X, ALU.add))
            plan(dve.tensor_tensor_scan(ends[:], tiles[:], w["zeros"][:, 0:E], 0.0, ALU.add, ALU.add))
            plan(dve.tensor_scalar(pad[:], tiles[:], -1.0, float(REGION), ALU.mult, ALU.add))
            plan(dve.tensor_tensor(passed[:], ends[:].unsqueeze(1).to_broadcast([C, TILES, E]),
                                   w["tile_no"].unsqueeze(2).to_broadcast([C, TILES, E]), ALU.is_le))
            plan(dve.tensor_reduce(ex[:], passed[:], AX.X, ALU.add))
            plan(dve.tensor_tensor(skip[:], passed[:], pad[:].unsqueeze(1).to_broadcast([C, TILES, E]), ALU.mult))
            plan(dve.tensor_reduce(un[:], skip[:], AX.X, ALU.add))
            plan(dve.tensor_tensor(un[:], un[:], w["tile_no"], ALU.add))
            plan(dve.tensor_scalar(table[:, 0, :], ex[:], float(E - 1), None, ALU.min))
            plan(dve.tensor_scalar(table[:, 1, :], un[:], 1.0, None, ALU.mult))

        @block.gpsimd
        def _(pool):
            pool.memset(blank[:], 0.0).then_inc(blank_ready, 1)
            pool.wait_ge(blank_ready, 1)
            pool.tensor_copy(blank[:].rearrange("t n (q r) -> t (n q) r", q=Q)[:, :, ROW - 1:ROW],
                             w["blank_rows"].unsqueeze(2)).then_inc(blank_ready, 1)
            with pool.Fori(0, TOKENS // TILE // 2) as i:
                for p in range(2):
                    pool.wait_ge(gates_ready, 2 * i + p + 1)
                    pool.sem_inc(fence, 1)
                    for q in range(Q):
                        for c in range(2):
                            pool.indirect_dma_start(xd_dram, bass.IndirectOffsetOnAxis(places[:, p, q, c:c + 1], 0),
                                                    rows[:, p, q, c, :], None).then_inc(sent[p], 16)
            for p in range(2):
                pool.wait_ge(sent[p], TOKENS // TILE // 2 * 16 * 2 * Q)

        @block.sync
        def _(sp):
            sp.wait_ge(blank_ready, 2)
            for n in range(IDLE):
                sp.dma_start(xd_dram[(E * REGION + n) * TILE:(E * REGION + n + 1) * TILE, :]
                             .rearrange("(t q) r -> t (q r)", q=Q), blank[:, E + n]).then_inc(blanks_sent, 16)
            sp.wait_ge(planned, 1)
            for e in range(E):
                first = sp.value_load(base_i[0:1, e:e + 1], min_val=0, max_val=E * REGION * TILE)
                sp.dma_start(xd_dram[bass.ds(first, TILE), :].rearrange("(t q) r -> t (q r)", q=Q),
                             blank[:, e]).then_inc(blanks_sent, 16)
            sp.wait_ge(blanks_sent, 16 * BLANKS)


def experts(nc, sb, sem, bank, w, layer, xd_dram, yd_dram, table, records):
    second = layer == 1
    FB = 4 * C
    NH = 4 if second else 2
    W2 = FB + 4
    B2 = W2 + NH * C
    REC = B2 + C
    rec = sb("rec", [C, RING, REC], F32)
    xr = sb("xr", [C, RING, Q, ROW], F32)
    xt = sb("xt", [C, 2, TILE], F32)
    hidden = sb("hidden", [C, 2, NH, TILE], F32)
    gate = sb("gate", [C, 2, TILE], F32)
    y1 = sb("y1", [C, 2, Q, C], F32)
    yo = sb("yo", [C, 2, Q, C], F32)
    places = sb("places", [C, 2, Q], mybir.dt.uint32)
    loaded = [sem(f"loaded{r}") for r in range(RING)]
    turned, xt_copied, g_ready, v_ready, gated = sem("turned"), sem("xt_copied"), sem("g_ready"), sem("v_ready"), sem("gated")
    h_ready, y_ready, y_copied, yo_ready, fence = sem("h_ready"), sem("y_ready"), sem("y_copied"), sem("yo_ready"), sem("fence")
    sent = [sem("sent0"), sem("sent1")]
    LOADS = 16 * (len(records) + 1)

    def over_tiles(eng, ahead, behind):
        def at(step, group, r):
            group, r = group + r // RING, r % RING
            step(RING * group + r, r, r % 2, RING // 2 * group + r // 2, group)

        at(ahead, 0, 0)
        with eng.Fori(0, TILES // RING - 1) as group:
            for r in range(RING):
                at(ahead, group, r + 1)
                at(behind, group, r)
        last = TILES // RING - 1
        for r in range(RING):
            if r < RING - 1:
                at(ahead, last, r + 1)
            at(behind, last, r)

    with nc.Block() as block:
        @block.sync
        def _(sp):
            def load(j, r):
                e = sp.value_load(table[0:1, 0, bass.ds(j, 1)], min_val=0, max_val=E - 1)
                u = sp.value_load(table[0:1, 1, bass.ds(j, 1)], min_val=0, max_val=UNITS_XD - 1)
                at = 0
                for record in records:
                    n = record.shape[2]
                    sp.dma_start(rec[:, r, at:at + n],
                                 record[bass.ds(e, 1)].rearrange("o c n -> c (o n)")).then_inc(loaded[r], 16)
                    at += n
                sp.dma_start(xr[:, r].rearrange("t q r -> t (q r)"),
                             xd_dram[bass.ds(u * TILE, TILE), :].rearrange("(t q) r -> t (q r)", q=Q)).then_inc(loaded[r], 16)

            for r in range(RING):
                load(r, r)
            with sp.Fori(0, TILES // RING - 1) as i:
                for r in range(RING):
                    sp.wait_ge(yo_ready, RING * i + r + 1)
                    load(RING * (i + 1) + r, r)

        @block.tensor
        def _(pe):
            def ahead(j, r, p, h, i):
                pe.wait_ge(loaded[r], (i + 1) * LOADS)
                for q in range(Q):
                    ins = pe.transpose(bank[:, p, q * C:(q + 1) * C], xr[:, r, q, 0:C], w["ident"])
                ins.then_inc(turned, 1)
                pe.wait_ge(xt_copied, j + 1)
                for f in range(4):
                    if not (isinstance(j, int) and j == 0):
                        if second:
                            pe.wait_ge(h_ready, (j - 1) * 4 + f + 1)
                        elif f % 2:
                            pe.wait_ge(h_ready, (j - 1) * 2 + f // 2 + 1)
                        else:
                            pe.wait_ge(gated, (j - 1) * 2 + f // 2 + 1)
                    ins = pe.matmul(bank[:, 2 + f, :], rec[:, r, f * C:(f + 1) * C], xt[:, p, :], start=True, stop=True)
                    ins.then_inc(g_ready if second or f % 2 == 0 else v_ready, 1)

            def behind(j, r, p, h, i):
                pe.wait_ge(h_ready, (j + 1) * NH)
                pe.wait_ge(y_copied, 2 * h)
                for q in range(Q):
                    for f in range(NH):
                        ins = pe.matmul(bank[:, 6 + p, q * C:(q + 1) * C], hidden[:, p, f, q * C:(q + 1) * C],
                                        rec[:, r, W2 + f * C:W2 + (f + 1) * C], start=(f == 0), stop=(f == NH - 1))
                ins.then_inc(y_ready, 1)

            over_tiles(pe, ahead, behind)

        @block.scalar
        def _(act):
            def ahead(j, r, p, h, i):
                act.wait_ge(y_ready, 2 * h)
                for f in range(NH):
                    act.wait_ge(g_ready, j * NH + f + 1)
                    if second:
                        act.activation(hidden[:, p, f, :], bank[:, 2 + f, :], ACT.Gelu,
                                       bias=rec[:, r, FB + f:FB + f + 1]).then_inc(h_ready, 1)
                    else:
                        if f == 0:
                            act.wait_ge(h_ready, j * 2)
                        act.activation(gate[:, f, :], bank[:, 2 + 2 * f, :], ACT.Silu,
                                       bias=rec[:, r, FB + 2 * f:FB + 2 * f + 1]).then_inc(gated, 1)

            over_tiles(act, ahead, lambda *_: None)

        @block.vector
        def _(dve):
            def ahead(j, r, p, h, i):
                dve.wait_ge(turned, j + 1)
                dve.tensor_copy(xt[:, p, :], bank[:, p, :]).then_inc(xt_copied, 1)
                if not second:
                    dve.wait_ge(y_ready, 2 * h)
                    for f in range(2):
                        dve.wait_ge(gated, j * 2 + f + 1)
                        dve.wait_ge(v_ready, j * 2 + f + 1)
                        dve.scalar_tensor_tensor(out=hidden[:, p, f, :], in0=bank[:, 3 + 2 * f, :],
                                                 scalar=rec[:, r, FB + 2 * f + 1:FB + 2 * f + 2], in1=gate[:, f, :],
                                                 op0=ALU.add, op1=ALU.mult).then_inc(h_ready, 1)

            def behind(j, r, p, h, i):
                dve.wait_ge(y_ready, j + 1)
                dve.tensor_tensor(y1[:, p], bank[:, 6 + p, :].rearrange("t (q c) -> t q c", q=Q),
                                  rec[:, r, B2:B2 + C].unsqueeze(1).to_broadcast([C, Q, C]), ALU.add).then_inc(y_copied, 1)
                dve.wait_ge(sent[p], h * (16 * Q))
                dve.tensor_scalar(places[:, p], xr[:, r, :, C + 1], 0.0, None, ALU.add)
                dve.wait_ge(y_copied, j + 1)
                dve.tensor_tensor(yo[:, p], y1[:, p], xr[:, r, :, C:C + 1].to_broadcast([C, Q, C]), ALU.mult).then_inc(yo_ready, 1)

            over_tiles(dve, ahead, behind)

        @block.gpsimd
        def _(pool):
            with pool.Fori(0, TILES // 2) as i:
                for p in range(2):
                    pool.wait_ge(yo_ready, 2 * i + p + 1)
                    pool.sem_inc(fence, 1)
                    for q in range(Q):
                        pool.indirect_dma_start(yd_dram, bass.IndirectOffsetOnAxis(places[:, p, q:q + 1], 0),
                                                yo[:, p, q, :], None).then_inc(sent[p], 16)
            for p in range(2):
                pool.wait_ge(sent[p], TILES // 2 * 16 * Q)


def combine(nc, sb, sem, bank, w, X, yd_dram, out):
    y = sb("y", [C, 2, 2, Q * C], F32)
    total = sb("total", [C, 2, Q * C], F32)
    loaded = [sem("loaded0"), sem("loaded1")]
    summed, turned, added, stored = sem("summed"), sem("turned"), sem("added"), sem("stored")
    PAIRS = TOKENS // TILE // 2

    with nc.Block() as block:
        @block.sync
        def _(sp):
            with sp.Fori(0, PAIRS) as i:
                for p in range(2):
                    sp.wait_ge(summed, 2 * i)
                    for c in range(2):
                        src = yd_dram[bass.ds((2 * i + p) * TILE + c * TOKENS, TILE), :].rearrange("(t q) c -> t (q c)", q=Q)
                        sp.dma_start(y[:, p, c, :], src).then_inc(loaded[p], 16)

        @block.vector
        def _(dve):
            with dve.Fori(0, PAIRS) as i:
                for p in range(2):
                    dve.wait_ge(loaded[p], (i + 1) * 32)
                    dve.wait_ge(turned, 2 * i)
                    dve.tensor_tensor(total[:, p, :], y[:, p, 0, :], y[:, p, 1, :], ALU.add).then_inc(summed, 1)
                for p in range(2):
                    t = 2 * i + p
                    dve.wait_ge(turned, t + 1)
                    tokens = X[:, bass.ds(t * TILE, TILE)].rearrange("c (t q) -> c q t", q=Q)
                    dve.tensor_tensor(tokens, tokens, bank[:, p, :].rearrange("c (q t) -> c q t", q=Q),
                                      ALU.add).then_inc(added, 1)

        @block.tensor
        def _(pe):
            with pe.Fori(0, PAIRS) as i:
                for p in range(2):
                    pe.wait_ge(summed, 2 * i + p + 1)
                    pe.wait_ge(added, 2 * i)
                    for q in range(Q):
                        ins = pe.transpose(bank[:, p, q * C:(q + 1) * C], total[:, p, q * C:(q + 1) * C], w["ident"])
                    ins.then_inc(turned, 1)

        @block.gpsimd
        def _(pool):
            if out is None:
                return
            for b in range(B):
                pool.wait_ge(added, 2 * b + 2)
                pool.dma_start(out[b], X[:, b * T:(b + 1) * T]).then_inc(stored, 16)
            pool.wait_ge(stored, 16 * B)


def fold_expert_weights(nc, sb, sem, bank, w, w1_dram, wgv_dram, b_dram, folded):
    w1 = sb("w1", [C, 2, 2 * C], F32)
    w1t = sb("w1t", [C, 2, C], F32)
    wgv = sb("wgv", [C, 2, 2, 4 * C], F32)
    bias = sb("bias", [C, 2, 6], F32)
    rec = sb("rec", [C, 2, 4 * C + 4], F32)
    loaded = [sem("loaded0"), sem("loaded1")]
    turned, copied, product, biases = sem("turned"), sem("copied"), sem("product"), sem("biases")
    product_copied, stored = sem("product_copied"), [sem("stored0"), sem("stored1")]

    with nc.Block() as block:
        @block.sync
        def _(sp):
            with sp.Fori(0, E // 2) as i:
                for p in range(2):
                    e = 2 * i + p
                    sp.wait_ge(product_copied, 4 * i)
                    sp.dma_start(w1[:, p], w1_dram[bass.ds(e, 1)].rearrange("o d h -> d (o h)")).then_inc(loaded[p], 16)
                    sp.dma_start(wgv[:, p], wgv_dram[bass.ds(e, 1)].rearrange("o (k h) f -> h (o k) f", k=2)).then_inc(loaded[p], 16)
                    sp.dma_start(bias[:, p], b_dram[bass.ds(e, 1)].rearrange("o c n -> c (o n)")).then_inc(loaded[p], 16)

        @block.tensor
        def _(pe):
            pe.wait_ge(w.loaded, 16 * w.count)
            with pe.Fori(0, E // 2) as i:
                for p in range(2):
                    e = 2 * i + p
                    pe.wait_ge(loaded[p], (i + 1) * 48)
                    pe.wait_ge(copied, e)
                    for k in range(2):
                        ins = pe.transpose(bank[:, 0, k * C:(k + 1) * C], w1[:, p, k * C:(k + 1) * C], w["ident"])
                    ins.then_inc(turned, 1)
                    pe.wait_ge(copied, e + 1)
                    pe.wait_ge(product_copied, 2 * e)
                    for k in range(2):
                        ins = pe.matmul(bank[:, 1, :], w1t[:, k, :], wgv[:, p, k, :], start=(k == 0), stop=(k == 1))
                    ins.then_inc(product, 1)
                    for f in range(4):
                        for k in range(2):
                            ins = pe.matmul(bank[:, 2, f:f + 1], wgv[:, p, k, f * C:(f + 1) * C], bias[:, p, k:k + 1],
                                            start=(k == 0), stop=(k == 1))
                    ins.then_inc(biases, 1)

        @block.vector
        def _(dve):
            with dve.Fori(0, E // 2) as i:
                for p in range(2):
                    e = 2 * i + p
                    dve.wait_ge(turned, e + 1)
                    dve.tensor_copy(w1t[:].rearrange("h k d -> h (k d)"), bank[:, 0, 0:2 * C]).then_inc(copied, 1)
                    dve.wait_ge(product, e + 1)
                    dve.wait_ge(stored[p], i * 16)
                    dve.tensor_copy(rec[:, p, 0:4 * C], bank[:, 1, :]).then_inc(product_copied, 1)
                    dve.wait_ge(biases, e + 1)
                    dve.tensor_tensor(rec[:, p, 4 * C:4 * C + 4], bank[:, 2, 0:4], bias[:, p, 2:6], ALU.add).then_inc(product_copied, 1)

        @block.scalar
        def _(act):
            with act.Fori(0, E // 2) as i:
                for p in range(2):
                    act.wait_ge(product_copied, 4 * i + 2 * p + 2)
                    act.dma_start(folded[bass.ds(2 * i + p, 1)].rearrange("o c n -> c (o n)"), rec[:, p]).then_inc(stored[p], 16)
            for p in range(2):
                act.wait_ge(stored[p], E // 2 * 16)


SIDE = 32
TAPS = 5
PAD = TAPS // 2
WIDE = SIDE + 2 * PAD


def multiscale_attention(nc, sb, sem, bank, w, X):
    xc = sb("xc", [C, T], F32)
    sq = sb("sq", [C, T], F32)
    rs = sb("rs", [C, T], F32)
    xn = sb("xn", [C, T], F32)
    pads = [sb(f"pad_{s}", [C, WIDE, WIDE], F32) for s in "qkv"]
    dw = sb("dw", [C, 2, T], F32)
    av = sb("av", [C, T], F32)
    qr = sb("qr", [C, 2, T], F32)
    kT = sb("kT", [C, 2, TC, C], F32)
    vT = sb("vT", [C, 2, TC, C + 1], F32)
    vk = sb("vk", [C, 2, C + 1], F32)
    vkm = sb("vkm", [C, 2, C], F32)
    ksm = sb("ksm", [C, 2, C], F32)
    rd = sb("rd", [C, 4, HALF], F32)
    o = sb("o", [C, 4, HALF], F32)
    yb = sb("yb", [C, 2, HALF], F32)
    taps = sb("taps", [C, TAPS * TAPS, C], F32)
    inv = sb("inv", [C, 1], F32)
    shift = sb("shift", [C, 1], F32)
    bn_log = sb("bn_log", [C, 1], F32)
    fence = sem("fence")
    cleared, bn_step, taps_ready, bn_ready = sem("cleared"), sem("bn_step"), sem("taps_ready"), sem("bn_ready")
    centred, copied, squared, var_ready, logged = sem("centred"), sem("copied"), sem("squared"), sem("var_ready"), sem("logged")
    rstd_ready, xn_ready, qkv_ready, padded = sem("rstd_ready"), sem("xn_ready"), sem("qkv_ready"), sem("padded")
    kv_ready, kv_copied, dw_step, av_ready, av_copied = sem("kv_ready"), sem("kv_copied"), sem("dw_step"), sem("av_ready"), sem("av_copied")
    av_turned, vt_copied, qa_ready, qa_copied = sem("av_turned"), sem("vt_copied"), sem("qa_ready"), sem("qa_copied")
    ka_ready, ka_copied, vk_ready, vk_copied, masked = sem("ka_ready"), sem("ka_copied"), sem("vk_ready"), sem("vk_copied"), sem("masked")
    num_ready, den_logged, rden_ready, o_ready = sem("num_ready"), sem("den_logged"), sem("rden_ready"), sem("o_ready")
    proj_ready, y_ready, added = sem("proj_ready"), sem("y_ready"), sem("added")
    NT = TAPS * TAPS

    def window(pad, tap, n=None):
        dy, dx = tap // TAPS, tap % TAPS
        r0, r = (dy, SIDE) if n is None else (dy + n * SIDE // 2, SIDE // 2)
        return pad[:, r0:r0 + r, dx:dx + SIDE]

    with nc.Block() as block:
        @block.tensor
        def _(pe):
            with pe.Fori(0, B) as b:
                pe.wait_ge(added, 2 * b)
                for n in range(2):
                    pe.matmul(bank[:, n, :], w["centre"], X[:, bass.ds(b * T + n * HALF, HALF)],
                              start=True, stop=True).then_inc(centred, 1)
                for n in range(2):
                    pe.wait_ge(squared, b * 2 + n + 1)
                    pe.matmul(bank[:, 2 + n, :], w["mean"], sq[:, n * HALF:(n + 1) * HALF],
                              start=True, stop=True).then_inc(var_ready, 1)
                pe.wait_ge(xn_ready, b * 2 + 2)
                for s, slot in ((0, 4), (1, 6), (2, 0)):
                    for n in range(2):
                        pe.matmul(bank[:, slot + n, :], w["c_qkv"][:, s * C:(s + 1) * C], xn[:, n * HALF:(n + 1) * HALF],
                                  start=True, stop=True).then_inc(qkv_ready, 1)
                for u in range(4):
                    if u == 2:
                        pe.wait_ge(padded, b * 8 + 4)
                    for c in (2 * u, 2 * u + 1):
                        ins = pe.matmul(bank[:, 2 + u, c % 2 * 2 * C:(c % 2 + 1) * 2 * C], xn[:, c * C:(c + 1) * C],
                                        w["c_qkv"][:, C:3 * C], start=True, stop=True)
                    ins.then_inc(kv_ready, 1)
                pe.wait_ge(taps_ready, NT)
                pe.wait_ge(padded, b * 8 + 8)
                for tap in range(NT):
                    for n in range(2):
                        ins = pe.matmul(bank[:, 6 + n, :], taps[:, tap, :], window(pads[2], tap, n),
                                        start=(tap == 0), stop=(tap == NT - 1))
                ins.then_inc(av_ready, 1)
                pe.wait_ge(av_copied, b * 2 + 2)
                for n in range(2):
                    for q in range(4):
                        c = 4 * n + q
                        ins = pe.transpose(bank[:, n, q * C:(q + 1) * C], av[:, c * C:(c + 1) * C], w["ident"])
                    ins.then_inc(av_turned, 1)
                pe.wait_ge(kv_copied, b * 8 + 8)
                pe.wait_ge(dw_step, (b + 1) * 2 * NT)
                for n in range(2):
                    pe.matmul(bank[:, 2 + n, :], w["c_pw"][:, 0:C], dw[:, 0, n * HALF:(n + 1) * HALF],
                              start=True, stop=True).then_inc(qa_ready, 1)
                for n in range(2):
                    for q in range(4):
                        c = 4 * n + q
                        ins = pe.matmul(bank[:, 4 + n, q * C:(q + 1) * C], dw[:, 1, c * C:(c + 1) * C],
                                        w["c_pw"][:, C:2 * C], start=True, stop=True)
                    ins.then_inc(ka_ready, 1)
                for m in range(2):
                    if m == 1:
                        pe.wait_ge(vt_copied, b * 2 + 2)
                        pe.wait_ge(ka_copied, b * 2 + 2)
                    for c in range(TC):
                        ins = pe.matmul(bank[:, 6 + m, 0:C + 1], kT[:, m, c, :], vT[:, m, c, :],
                                        start=(c == 0), stop=(c == TC - 1))
                    ins.then_inc(vk_ready, 1)
                pe.wait_ge(qa_copied, b * 2 + 2)
                for m in range(2):
                    pe.wait_ge(masked, b * 2 + m + 1)
                    for n in range(2):
                        slot = 2 * (2 * m + n)
                        if slot == 6:
                            pe.wait_ge(masked, b * 2 + 2)
                        q = qr[:, m, n * HALF:(n + 1) * HALF]
                        pe.matmul(bank[:, slot, :], vkm[:, m, :], q, start=True, stop=True)
                        pe.matmul(bank[:, slot + 1, :], ksm[:, m, :], q, start=True, stop=True).then_inc(num_ready, 1)
                for n in range(2):
                    pe.wait_ge(o_ready, b * 4 + 3 + n)
                    for m in range(2):
                        ins = pe.matmul(bank[:, 1 + 2 * n, :], w["c_proj"][:, m * C:(m + 1) * C], o[:, 2 * m + n, :],
                                        start=(m == 0), stop=(m == 1))
                    ins.then_inc(proj_ready, 1)

        @block.scalar
        def _(act):
            load_tables(nc, act, LN_EXP_TABLES)
            act.wait_ge(bn_step, 1)
            act.activation(bn_log[:], w["bn"][:, 3:4], ACT.Ln, bias=w["eps"][:, 1:2]).then_inc(bn_step, 1)
            act.wait_ge(bn_step, 2)
            act.activation(bn_log[:], bn_log[:], ACT.Exp, scale=-0.5).then_inc(bn_step, 1)
            with act.Fori(0, B) as b:
                for n in range(2):
                    act.wait_ge(copied, b * 2 + n + 1)
                    act.activation(sq[:, n * HALF:(n + 1) * HALF], xc[:, n * HALF:(n + 1) * HALF], ACT.Square).then_inc(squared, 1)
                for n in range(2):
                    act.wait_ge(var_ready, b * 2 + n + 1)
                    act.activation(rs[:, n * HALF:(n + 1) * HALF], bank[:, 2 + n, :], ACT.Ln, bias=w["eps"][:, 0:1]).then_inc(logged, 1)
                for n in range(2):
                    act.wait_ge(logged, b * 2 + n + 1)
                    act.activation(rs[:, n * HALF:(n + 1) * HALF], rs[:, n * HALF:(n + 1) * HALF], ACT.Exp,
                                   scale=-0.5).then_inc(rstd_ready, 1)
                act.wait_ge(cleared, 4)
                for s, slot in ((0, 4), (1, 6), (2, 0)):
                    for n in range(2):
                        act.wait_ge(qkv_ready, b * 6 + 2 * s + n + 1)
                        rows = slice(PAD + n * SIDE // 2, PAD + (n + 1) * SIDE // 2)
                        act.activation(pads[s][:, rows, PAD:PAD + SIDE],
                                       bank[:, slot + n, :].rearrange("c (y x) -> c y x", x=SIDE), ACT.Copy).then_inc(padded, 1)
                        if s == 0:
                            act.activation(qr[:, 0, n * HALF:(n + 1) * HALF], bank[:, slot + n, :], ACT.Relu).then_inc(padded, 1)
                for u in range(4):
                    act.wait_ge(kv_ready, b * 4 + u + 1)
                    src = bank[:, 2 + u, :].rearrange("t (c s e) -> t c s e", c=2, s=2)
                    act.activation(kT[:, 0, 2 * u:2 * u + 2, :], src[:, :, 0, :], ACT.Relu).then_inc(kv_copied, 1)
                    act.activation(vT[:, 0, 2 * u:2 * u + 2, 0:C], src[:, :, 1, :], ACT.Copy).then_inc(kv_copied, 1)
                act.wait_ge(av_ready, b + 1)
                for n in range(2):
                    act.activation(av[:, n * HALF:(n + 1) * HALF], bank[:, 6 + n, :], ACT.Copy).then_inc(av_copied, 1)
                for n in range(2):
                    act.wait_ge(av_turned, b * 2 + n + 1)
                    act.activation(vT[:, 1, 4 * n:4 * n + 4, 0:C], bank[:, n, :].rearrange("t (c e) -> t c e", c=4),
                                   ACT.Copy).then_inc(vt_copied, 1)
                for n in range(2):
                    act.wait_ge(qa_ready, b * 2 + n + 1)
                    act.activation(qr[:, 1, n * HALF:(n + 1) * HALF], bank[:, 2 + n, :], ACT.Relu).then_inc(qa_copied, 1)
                for n in range(2):
                    act.wait_ge(ka_ready, b * 2 + n + 1)
                    act.activation(kT[:, 1, 4 * n:4 * n + 4, :].rearrange("t c e -> t (c e)"), bank[:, 4 + n, :],
                                   ACT.Relu).then_inc(ka_copied, 1)
                for m in range(4):
                    act.wait_ge(num_ready, b * 4 + m + 1)
                    act.activation(rd[:, m, :], bank[:, 2 * m + 1, :], ACT.Ln, bias=w["eps"][:, 3:4]).then_inc(den_logged, 1)
                    act.wait_ge(den_logged, b * 4 + m + 1)
                    act.activation(rd[:, m, :], rd[:, m, :], ACT.Exp, scale=-1.0).then_inc(rden_ready, 1)
                act.wait_ge(bn_ready, 1)
                for n in range(2):
                    act.wait_ge(proj_ready, b * 2 + n + 1)
                    act.activation(yb[:, n, :], bank[:, 1 + 2 * n, :], ACT.Identity, scale=inv[:, 0:1],
                                   bias=shift[:, 0:1]).then_inc(y_ready, 1)

        @block.vector
        def _(dve):
            dve.memset(vT[:], 1.0).then_inc(cleared, 1)
            dve.engine_nop().then_inc(bn_step, 1)
            dve.wait_ge(bn_step, 3)
            dve.tensor_tensor(inv[:], w["bn"][:, 0:1], bn_log[:], ALU.mult).then_inc(bn_step, 1)
            dve.wait_ge(bn_step, 4)
            dve.tensor_tensor(shift[:], w["bn"][:, 2:3], inv[:], ALU.mult).then_inc(bn_step, 1)
            dve.wait_ge(bn_step, 5)
            dve.tensor_tensor(shift[:], w["bn"][:, 1:2], shift[:], ALU.subtract).then_inc(bn_ready, 1)
            for tap in range(NT):
                dve.tensor_scalar(taps[:, tap, :], w["c_pw"][:, 2 * C:3 * C], w["c_dw"][:, 2 * NT + tap:2 * NT + tap + 1],
                                  None, ALU.mult).then_inc(taps_ready, 1)
            with dve.Fori(0, B) as b:
                for n in range(2):
                    dve.wait_ge(centred, b * 2 + n + 1)
                    dve.tensor_copy(xc[:, n * HALF:(n + 1) * HALF], bank[:, n, :]).then_inc(copied, 1)
                for n in range(2):
                    dve.wait_ge(rstd_ready, b * 2 + n + 1)
                    dve.tensor_tensor(xn[:, n * HALF:(n + 1) * HALF], xc[:, n * HALF:(n + 1) * HALF],
                                      rs[:, n * HALF:(n + 1) * HALF], ALU.mult).then_inc(xn_ready, 1)
                dve.wait_ge(padded, b * 8 + 6)
                for tap in range(NT):
                    for s in range(2):
                        plane = dw[:, s, :].rearrange("c (y x) -> c y x", x=SIDE)
                        weight = w["c_dw"][:, s * NT + tap:s * NT + tap + 1]
                        if tap == 0:
                            dve.tensor_scalar(plane, window(pads[s], tap), weight, None, ALU.mult).then_inc(dw_step, 1)
                        else:
                            dve.wait_ge(dw_step, b * 2 * NT + 2 * tap - 1 + s)
                            dve.scalar_tensor_tensor(out=plane, in0=window(pads[s], tap), scalar=weight, in1=plane,
                                                     op0=ALU.mult, op1=ALU.add).then_inc(dw_step, 1)
                for m in range(2):
                    dve.wait_ge(vk_ready, b * 2 + m + 1)
                    dve.tensor_copy(vk[:, m, :], bank[:, 6 + m, 0:C + 1]).then_inc(vk_copied, 1)
                    dve.wait_ge(vk_copied, b * 2 + m + 1)
                    dve.tensor_tensor(vkm[:, m, :], vk[:, m, 0:C], w["heads"], ALU.mult)
                    dve.tensor_scalar(ksm[:, m, :], w["heads"], vk[:, m, C:C + 1], None, ALU.mult).then_inc(masked, 1)
                for m in range(4):
                    dve.wait_ge(rden_ready, b * 4 + m + 1)
                    dve.tensor_tensor(o[:, m, :], bank[:, 2 * m, :], rd[:, m, :], ALU.mult).then_inc(o_ready, 1)
                for n in range(2):
                    dve.wait_ge(y_ready, b * 2 + n + 1)
                    cols = X[:, bass.ds(b * T + n * HALF, HALF)]
                    dve.tensor_tensor(cols, cols, yb[:, n, :], ALU.add).then_inc(added, 1)

        @block.gpsimd
        def _(pool):
            for pad in pads:
                pool.memset(pad[:], 0.0).then_inc(cleared, 1)




def metaformer(nc, x_in, weights, w1, wgv, b_gv, rest0, rec1, out):
    names = [0]

    def allocator(ctx, make):
        def allocate(name, *args):
            names[0] += 1
            return ctx.enter_context(make(f"{name}_{names[0]}", *args))
        return allocate

    def stage(run, *args):
        signals = []

        def own_sem(name):
            names[0] += 1
            signals.append(nc.alloc_semaphore(name=f"{name}_{names[0]}"))
            return signals[-1]

        with ExitStack() as own:
            run(nc, allocator(own, nc.sbuf_tensor), own_sem, bank, w, *args)
        nc.clear_and_free_semaphores(signals)
        nc.all_engine_barrier()

    parts_dram = nc.dram_tensor("qk_parts", (B, 2, 3, C, T), BF16).ap()
    v_dram = nc.dram_tensor("v_turned", (B, C, TC * HEADS * VH), F32).ap()
    folded = nc.dram_tensor("folded", (E, C, 4 * C + 4), F32).ap()
    xd_dram = [nc.dram_tensor(f"dispatched{n}", (UNITS_XD * TILE, ROW), F32).ap() for n in range(2)]
    yd_dram = [nc.dram_tensor(f"results{n}", (SPARE + BLANKS * TILE, C), F32).ap() for n in range(2)]

    with ExitStack() as ctx:
        sb, sem = allocator(ctx, nc.sbuf_tensor), allocator(ctx, nc.semaphore)
        bank = ctx.enter_context(nc.psum_tensor("bank", [C, 8, HALF], F32))
        w = Weights(nc, sb, sem, weights)
        X = sb("X", [C, TOKENS], F32)
        table = sb("table", [C, 2, TILES], mybir.dt.int32)
        stage(fold_expert_weights, w1, wgv, b_gv, folded)
        with ExitStack() as own:
            XF = allocator(own, nc.sbuf_tensor)("XF", [C, TOKENS], F32)
            stage(normalize_and_project, X, XF, x_in, parts_dram, v_dram)
            stage(attention, X, XF, parts_dram, v_dram)
        stage(route, X, 0, xd_dram[0], table)
        stage(experts, 0, xd_dram[0], yd_dram[0], table, [folded, rest0])
        stage(combine, X, yd_dram[0], None)
        stage(multiscale_attention, X)
        stage(route, X, 1, xd_dram[1], table)
        stage(experts, 1, xd_dram[1], yd_dram[1], table, [rec1])
        stage(combine, X, yd_dram[1], out)


def small_tensors(I):
    f4 = np.float32
    eye = np.eye(C, dtype=f4)
    lane = np.arange(C)
    qkv, qkv_b, proj = I["L0_conv_qkv_w"], I["L0_conv_qkv_b"], I["L0_conv_proj_w"]
    wv = np.zeros((C, HEADS, VH), f4)
    wv[:, :, :CH] = qkv[2 * C:].T.reshape(C, HEADS, CH)
    bv = np.ones((C, 2, HEADS, VH), f4)
    bv[:, :, :, :CH] = qkv_b[2 * C:].reshape(1, 1, HEADS, CH)
    proj_heads = np.zeros((2, HEADS // 2, VH, C), f4)
    proj_heads[:, :, :CH] = proj.T.reshape(2, HEADS // 2, CH, C)
    row_ids = np.zeros((C, 2, Q, 2), f4)
    row_ids[:] = (lane[:, None, None, None] + TILE * np.arange(2)[:, None, None] + C * np.arange(Q)[:, None]
                  + TOKENS * np.arange(2))
    blank_rows = SPARE + TILE * np.arange(BLANKS)[:, None] + Q * lane[:, None, None] + np.arange(Q)
    chunks = np.arange(3 * C).reshape(HEADS, 3, CH).transpose(1, 0, 2).reshape(-1)
    pw = I["L1_conv_w_pw"][:, :, 0, 0][chunks].reshape(3, C // 8, 8, 8)
    c_pw = np.zeros((3, C // 8, 8, C // 8, 8), f4)
    for g in range(C // 8):
        c_pw[:, g, :, g, :] = pw[:, g].transpose(0, 2, 1)
    w = dict(
        ident=eye, centre=eye - f4(1 / C), mean=np.full((C, C), 1 / C), before_f=np.triu(np.ones((C, C)), 1),
        group=np.kron(np.eye(C // 4), np.full((4, 4), 0.25)), eps=np.tile([1e-6, 1e-5, 1e-10, 1e-15], (C, 1)),
        wqk=qkv[:2 * C].T, wv=wv.reshape(C, -1), bqk=qkv_b[:2 * C].reshape(2, C).T, bv=bv.reshape(C, -1),
        gn=np.stack([I["L0_conv_gn_w"], I["L0_conv_gn_b"]], 1), wproj=proj.T,
        wproj_heads=proj_heads.reshape(2, C, C).transpose(1, 0, 2).reshape(C, -1), bproj=I["L0_conv_proj_b"].reshape(C, 1),
        moe0_router=I["L0_ffn_router_w"], moe0_router_bias=np.tile(I["L0_ffn_router_b"], (C, Q)),
        moe1_router=I["L1_ffn_gate_w"], moe1_router_bias=np.zeros((C, Q * E)),
        ln=np.stack([I["L1_ffn_ln_g"], I["L1_ffn_ln_b"]], 1), firstness=np.tile(np.arange(E, 0, -1), (C, Q)),
        region=np.tile(np.arange(E) * REGION * TILE, (C, 1)), row_ids=row_ids.reshape(C, -1),
        k_tile=np.tile(np.arange(TOKENS // TILE) * TILE, (C, E)), tile_no=np.tile(np.arange(TILES), (C, 1)),
        zeros=np.zeros((C, E)), blank_rows=blank_rows.reshape(C, -1),
        c_qkv=I["L1_conv_w_qkv"][:, :, 0, 0][chunks].T,
        c_dw=I["L1_conv_w_dw"].reshape(3 * C, -1)[chunks].reshape(3, C, -1).transpose(1, 0, 2).reshape(C, -1),
        c_pw=c_pw.reshape(3, C, C).transpose(1, 0, 2).reshape(C, -1),
        c_proj=I["L1_conv_w_proj"][:, :, 0, 0].T.reshape(2, C, C).transpose(1, 0, 2).reshape(C, -1),
        bn=np.stack([I["L1_conv_bn_" + n] for n in ("gamma", "beta", "mean", "var")], 1),
        heads=np.kron(np.eye(HEADS), np.ones((CH, CH))))
    return {k: np.ascontiguousarray(v, f4) for k, v in w.items()}


def expert_tensors(I):
    def interleaved(g, v):
        g, v = (a.reshape(a.shape[:-1] + (2, 1, C)) for a in (g, v))
        return np.concatenate([g, v], -2).reshape(g.shape[:-3] + (4, C))

    def down(w2, b2, n):
        blocks = w2.reshape(E, n, C, C).transpose(0, 2, 1, 3).reshape(E, C, n * C)
        return np.concatenate([blocks, np.broadcast_to(b2[:, None, :], (E, C, C))], 2)

    b = np.concatenate([I["L0_ffn_b1"].reshape(E, 2, C), interleaved(I["L0_ffn_bg"], I["L0_ffn_bv"])], 1)
    big = dict(
        w1=I["L0_ffn_w1"], wgv=interleaved(I["L0_ffn_wg"], I["L0_ffn_wv"]).reshape(E, 2 * C, 4 * C),
        b_gv=b.transpose(0, 2, 1), rest0=down(I["L0_ffn_w2"], I["L0_ffn_b2"], 2),
        rec1=np.concatenate([I["L1_ffn_w1"], I["L1_ffn_b1"].reshape(E, 4, C).transpose(0, 2, 1),
                             down(I["L1_ffn_w2"], I["L1_ffn_b2"], 4)], 2))
    return {k: np.ascontiguousarray(v, np.float32) for k, v in big.items()}


def kernel(**inputs):
    import concourse.bacc as bacc
    from concourse.bass_utils import run_bass_kernel_spmd

    I = {k: np.asarray(v) for k, v in inputs.items()}
    nc = bacc.Bacc("TRN2", target_bir_lowering=False, num_devices=1)
    arrays = {}

    def declare(name, a):
        arrays[name] = a
        return nc.dram_tensor(name, a.shape, F32, kind="ExternalInput").ap()

    x_in = declare("x", np.ascontiguousarray(I["x"].reshape(B, C, T)))
    weights = {k: declare("w_" + k, v) for k, v in small_tensors(I).items()}
    big = {k: declare("e_" + k, v) for k, v in expert_tensors(I).items()}
    out = nc.dram_tensor("out", (B, C, T), F32, kind="ExternalOutput").ap()
    metaformer(nc, x_in, weights, big["w1"], big["wgv"], big["b_gv"], big["rest0"], big["rec1"], out)
    r = run_bass_kernel_spmd(nc, [arrays], core_ids=[0])
    return r.results[0]["out"].reshape(I["x"].shape)
```

```python
from contextlib import ExitStack

import numpy as np
import concourse.bass as bass
from concourse import mybir

F32 = mybir.dt.float32
BF16 = mybir.dt.bfloat16
ALU = mybir.AluOpType
ACT = mybir.ActivationFunctionType
AX = mybir.AxisListType

C = 128
B = 8
T = 1024
HALF = 512
HEADS = 8
CH = C // HEADS
VH = 2 * CH
TC = T // C
QK_SCALE = 0.5
Q_PARTS = (0, 0, 0, 1, 1, 2)
K_PARTS = (0, 1, 2, 0, 1, 0)
KB = len(Q_PARTS) * CH
KM = KB + 3


LN_EXP_TABLES = 6


def load_tables(nc, act, tables):
    act.add_instruction(mybir.InstLoadActFuncSet(name=nc.get_next_instruction_name(), ins=[], outs=[],
                                                 engine=mybir.EngineType.Activation, act_func_set_id=tables))


def split_in_three(eng, value, rest, parts, done, b, held=None):
    if held is not None:
        eng.sem_inc(held, 1)
    eng.tensor_copy(parts[:, 0], value).then_inc(done, 1)
    eng.wait_ge(done, b * 4 + 1)
    eng.tensor_tensor(rest, value, parts[:, 0], ALU.subtract).then_inc(done, 1)
    eng.wait_ge(done, b * 4 + 2)
    if held is not None:
        eng.sem_inc(held, 1)
    eng.tensor_copy(parts[:, 1], rest).then_inc(done, 1)
    eng.wait_ge(done, b * 4 + 3)
    eng.tensor_tensor(parts[:, 2], rest, parts[:, 1], ALU.subtract).then_inc(done, 1)


def normalize_and_project(nc, sb, sem, bank, w, X, XF, parts_dram, v_dram):
    xc = sb("xc", [C, T], F32)
    sq = sb("sq", [C, T], F32)
    rstd = sb("rstd", [C, T], F32)
    normed = sb("normed", [C, 2, T], F32)
    qk = sb("qk", [C, 2, T], F32)
    rest = sb("rest", [C, 2, T], F32)
    parts = sb("parts", [C, 2, 2, 3, T], BF16)
    vt = sb("vt", [C, 2, TC * HEADS * VH], F32)
    bqk = sb("bqk", [C, 2], F32)
    bn = sb("bn", [C, 2, 6], F32)
    mv = sb("mv", [C, 3], F32)
    gmean = sb("gmean", [C, 1], F32)
    gvar = sb("gvar", [C, 1], F32)
    gmean2 = sb("gmean2", [C, 1], F32)
    glog = sb("glog", [C, 1], F32)
    grs = sb("grs", [C, 1], F32)
    ga = sb("ga", [C, 1], F32)
    gma = sb("gma", [C, 1], F32)
    gb = sb("gb", [C, 1], F32)
    bias_scaled = sem("bias_scaled")
    centred, xc_copied, squared, var_ready = sem("centred"), sem("xc_copied"), sem("squared"), sem("var_ready")
    ln_logged, rstd_ready, xf_ready = sem("ln_logged"), sem("rstd_ready"), sem("xf_ready")
    stats_part, stats_ready, group_ready = sem("stats_part"), sem("stats_ready"), sem("group_ready")
    gmean_ready, gvar_ready, g_logged, grs_ready = sem("gmean_ready"), sem("gvar_ready"), sem("g_logged"), sem("grs_ready")
    gab_ready, normed_ready, qk_ready, qk_biased = sem("gab_ready"), sem("normed_ready"), sem("qk_ready"), sem("qk_biased")
    first_parts, second_parts = sem("first_parts"), sem("second_parts")
    q_rest, k_rest, q_split, k_split = sem("q_rest"), sem("k_rest"), sem("q_split"), sem("k_split")
    v_ready, v_copied, stats_held = sem("v_ready"), sem("v_copied"), sem("stats_held")
    parts_stored, v_stored = sem("parts_stored"), sem("v_stored")

    def half(n):
        return slice(n * HALF, (n + 1) * HALF)

    def over_images(eng, step):
        step(None, None, 0, 0)
        with eng.Fori(0, B // 2 - 1) as i:
            step(2 * i, 0, 2 * i + 1, 1)
            step(2 * i + 1, 1, 2 * i + 2, 0)
        step(B - 2, 0, B - 1, 1)
        step(B - 1, 1, None, None)

    with nc.Block() as block:
        @block.sync
        def _(sp):
            def store(b, p):
                sp.wait_ge(v_copied, b * 4 + 4)
                sp.dma_start(v_dram[bass.ds(b, 1)].rearrange("o c n -> c (o n)"), vt[:, p]).then_inc(v_stored, 16)
                sp.wait_ge(q_split, b + 1)
                sp.dma_start(parts_dram[bass.ds(b, 1), 0].rearrange("o w c t -> c (o w) t"), parts[:, p, 0]).then_inc(parts_stored, 16)
                sp.wait_ge(k_split, b + 1)
                sp.dma_start(parts_dram[bass.ds(b, 1), 1].rearrange("o w c t -> c (o w) t"), parts[:, p, 1]).then_inc(parts_stored, 16)

            with sp.Fori(0, B // 2) as i:
                store(2 * i, 0)
                store(2 * i + 1, 1)
            sp.wait_ge(v_stored, 16 * B)
            sp.wait_ge(parts_stored, 32 * B)

        @block.tensor
        def _(pe):
            for b in range(B):
                pe.wait_ge(w.x_loaded[b], 16)

            def step(b, p, nb, np_):
                if nb is not None:
                    pe.wait_ge(xc_copied, nb * 2)
                    for n in range(2):
                        pe.matmul(bank[:, n, :], w["centre"], X[:, bass.ds(nb * T + n * HALF, HALF)],
                                  start=True, stop=True).then_inc(centred, 1)
                if b is not None:
                    pe.wait_ge(v_copied, b * 4)
                    pe.wait_ge(normed_ready, b + 1)
                for s in range(2):
                    if s == 1 and nb is not None:
                        pe.wait_ge(gvar_ready, nb)
                        for n in range(2):
                            pe.wait_ge(squared, nb * 2 + n + 1)
                            pe.matmul(bank[:, 2 + n, :], w["mean"], sq[:, half(n)], start=True, stop=True).then_inc(var_ready, 1)
                    for n in range(2) if b is not None else ():
                        pe.matmul(bank[:, 4 + 2 * s + n, :], w["wqk"][:, s * C:(s + 1) * C],
                                  normed[:, p, half(n)], start=True, stop=True).then_inc(qk_ready, 1)
                for v in range(4) if b is not None else ():
                    pe.wait_ge(qk_biased, b * 4 + v + 1)
                    for u in range(2):
                        c = 2 * v + u
                        ins = pe.matmul(bank[:, 4 + v, 256 * u:256 * u + 256], normed[:, p, c * C:(c + 1) * C],
                                        w["wv"], start=True, stop=True)
                    ins.then_inc(v_ready, 1)
                if nb is not None:
                    pe.wait_ge(stats_ready, nb + 1)
                    pe.matmul(bank[:, 2, 0:3], w["group"], mv[:], start=True, stop=True).then_inc(group_ready, 1)

            over_images(pe, step)

        @block.scalar
        def _(act):
            act.activation(bqk[:], w["bqk"], ACT.Copy, scale=QK_SCALE).then_inc(bias_scaled, 1)
            act.wait_ge(bias_scaled, 1)

            def project(b, s):
                if s == 0:
                    act.wait_ge(q_rest, b)
                    act.wait_ge(k_rest, b)
                for n in range(2):
                    act.wait_ge(qk_ready, b * 4 + 2 * s + n + 1)
                    act.activation(qk[:, s, half(n)], bank[:, 4 + 2 * s + n, :], ACT.Identity,
                                   bias=bqk[:, s:s + 1], scale=QK_SCALE).then_inc(qk_biased, 1)

            def step(b, p, nb, np_):
                if nb is not None:
                    act.wait_ge(var_ready, nb * 2)
                    for n in range(2):
                        act.wait_ge(xc_copied, nb * 2 + n + 1)
                        act.activation(sq[:, half(n)], xc[:, half(n)], ACT.Square).then_inc(squared, 1)
                if b is not None:
                    project(b, 0)
                if nb is not None:
                    act.wait_ge(xf_ready, nb * 2)
                    for n in range(2):
                        act.wait_ge(var_ready, nb * 2 + n + 1)
                        act.activation(rstd[:, half(n)], bank[:, 2 + n, :], ACT.Ln, bias=w["eps"][:, 0:1]).then_inc(ln_logged, 1)
                    for n in range(2):
                        act.wait_ge(ln_logged, nb * 2 + n + 1)
                        act.activation(rstd[:, half(n)], rstd[:, half(n)], ACT.Exp, scale=-0.5).then_inc(rstd_ready, 1)
                if b is not None:
                    project(b, 1)
                    for s in range(2):
                        act.wait_ge(parts_stored, (b // 2 * 64) if isinstance(b, int) else (b - p) * 32)
                        act.wait_ge(qk_biased, b * 4 + 2 * s + 2)
                        act.activation(parts[:, p, s, 0], qk[:, s], ACT.Copy).then_inc(first_parts, 1)
                if nb is not None:
                    act.wait_ge(gvar_ready, nb + 1)
                    act.activation(glog[:], gvar[:], ACT.Ln, bias=w["eps"][:, 1:2]).then_inc(g_logged, 1)
                    act.wait_ge(g_logged, nb + 1)
                    act.activation(grs[:], glog[:], ACT.Exp, scale=-0.5).then_inc(grs_ready, 1)
                if b is not None:
                    for s, rest_ready in enumerate((q_rest, k_rest)):
                        act.wait_ge(rest_ready, b + 1)
                        act.activation(parts[:, p, s, 1], rest[:, s], ACT.Copy).then_inc(second_parts, 1)

            over_images(act, step)

        def split_rest(eng, s, b, p, rest_ready):
            eng.wait_ge(q_split if s == 0 else k_split, b)
            eng.wait_ge(first_parts, b * 2 + s + 1)
            eng.tensor_tensor(rest[:, s], qk[:, s], parts[:, p, s, 0], ALU.subtract).then_inc(rest_ready, 1)

        def split_last(eng, s, b, p, split):
            eng.wait_ge(second_parts, b * 2 + s + 1)
            eng.tensor_tensor(parts[:, p, s, 2], rest[:, s], parts[:, p, s, 1], ALU.subtract).then_inc(split, 1)

        @block.vector
        def _(dve):
            def copy_v(b, p, v):
                dve.wait_ge(v_ready, b * 4 + v + 1)
                dve.tensor_tensor(vt[:, p, half(v)], bank[:, 4 + v, :], w["bv"], ALU.add).then_inc(v_copied, 1)

            def step(b, p, nb, np_):
                if nb is not None:
                    for n in range(2):
                        dve.wait_ge(centred, nb * 2 + n + 1)
                        dve.tensor_copy(xc[:, half(n)], bank[:, n, :]).then_inc(xc_copied, 1)
                    for n in range(2):
                        dve.wait_ge(xc_copied, nb * 2 + n + 1)
                        dve.wait_ge(rstd_ready, nb * 2 + n + 1)
                        dve.tensor_tensor(XF[:, bass.ds(nb * T + n * HALF, HALF)], xc[:, half(n)], rstd[:, half(n)],
                                          ALU.mult).then_inc(xf_ready, 1)
                    for n in range(2):
                        dve.wait_ge(xf_ready, nb * 2 + n + 1)
                        dve.sem_inc(stats_held, 1)
                        dve.bn_stats(bn[:, n, :], XF[:, bass.ds(nb * T + n * HALF, HALF)]).then_inc(stats_part, 1)
                    dve.wait_ge(stats_part, nb * 3 + 2)
                    dve.sem_inc(stats_held, 1)
                    dve.bn_aggr(mv[:, 0:2], bn[:]).then_inc(stats_part, 1)
                    dve.wait_ge(stats_part, nb * 3 + 3)
                    dve.scalar_tensor_tensor(out=mv[:, 2:3], in0=mv[:, 0:1], scalar=mv[:, 0:1], in1=mv[:, 1:2],
                                             op0=ALU.mult, op1=ALU.add).then_inc(stats_ready, 1)
                if b is not None:
                    dve.wait_ge(v_stored, (b // 2 * 32) if isinstance(b, int) else (b - p) * 16)
                    copy_v(b, p, 0)
                    copy_v(b, p, 1)
                if nb is not None:
                    dve.wait_ge(group_ready, nb + 1)
                    dve.tensor_copy(gmean[:], bank[:, 2, 0:1]).then_inc(gmean_ready, 1)
                    dve.wait_ge(gmean_ready, nb * 2 + 1)
                    dve.tensor_tensor(gmean2[:], gmean[:], gmean[:], ALU.mult).then_inc(gmean_ready, 1)
                    dve.wait_ge(gmean_ready, nb * 2 + 2)
                    dve.tensor_tensor(gvar[:], bank[:, 2, 2:3], gmean2[:], ALU.subtract).then_inc(gvar_ready, 1)
                if b is not None:
                    copy_v(b, p, 2)
                    copy_v(b, p, 3)
                    split_rest(dve, 0, b, p, q_rest)
                if nb is not None:
                    dve.wait_ge(grs_ready, nb + 1)
                    dve.tensor_tensor(ga[:], grs[:], w["gn"][:, 0:1], ALU.mult).then_inc(gab_ready, 1)
                    dve.wait_ge(gab_ready, nb * 3 + 1)
                    dve.tensor_tensor(gma[:], gmean[:], ga[:], ALU.mult).then_inc(gab_ready, 1)
                    dve.wait_ge(gab_ready, nb * 3 + 2)
                    dve.tensor_tensor(gb[:], w["gn"][:, 1:2], gma[:], ALU.subtract).then_inc(gab_ready, 1)
                    dve.wait_ge(gab_ready, nb * 3 + 3)
                    if b is not None:
                        dve.wait_ge(v_ready, b * 4)
                    dve.tensor_scalar(normed[:, np_], XF[:, bass.ds(nb * T, T)], ga[:, 0:1], gb[:, 0:1],
                                      ALU.mult, ALU.add).then_inc(normed_ready, 1)
                if b is not None:
                    split_last(dve, 0, b, p, q_split)

            over_images(dve, step)

        @block.gpsimd
        def _(pool):
            def step(b, p, nb, np_):
                if b is not None:
                    split_rest(pool, 1, b, p, k_rest)
                    split_last(pool, 1, b, p, k_split)

            over_images(pool, step)


STEPS = 32
SLOTS = 4
FIRST, OWN = 129, 130


def units_of(prev, more):
    units = [("max", k) for k in range(2 * HEADS * TC)] if more else []
    units.insert(3, ("rows", 1))
    if more:
        units.insert(68, ("rows", 0))
    if prev:
        at = 30 if more else 1
        units[at:at] = [("proj", 0), ("proj", 1)]
    return units


FIRST_UNITS = [unit for unit in units_of(False, True) if unit != ("rows", 1)]


def units_before(b):
    return (OWN + 2) * b + FIRST + OWN - (OWN + 2)


def attention(nc, sb, sem, bank, w, X, XF, parts_dram, v_dram):
    qs = sb("qs", [KM, 2, HEADS, T], BF16)
    ks = sb("ks", [KM, 2, HEADS, T], BF16)
    vt = sb("vt", [C, 2, TC, HEADS * VH], F32)
    P = sb("P", [C, SLOTS, 2 * HALF], F32)
    mx = sb("mx", [C, 64, 2], F32)
    nm = sb("nm", [C, 64], F32)
    nmT = sb("nmT", [32, C], F32)
    nm_rest = sb("nm_rest", [32, C], F32)
    nm_parts = sb("nm_parts", [32, 3, C], BF16)
    o = sb("o", [C, HALF], F32)
    den = sb("den", [C, HALF], F32)
    rden = sb("rden", [C, HALF], F32)
    a = sb("a", [C, 2, T], F32)
    ones_set, rows_loaded, v_loaded = sem("ones_set"), sem("rows_loaded"), sem("v_loaded")
    qk_loaded = [sem("qk0_loaded"), sem("qk1_loaded")]
    unit_filled, unit_freed, negated, rows_split = sem("unit_filled"), sem("unit_freed"), sem("negated"), sem("rows_split")
    scores_ready, probs_ready, pv_done = sem("scores_ready"), sem("probs_ready"), sem("pv_done")
    o_copied, den_ready, den_logged, rden_ready, a_ready = (
        sem("o_copied"), sem("den_ready"), sem("den_logged"), sem("rden_ready"), sem("a_ready"))
    held, split_held = sem("held"), sem("split_held")
    LOADS = 16 * (len(Q_PARTS) + len(K_PARTS))

    def over_images(eng, first, body, last):
        first()
        body(0, None, 0, FIRST, False, True)
        with eng.Fori(0, B // 2 - 1) as i:
            body(2 * i + 1, 2 * i, 1, units_before(2 * i + 1), True, True)
            body(2 * i + 2, 2 * i + 1, 0, units_before(2 * i + 2), True, True)
        body(B - 1, B - 2, 1, units_before(B - 1), True, False)
        last()

    LAST = units_before(B - 1) + len(units_of(True, False))

    def units_at(e, units):
        if len(units) < STEPS:
            return [(index, unit) for index, unit in enumerate(units) if e == (0 if unit[0] == "rows" else 6)]
        return list(enumerate(units))[e * len(units) // STEPS:(e + 1) * len(units) // STEPS]

    with nc.Block() as block:
        @block.sync
        def _(sp):
            def load_qk(b, par, g):
                for r, (qp, kp) in enumerate(zip(Q_PARTS, K_PARTS)):
                    for s, part, stack in ((0, qp, qs), (1, kp, ks)):
                        src = parts_dram[bass.ds(b, 1), s, part, g * C // 2:(g + 1) * C // 2].rearrange("o (h i) t -> i (o h) t", i=CH)
                        sp.dma_start(stack[r * CH:(r + 1) * CH, par, 4 * g:4 * g + 4], src).then_inc(qk_loaded[g], 16)

            def load_v(b, par):
                sp.dma_start(vt[:, par].rearrange("c s n -> c (s n)"),
                             v_dram[bass.ds(b, 1)].rearrange("o c n -> c (o n)")).then_inc(v_loaded, 16)

            def max_rows(b, par, g):
                sp.wait_ge(rows_split, b * 8 + 4 * g + 4)
                for part in range(3):
                    sp.dma_start(qs[KB + part:KB + part + 1, par, 4 * g:4 * g + 4, :]
                                 .rearrange("p h (c t) -> p (h c) t", t=C),
                                 nm_parts[:, part, :]).then_inc(rows_loaded, 16)

            def first():
                load_qk(0, 0, 0)
                load_qk(0, 0, 1)
                load_v(0, 0)
                max_rows(0, 0, 0)
                load_qk(1, 1, 0)

            def body(b, par, prev, more, ahead):
                if more:
                    if prev:
                        sp.wait_ge(pv_done, b * STEPS)
                    load_qk(b + 1, 1 - par, 1)
                    load_v(b + 1, 1 - par)
                max_rows(b, par, 1)
                if ahead:
                    sp.wait_ge(pv_done, b * STEPS + STEPS // 2)
                    load_qk(b + 2, par, 0)
                if more:
                    max_rows(b + 1, 1 - par, 0)

            first()
            body(0, 0, False, True, True)
            with sp.Fori(0, B // 2 - 2) as i:
                body(2 * i + 1, 1, True, True, True)
                body(2 * i + 2, 0, True, True, True)
            body(B - 3, 1, True, True, True)
            body(B - 2, 0, True, True, False)
            body(B - 1, 1, True, False, False)
            sp.wait_ge(rows_loaded, B * 96)

        @block.tensor
        def _(pe):
            def rows(b, g, slot):
                pe.wait_ge(negated, b * 2 + g + 1)
                pe.transpose(bank[0:32, slot, 0:C], nm[:, 32 * g:32 * g + 32], w["ident"]).then_inc(unit_filled, 1)

            def take_max(b, par, k, slot):
                h, c, half = k // 16, k // 2 % TC, k % 2
                if k % 64 == 0:
                    pe.wait_ge(qk_loaded[k // 64], (b + 1) * LOADS)
                pe.matmul(bank[:, slot, :], qs[0:KB, par, h, c * C:(c + 1) * C],
                          ks[0:KB, par, h, half * HALF:(half + 1) * HALF], start=True, stop=True).then_inc(unit_filled, 1)

            def project(b, n, slot):
                if n == 0:
                    pe.wait_ge(a_ready, b * 4 + 4)
                pe.matmul(bank[:, slot, :], w["wproj"], XF[:, bass.ds(b * T + n * HALF, HALF)], start=True, stop=False)
                for g in range(2):
                    ins = pe.matmul(bank[:, slot, :], w["wproj_heads"][:, g * C:(g + 1) * C],
                                    a[:, g, n * HALF:(n + 1) * HALF], start=False, stop=(g == 1))
                ins.then_inc(unit_filled, 1)

            def first():
                for index, (kind, k) in enumerate(FIRST_UNITS):
                    if index >= 3:
                        pe.wait_ge(unit_freed, index - 2)
                    if kind == "max":
                        take_max(0, 0, k, 5 + index % 3)
                    else:
                        rows(0, 0, 5 + index % 3)

            def weigh(b, par, e):
                g, n, s = e // 16, e // 8 % 2, e % 8
                pe.wait_ge(probs_ready, b * 2 * STEPS + 2 * e + 2)
                if e == 0:
                    pe.wait_ge(v_loaded, (b + 1) * 16)
                if s == 0:
                    pe.wait_ge(o_copied, b * 4 + 2 * g + n)
                for j in range(4):
                    head = 4 * g + j
                    ins = pe.matmul(bank[32 * j:32 * j + 32, 4, :], vt[:, par, s, head * VH:(head + 1) * VH],
                                    P[:, (2 * e + j // 2) % SLOTS, j % 2 * HALF:(j % 2 + 1) * HALF],
                                    start=(s == 0), stop=(s == 7))
                ins.then_inc(pv_done, 1)

            def body(b, before, par, base, prev, more):
                units = units_of(prev, more)
                for e in range(STEPS):
                    g, n, s = e // 16, e // 8 % 2, e % 8
                    now = units_at(e, units)
                    for pair in range(2):
                        x = 2 * e + pair
                        if e == 0 and pair == 0 and not prev:
                            pe.wait_ge(ones_set, 1)
                        if e % 16 == 0 and pair == 0:
                            pe.wait_ge(rows_loaded, b * 96 + 48 * g + 48)
                        pe.wait_ge(probs_ready, b * 2 * STEPS + (x - 1 if prev else max(x - 1, 0)))
                        for u in range(2):
                            head = 4 * g + 2 * pair + u
                            ins = pe.matmul(bank[:, 2 * pair + u, :], ks[:, par, head, s * C:(s + 1) * C],
                                            qs[:, par, head, n * HALF:(n + 1) * HALF], start=True, stop=True)
                        ins.then_inc(scores_ready, 1)
                        for index, (kind, k) in now[:2] if pair == 0 else now[2:]:
                            slot = 5 + index % 3
                            pe.wait_ge(unit_freed, base + max(index - 2, 0))
                            if kind == "max":
                                take_max(b + 1, 1 - par, k, slot)
                            elif kind == "rows":
                                rows(b if k else b + 1, k, slot)
                            else:
                                project(before, k, slot)
                    if e:
                        weigh(b, par, e - 1)
                    elif prev:
                        weigh(before, 1 - par, STEPS - 1)

            def last():
                weigh(B - 1, (B - 1) % 2, STEPS - 1)
                pe.wait_ge(unit_freed, LAST)
                for n in range(2):
                    project(B - 1, n, 5 + n)

            over_images(pe, first, body, last)

        @block.scalar
        def _(act):
            def numerators(b, q):
                act.wait_ge(pv_done, b * STEPS + 8 * q + 8)
                act.wait_ge(a_ready, b * 4 + q)
                act.activation(o[:], bank[:, 4, :], ACT.Copy).then_inc(o_copied, 1)

            def reciprocal(b, q):
                act.wait_ge(den_ready, b * 4 + q + 1)
                act.wait_ge(a_ready, b * 4 + q)
                act.activation(rden[:], den[:], ACT.Ln).then_inc(den_logged, 1)
                act.wait_ge(den_logged, b * 4 + q + 1)
                act.activation(rden[:], rden[:], ACT.Exp, scale=-1.0).then_inc(rden_ready, 1)

            def body(b, before, par, base, prev, more):
                for e in range(STEPS):
                    image, q = (b, e // 8 - 1) if e >= 8 else (before, 3)
                    act.wait_ge(pv_done, b * STEPS + (e - 1 if prev else max(e - 1, 0)))
                    if e % 8 == 1 and (prev or e >= 8):
                        numerators(image, q)
                    for pair in range(2):
                        x = 2 * e + pair
                        act.wait_ge(scores_ready, b * 2 * STEPS + x + 1)
                        act.activation(P[:, x % SLOTS, :], bank[:, 2 * pair:2 * pair + 2, :]
                                       .rearrange("p a t -> p (a t)"), ACT.Exp).then_inc(probs_ready, 1)
                    if e % 8 == 2 and (prev or e >= 8):
                        reciprocal(image, q)

            def last():
                numerators(B - 1, 3)
                reciprocal(B - 1, 3)

            over_images(act, lambda: None, body, last)

        @block.vector
        def _(dve):
            def reduce(k, slot, filled):
                dve.wait_ge(unit_filled, filled)
                dve.tensor_reduce(mx[:, k // 2, k % 2:k % 2 + 1], bank[:, slot, :], AX.X, ALU.max).then_inc(unit_freed, 1)
                if k % 64 == 63:
                    g = k // 64
                    dve.wait_ge(unit_freed, filled)
                    dve.tensor_reduce(nm[:, 32 * g:32 * g + 32], mx[:, 32 * g:32 * g + 32, :], AX.X, ALU.max,
                                      negate=True).then_inc(negated, 1)

            def rows(b, g, slot, filled):
                dve.wait_ge(unit_filled, filled)
                dve.wait_ge(rows_split, b * 8 + 4 * g)
                dve.tensor_copy(nmT[:], bank[0:32, slot, 0:C]).then_inc(unit_freed, 1)

            def add(b, n, slot, filled):
                cols = X[:, bass.ds(b * T + n * HALF, HALF)]
                dve.wait_ge(unit_filled, filled)
                dve.scalar_tensor_tensor(out=cols, in0=bank[:, slot, :], scalar=w["bproj"], in1=cols,
                                         op0=ALU.add, op1=ALU.add).then_inc(unit_freed, 1)

            def sums(b, q):
                dve.wait_ge(o_copied, b * 4 + q + 1)
                dve.wait_ge(den_logged, b * 4 + q)
                dve.sem_inc(held, 1)
                dve.stream_shuffle(den[:], o[:], [CH + i % CH for i in range(32)]).then_inc(den_ready, 1)

            def first():
                for unit, (kind, k) in enumerate(FIRST_UNITS):
                    if kind == "max":
                        reduce(k, 5 + unit % 3, unit + 1)
                    else:
                        rows(0, 0, 5 + unit % 3, unit + 1)

            def body(b, before, par, base, prev, more):
                units = units_of(prev, more)
                for e in range(STEPS):
                    for index, (kind, k) in units_at(e, units):
                        slot, filled = 5 + index % 3, base + index + 1
                        if kind == "max":
                            reduce(k, slot, filled)
                        elif kind == "rows":
                            rows(b if k else b + 1, k, slot, filled)
                        else:
                            add(before, k, slot, filled)
                    if e % 8 == 1 and (prev or e >= 8):
                        sums(*((b, e // 8 - 1) if e >= 8 else (before, 3)))

            def last():
                sums(B - 1, 3)
                for n in range(2):
                    add(B - 1, n, 5 + n, LAST + n + 1)
                dve.wait_ge(unit_freed, LAST + 2)

            over_images(dve, first, body, last)

        @block.gpsimd
        def _(pool):
            def split_rows(b, g, freed):
                pool.wait_ge(unit_freed, freed)
                pool.wait_ge(rows_loaded, b * 96 + 48 * g)
                split_in_three(pool, nmT[:], nm_rest[:], nm_parts[:], rows_split, b * 2 + g, split_held)

            def divide(b, q, used=None):
                pool.wait_ge(rden_ready, b * 4 + q + 1)
                if used is not None:
                    pool.wait_ge(unit_filled, used)
                g, n = q // 2, q % 2
                pool.tensor_tensor(a[:, g, n * HALF:(n + 1) * HALF], o[:], rden[:], ALU.mult).then_inc(a_ready, 1)

            def first():
                pool.memset(ks[KB:KM, :, :, :], 1.0).then_inc(ones_set, 1)
                split_rows(0, 0, FIRST_UNITS.index(("rows", 0)) + 1)

            def body(b, before, par, base, prev, more):
                units = units_of(prev, more)
                split_rows(b, 1, base + units.index(("rows", 1)) + 1)
                if prev:
                    divide(before, 3)
                divide(b, 0, base + units.index(("proj", 1)) + 1 if prev else None)
                if more:
                    row_unit = units.index(("rows", 0))
                    divide(b, 1)
                    split_rows(b + 1, 0, base + row_unit + 1)
                else:
                    divide(b, 1)
                divide(b, 2)

            over_images(pool, first, body, lambda: divide(B - 1, 3))


class Weights:

    def __init__(self, nc, sb, sem, columns):
        self.loaded, self.x_loaded = sem("weights_loaded"), [sem(f"x{b}_loaded") for b in range(B)]
        self.all = sb("weights", [C, sum(columns.values())], F32)
        self.at, first = {}, 0
        for name, n in columns.items():
            self.at[name] = (first, first + n)
            first += n
        ones, before = sb("ones", [C, C], BF16), sb("before", [C, C], BF16)
        self.ones, self.before = ones[:], before[:]
        self.cast = sem("constants_cast")

    def __getitem__(self, name):
        first, end = self.at[name]
        return self.all[:, first:end]


E = 8
TOKENS = B * T
TILE = 512
Q = TILE // C
ROW = C + 2
REGION = TOKENS // TILE + 1
TILES = 40
RING = 4
IDLE = TILES - 2 * TOKENS // TILE
UNITS_XD = E * REGION + IDLE
BLANKS = E + IDLE
SPARE = 2 * TOKENS


def route(nc, sb, sem, bank, w, X, layer, xd_dram, table):
    second = layer == 1
    k = f"moe{layer}_"
    xc = sb("xc", [C, 2, TILE], F32)
    sq = sb("sq", [C, 2, TILE], F32)
    rs = sb("rs", [C, 2, TILE], F32)
    rs2 = sb("rs2", [C, 2, TILE], F32)
    xl = sb("xl", [C, 2, TILE], F32)
    xn = sb("xn", [C, 2, TILE], F32)
    rows = sb("rows", [C, 2, Q, 2, ROW], F32)
    places = sb("places", [C, 2, Q, 2], mybir.dt.uint32)
    small = {n: sb(n, [C, Q, E], F32) for n in
             ("logits", "shifted", "e", "p", "eq", "key", "best", "p2", "eq2", "key2", "second", "slot", "at")}
    per = {n: sb(n, [C, Q], F32) for n in ("lmax", "esum", "rsum", "g1", "k1", "g2", "k2")}
    per["place"] = sb("place", [C, Q, 2], F32)
    ids = sb("ids", [C, 2, Q, 2], F32)
    count = sb("count", [C, E], F32)
    blank = sb("blank", [C, BLANKS, Q * ROW], F32)
    mask = sb("mask", [C, Q, E], BF16)
    base = sb("base", [C, E], F32)
    count16 = sb("count16", [C, E, 16], F32)
    tiles = sb("tiles", [C, E], F32)
    ends = sb("ends", [C, E], F32)
    pad = sb("pad", [C, E], F32)
    passed = sb("passed", [C, TILES, E], F32)
    skip = sb("skip", [C, TILES, E], F32)
    ex = sb("ex", [C, TILES], F32)
    un = sb("un", [C, TILES], F32)
    base_i = sb("base_i", [C, E], mybir.dt.int32)
    centred, copied, squared, var_ready = sem("centred"), sem("copied"), sem("squared"), sem("var_ready")
    logged, rstd_ready, xn_ready, router_ready = sem("logged"), sem("rstd_ready"), sem("xn_ready"), sem("router_ready")
    turned, rows_ready, exp_ready, mask_ready = sem("turned"), sem("rows_ready"), sem("exp_ready"), sem("mask_ready")
    ranked, step, gates_ready, sent = sem("ranked"), sem("step"), sem("gates_ready"), [sem("sent0"), sem("sent1")]
    planned, blanks_sent, base_set, blank_ready = sem("planned"), sem("blanks_sent"), sem("base_set"), sem("blank_ready")
    fence, normed_once = sem("fence"), sem("normed_once")
    STEPS_TILE = 23

    with nc.Block() as block:
        @block.tensor
        def _(pe):
            with pe.Fori(0, TOKENS // TILE // 2) as i:
                for p in range(2):
                    pe.wait_ge(copied, 2 * i + p)
                    pe.matmul(bank[:, 4 * p, :], w["centre"], X[:, bass.ds((2 * i + p) * TILE, TILE)],
                              start=True, stop=True).then_inc(centred, 1)
                for p in range(2):
                    pe.wait_ge(squared, 2 * i + p + 1)
                    pe.matmul(bank[:, 4 * p + 1, :], w["mean"], sq[:, p, :], start=True, stop=True).then_inc(var_ready, 1)
                for p in range(2):
                    pe.wait_ge(xn_ready, 2 * i + p + 1)
                    for q in range(Q):
                        ins = pe.matmul(bank[:, 4 * p + 2, q * E:(q + 1) * E], xn[:, p, q * C:(q + 1) * C],
                                        w[k + "router"], start=True, stop=True)
                    ins.then_inc(router_ready, 1)
                    pe.wait_ge(rows_ready, 2 * i)
                    for q in range(Q):
                        ins = pe.transpose(bank[:, 4 * p + 3, q * C:(q + 1) * C], xn[:, p, q * C:(q + 1) * C], w["ident"])
                    ins.then_inc(turned, 1)
                for p in range(2):
                    pe.wait_ge(mask_ready, 2 * i + p + 1)
                    for q in range(Q + 1):
                        out = bank[:, 4 * p + 2, 64 + q * E:64 + (q + 1) * E]
                        for q2 in range(q):
                            ins = pe.matmul(out, w.ones, mask[:, q2, :], start=(q2 == 0), stop=(q == Q and q2 == q - 1))
                        if q < Q:
                            ins = pe.matmul(out, w.before, mask[:, q, :], start=(q == 0), stop=True)
                    ins.then_inc(ranked, 1)

        @block.scalar
        def _(act):
            load_tables(nc, act, LN_EXP_TABLES)
            with act.Fori(0, TOKENS // TILE // 2) as i:
                for p in range(2):
                    act.wait_ge(copied, 2 * i + p + 1)
                    act.activation(sq[:, p, :], xc[:, p, :], ACT.Square).then_inc(squared, 1)
                for p in range(2):
                    act.wait_ge(var_ready, 2 * i + p + 1)
                    act.wait_ge(xn_ready, 2 * i)
                    act.activation(rs[:, p, :], bank[:, 4 * p + 1, :], ACT.Ln, bias=w["eps"][:, 1:2]).then_inc(logged, 1)
                    if second:
                        act.activation(rs2[:, p, :], bank[:, 4 * p + 1, :], ACT.Ln, bias=w["eps"][:, 2:3],
                                       scale=1.0 + 1e-5).then_inc(logged, 1)
                m = 2 if second else 1
                for p in range(2):
                    act.wait_ge(logged, (2 * i + p + 1) * m)
                    act.activation(rs[:, p, :], rs[:, p, :], ACT.Exp, scale=-0.5).then_inc(rstd_ready, 1)
                    if second:
                        act.activation(rs2[:, p, :], rs2[:, p, :], ACT.Exp, scale=-0.5).then_inc(rstd_ready, 1)
                for p in range(2):
                    act.wait_ge(turned, 2 * i + p + 1)
                    act.wait_ge(sent[p], i * 16 * 2 * Q)
                    act.activation(rows[:, p, :, :, 0:C], bank[:, 4 * p + 3, :].rearrange("t (q c) -> t q c", q=Q)
                                   .unsqueeze(2).to_broadcast([C, Q, 2, C]), ACT.Copy).then_inc(rows_ready, 1)
                for p in range(2):
                    act.wait_ge(step, (2 * i + p) * STEPS_TILE + 3)
                    act.activation(small["e"][:], small["shifted"][:], ACT.Exp).then_inc(exp_ready, 1)

        @block.vector
        def _(dve):
            dve.tensor_copy(base[:], w["region"])
            dve.tensor_copy(ids[:].rearrange("t p q c -> t (p q c)"), w["row_ids"]).then_inc(base_set, 1)
            dve.wait_ge(base_set, 1)
            with dve.Fori(0, TOKENS // TILE // 2) as i:
                for p in range(2):
                    dve.wait_ge(centred, 2 * i + p + 1)
                    dve.tensor_copy(xc[:, p, :], bank[:, 4 * p, :]).then_inc(copied, 1)
                for p in range(2):
                    t = 2 * i + p
                    if not second:
                        dve.wait_ge(rstd_ready, t + 1)
                        dve.wait_ge(turned, 2 * i)
                        dve.tensor_tensor(xn[:, p, :], xc[:, p, :], rs[:, p, :], ALU.mult).then_inc(xn_ready, 1)
                        continue
                    dve.wait_ge(rstd_ready, 2 * t + 2)
                    dve.wait_ge(turned, 2 * i)
                    dve.tensor_tensor(xl[:, p, :], xc[:, p, :], rs[:, p, :], ALU.mult).then_inc(normed_once, 1)
                    dve.tensor_tensor(rs2[:, p, :], xc[:, p, :], rs2[:, p, :], ALU.mult).then_inc(normed_once, 1)
                    dve.wait_ge(normed_once, 2 * t + 1)
                    tokens = X[:, bass.ds(t * TILE, TILE)]
                    dve.tensor_tensor(tokens, tokens, xl[:, p, :], ALU.add)
                    dve.wait_ge(normed_once, 2 * t + 2)
                    dve.tensor_scalar(xn[:, p, :], rs2[:, p, :], w["ln"][:, 0:1], w["ln"][:, 1:2],
                                      ALU.mult, ALU.add).then_inc(xn_ready, 1)
                for p in range(2):
                    t = 2 * i + p
                    done = [0]
                    s, v = small, per
                    wide = lambda a: a[:].unsqueeze(2).to_broadcast([C, Q, E])

                    def then(ins):
                        ins.then_inc(step, 1)
                        done[0] += 1
                        dve.wait_ge(step, t * STEPS_TILE + done[0])

                    dve.wait_ge(router_ready, t + 1)
                    then(dve.tensor_tensor(s["logits"][:].rearrange("t q e -> t (q e)"), bank[:, 4 * p + 2, 0:Q * E],
                                           w[k + "router_bias"], ALU.add))
                    then(dve.tensor_reduce(v["lmax"][:], s["logits"][:], AX.X, ALU.max))
                    then(dve.tensor_tensor(s["shifted"][:], s["logits"][:], wide(v["lmax"]), ALU.subtract))
                    dve.wait_ge(exp_ready, t + 1)
                    then(dve.tensor_reduce(v["esum"][:], s["e"][:], AX.X, ALU.add))
                    then(dve.reciprocal(v["rsum"][:], v["esum"][:]))
                    then(dve.tensor_tensor(s["p"][:], s["e"][:], wide(v["rsum"]), ALU.mult))
                    for probs, gate, eq, key, kmax, hot in (("p", "g1", "eq", "key", "k1", "best"),
                                                            ("p2", "g2", "eq2", "key2", "k2", "second")):
                        if hot == "second":
                            then(dve.scalar_tensor_tensor(out=s["p2"][:], in0=s["best"][:], scalar=-2.0, in1=s["p"][:],
                                                          op0=ALU.mult, op1=ALU.add))
                        then(dve.tensor_reduce(v[gate][:], s[probs][:], AX.X, ALU.max))
                        then(dve.tensor_tensor(s[eq][:], s[probs][:], wide(v[gate]), ALU.is_equal))
                        then(dve.tensor_tensor(s[key][:].rearrange("t q e -> t (q e)"),
                                               s[eq][:].rearrange("t q e -> t (q e)"), w["firstness"], ALU.mult))
                        then(dve.tensor_reduce(v[kmax][:], s[key][:], AX.X, ALU.max))
                        then(dve.tensor_tensor(s[hot][:], s[key][:], wide(v[kmax]), ALU.is_equal))
                    dve.wait_ge(ranked, t)
                    dve.tensor_tensor(mask[:], s["best"][:], s["second"][:], ALU.add).then_inc(mask_ready, 1)
                    dve.wait_ge(rows_ready, t + 1)
                    dve.tensor_copy(rows[:, p, :, 0, C:C + 1], v["g1"][:].unsqueeze(2))
                    dve.tensor_copy(rows[:, p, :, 1, C:C + 1], v["g2"][:].unsqueeze(2))
                    dve.tensor_copy(rows[:, p, :, :, C + 1:C + 2], ids[:, p].unsqueeze(3))
                    then(dve.tensor_scalar(ids[:, p], ids[:, p], 2.0 * TILE, None, ALU.add))
                    dve.wait_ge(ranked, t + 1)
                    then(dve.tensor_tensor(s["slot"][:], bank[:, 4 * p + 2, 64:64 + Q * E].rearrange("t (q e) -> t q e", q=Q),
                                           base[:].unsqueeze(1).to_broadcast([C, Q, E]), ALU.add))
                    dve.tensor_tensor(base[:], base[:], bank[:, 4 * p + 2, 64 + Q * E:64 + (Q + 1) * E], ALU.add)
                    for c, hot in enumerate(("best", "second")):
                        then(dve.tensor_tensor(s["at"][:], s["slot"][:], s[hot][:], ALU.mult))
                        then(dve.tensor_reduce(v["place"][:, :, c:c + 1], s["at"][:], AX.X, ALU.add))
                    dve.tensor_copy(places[:, p], v["place"][:]).then_inc(gates_ready, 1)
                    assert done[0] == STEPS_TILE
            done = [0]

            def plan(ins):
                ins.then_inc(planned, 1)
                done[0] += 1
                dve.wait_ge(planned, done[0])

            dve.wait_ge(gates_ready, TOKENS // TILE)
            plan(dve.tensor_copy(base_i[:], base[:]))
            plan(dve.tensor_tensor(count[:], base[:], w["region"], ALU.subtract))
            plan(dve.tensor_tensor(count16[:], count[:].unsqueeze(2).to_broadcast([C, E, 16]),
                                   w["k_tile"].rearrange("t (e k) -> t e k", e=E), ALU.is_gt))
            plan(dve.tensor_reduce(tiles[:], count16[:], AX.X, ALU.add))
            plan(dve.tensor_tensor_scan(ends[:], tiles[:], w["zeros"][:, 0:E], 0.0, ALU.add, ALU.add))
            plan(dve.tensor_scalar(pad[:], tiles[:], -1.0, float(REGION), ALU.mult, ALU.add))
            plan(dve.tensor_tensor(passed[:], ends[:].unsqueeze(1).to_broadcast([C, TILES, E]),
                                   w["tile_no"].unsqueeze(2).to_broadcast([C, TILES, E]), ALU.is_le))
            plan(dve.tensor_reduce(ex[:], passed[:], AX.X, ALU.add))
            plan(dve.tensor_tensor(skip[:], passed[:], pad[:].unsqueeze(1).to_broadcast([C, TILES, E]), ALU.mult))
            plan(dve.tensor_reduce(un[:], skip[:], AX.X, ALU.add))
            plan(dve.tensor_tensor(un[:], un[:], w["tile_no"], ALU.add))
            plan(dve.tensor_scalar(table[:, 0, :], ex[:], float(E - 1), None, ALU.min))
            plan(dve.tensor_scalar(table[:, 1, :], un[:], 1.0, None, ALU.mult))

        @block.gpsimd
        def _(pool):
            pool.memset(blank[:], 0.0).then_inc(blank_ready, 1)
            pool.wait_ge(blank_ready, 1)
            pool.tensor_copy(blank[:].rearrange("t n (q r) -> t (n q) r", q=Q)[:, :, ROW - 1:ROW],
                             w["blank_rows"].unsqueeze(2)).then_inc(blank_ready, 1)
            with pool.Fori(0, TOKENS // TILE // 2) as i:
                for p in range(2):
                    pool.wait_ge(gates_ready, 2 * i + p + 1)
                    pool.sem_inc(fence, 1)
                    for q in range(Q):
                        for c in range(2):
                            pool.indirect_dma_start(xd_dram, bass.IndirectOffsetOnAxis(places[:, p, q, c:c + 1], 0),
                                                    rows[:, p, q, c, :], None).then_inc(sent[p], 16)
            for p in range(2):
                pool.wait_ge(sent[p], TOKENS // TILE // 2 * 16 * 2 * Q)

        @block.sync
        def _(sp):
            sp.wait_ge(blank_ready, 2)
            for n in range(IDLE):
                sp.dma_start(xd_dram[(E * REGION + n) * TILE:(E * REGION + n + 1) * TILE, :]
                             .rearrange("(t q) r -> t (q r)", q=Q), blank[:, E + n]).then_inc(blanks_sent, 16)
            sp.wait_ge(planned, 1)
            for e in range(E):
                first = sp.value_load(base_i[0:1, e:e + 1], min_val=0, max_val=E * REGION * TILE)
                sp.dma_start(xd_dram[bass.ds(first, TILE), :].rearrange("(t q) r -> t (q r)", q=Q),
                             blank[:, e]).then_inc(blanks_sent, 16)
            sp.wait_ge(blanks_sent, 16 * BLANKS)


def experts(nc, sb, sem, bank, w, layer, xd_dram, yd_dram, table, records):
    second = layer == 1
    FB = 4 * C
    NH = 4 if second else 2
    W2 = FB + 4
    B2 = W2 + NH * C
    REC = B2 + C
    rec = sb("rec", [C, RING, REC], F32)
    xr = sb("xr", [C, RING, Q, ROW], F32)
    xt = sb("xt", [C, 2, TILE], F32)
    hidden = sb("hidden", [C, 2, NH, TILE], F32)
    gate = sb("gate", [C, 2, TILE], F32)
    y1 = sb("y1", [C, 2, Q, C], F32)
    yo = sb("yo", [C, 2, Q, C], F32)
    places = sb("places", [C, 2, Q], mybir.dt.uint32)
    loaded = [sem(f"loaded{r}") for r in range(RING)]
    turned, xt_copied, g_ready, v_ready, gated = sem("turned"), sem("xt_copied"), sem("g_ready"), sem("v_ready"), sem("gated")
    h_ready, y_ready, y_copied, yo_ready, fence = sem("h_ready"), sem("y_ready"), sem("y_copied"), sem("yo_ready"), sem("fence")
    sent = [sem("sent0"), sem("sent1")]
    LOADS = 16 * (len(records) + 1)

    def over_tiles(eng, ahead, behind):
        def at(step, group, r):
            group, r = group + r // RING, r % RING
            step(RING * group + r, r, r % 2, RING // 2 * group + r // 2, group)

        at(ahead, 0, 0)
        with eng.Fori(0, TILES // RING - 1) as group:
            for r in range(RING):
                at(ahead, group, r + 1)
                at(behind, group, r)
        last = TILES // RING - 1
        for r in range(RING):
            if r < RING - 1:
                at(ahead, last, r + 1)
            at(behind, last, r)

    with nc.Block() as block:
        @block.sync
        def _(sp):
            def load(j, r):
                e = sp.value_load(table[0:1, 0, bass.ds(j, 1)], min_val=0, max_val=E - 1)
                u = sp.value_load(table[0:1, 1, bass.ds(j, 1)], min_val=0, max_val=UNITS_XD - 1)
                at = 0
                for record in records:
                    n = record.shape[2]
                    sp.dma_start(rec[:, r, at:at + n],
                                 record[bass.ds(e, 1)].rearrange("o c n -> c (o n)")).then_inc(loaded[r], 16)
                    at += n
                sp.dma_start(xr[:, r].rearrange("t q r -> t (q r)"),
                             xd_dram[bass.ds(u * TILE, TILE), :].rearrange("(t q) r -> t (q r)", q=Q)).then_inc(loaded[r], 16)

            for r in range(RING):
                load(r, r)
            with sp.Fori(0, TILES // RING - 1) as i:
                for r in range(RING):
                    sp.wait_ge(yo_ready, RING * i + r + 1)
                    load(RING * (i + 1) + r, r)

        @block.tensor
        def _(pe):
            def ahead(j, r, p, h, i):
                pe.wait_ge(loaded[r], (i + 1) * LOADS)
                for q in range(Q):
                    ins = pe.transpose(bank[:, p, q * C:(q + 1) * C], xr[:, r, q, 0:C], w["ident"])
                ins.then_inc(turned, 1)
                pe.wait_ge(xt_copied, j + 1)
                for f in range(4):
                    if not (isinstance(j, int) and j == 0):
                        if second:
                            pe.wait_ge(h_ready, (j - 1) * 4 + f + 1)
                        elif f % 2:
                            pe.wait_ge(h_ready, (j - 1) * 2 + f // 2 + 1)
                        else:
                            pe.wait_ge(gated, (j - 1) * 2 + f // 2 + 1)
                    ins = pe.matmul(bank[:, 2 + f, :], rec[:, r, f * C:(f + 1) * C], xt[:, p, :], start=True, stop=True)
                    ins.then_inc(g_ready if second or f % 2 == 0 else v_ready, 1)

            def behind(j, r, p, h, i):
                pe.wait_ge(h_ready, (j + 1) * NH)
                pe.wait_ge(y_copied, 2 * h)
                for q in range(Q):
                    for f in range(NH):
                        ins = pe.matmul(bank[:, 6 + p, q * C:(q + 1) * C], hidden[:, p, f, q * C:(q + 1) * C],
                                        rec[:, r, W2 + f * C:W2 + (f + 1) * C], start=(f == 0), stop=(f == NH - 1))
                ins.then_inc(y_ready, 1)

            over_tiles(pe, ahead, behind)

        @block.scalar
        def _(act):
            def ahead(j, r, p, h, i):
                act.wait_ge(y_ready, 2 * h)
                for f in range(NH):
                    act.wait_ge(g_ready, j * NH + f + 1)
                    if second:
                        act.activation(hidden[:, p, f, :], bank[:, 2 + f, :], ACT.Gelu,
                                       bias=rec[:, r, FB + f:FB + f + 1]).then_inc(h_ready, 1)
                    else:
                        if f == 0:
                            act.wait_ge(h_ready, j * 2)
                        act.activation(gate[:, f, :], bank[:, 2 + 2 * f, :], ACT.Silu,
                                       bias=rec[:, r, FB + 2 * f:FB + 2 * f + 1]).then_inc(gated, 1)

            over_tiles(act, ahead, lambda *_: None)

        @block.vector
        def _(dve):
            def ahead(j, r, p, h, i):
                dve.wait_ge(turned, j + 1)
                dve.tensor_copy(xt[:, p, :], bank[:, p, :]).then_inc(xt_copied, 1)
                if not second:
                    dve.wait_ge(y_ready, 2 * h)
                    for f in range(2):
                        dve.wait_ge(gated, j * 2 + f + 1)
                        dve.wait_ge(v_ready, j * 2 + f + 1)
                        dve.scalar_tensor_tensor(out=hidden[:, p, f, :], in0=bank[:, 3 + 2 * f, :],
                                                 scalar=rec[:, r, FB + 2 * f + 1:FB + 2 * f + 2], in1=gate[:, f, :],
                                                 op0=ALU.add, op1=ALU.mult).then_inc(h_ready, 1)

            def behind(j, r, p, h, i):
                dve.wait_ge(y_ready, j + 1)
                dve.tensor_tensor(y1[:, p], bank[:, 6 + p, :].rearrange("t (q c) -> t q c", q=Q),
                                  rec[:, r, B2:B2 + C].unsqueeze(1).to_broadcast([C, Q, C]), ALU.add).then_inc(y_copied, 1)
                dve.wait_ge(sent[p], h * (16 * Q))
                dve.tensor_scalar(places[:, p], xr[:, r, :, C + 1], 0.0, None, ALU.add)
                dve.wait_ge(y_copied, j + 1)
                dve.tensor_tensor(yo[:, p], y1[:, p], xr[:, r, :, C:C + 1].to_broadcast([C, Q, C]), ALU.mult).then_inc(yo_ready, 1)

            over_tiles(dve, ahead, behind)

        @block.gpsimd
        def _(pool):
            with pool.Fori(0, TILES // 2) as i:
                for p in range(2):
                    pool.wait_ge(yo_ready, 2 * i + p + 1)
                    pool.sem_inc(fence, 1)
                    for q in range(Q):
                        pool.indirect_dma_start(yd_dram, bass.IndirectOffsetOnAxis(places[:, p, q:q + 1], 0),
                                                yo[:, p, q, :], None).then_inc(sent[p], 16)
            for p in range(2):
                pool.wait_ge(sent[p], TILES // 2 * 16 * Q)


def combine(nc, sb, sem, bank, w, X, yd_dram, out):
    y = sb("y", [C, 2, 2, Q * C], F32)
    total = sb("total", [C, 2, Q * C], F32)
    loaded = [sem("loaded0"), sem("loaded1")]
    summed, turned, added, stored = sem("summed"), sem("turned"), sem("added"), sem("stored")
    PAIRS = TOKENS // TILE // 2

    with nc.Block() as block:
        @block.sync
        def _(sp):
            with sp.Fori(0, PAIRS) as i:
                for p in range(2):
                    sp.wait_ge(summed, 2 * i)
                    for c in range(2):
                        src = yd_dram[bass.ds((2 * i + p) * TILE + c * TOKENS, TILE), :].rearrange("(t q) c -> t (q c)", q=Q)
                        sp.dma_start(y[:, p, c, :], src).then_inc(loaded[p], 16)

        @block.vector
        def _(dve):
            with dve.Fori(0, PAIRS) as i:
                for p in range(2):
                    dve.wait_ge(loaded[p], (i + 1) * 32)
                    dve.wait_ge(turned, 2 * i)
                    dve.tensor_tensor(total[:, p, :], y[:, p, 0, :], y[:, p, 1, :], ALU.add).then_inc(summed, 1)
                for p in range(2):
                    t = 2 * i + p
                    dve.wait_ge(turned, t + 1)
                    tokens = X[:, bass.ds(t * TILE, TILE)].rearrange("c (t q) -> c q t", q=Q)
                    dve.tensor_tensor(tokens, tokens, bank[:, p, :].rearrange("c (q t) -> c q t", q=Q),
                                      ALU.add).then_inc(added, 1)

        @block.tensor
        def _(pe):
            with pe.Fori(0, PAIRS) as i:
                for p in range(2):
                    pe.wait_ge(summed, 2 * i + p + 1)
                    pe.wait_ge(added, 2 * i)
                    for q in range(Q):
                        ins = pe.transpose(bank[:, p, q * C:(q + 1) * C], total[:, p, q * C:(q + 1) * C], w["ident"])
                    ins.then_inc(turned, 1)

        @block.gpsimd
        def _(pool):
            if out is None:
                return
            for b in range(B):
                pool.wait_ge(added, 2 * b + 2)
                pool.dma_start(out[b], X[:, b * T:(b + 1) * T]).then_inc(stored, 16)
            pool.wait_ge(stored, 16 * B)


W1_COLS, WGV_COLS = 2 * C, 2 * 4 * C


def load_and_fold(nc, sb, sem, bank, w, weights_dram, x_dram, X, fold_dram, folded):
    src = sb("src", [C, E, W1_COLS + WGV_COLS + 6], F32)
    w1t = sb("w1t", [C, 2, 2, C], F32)
    rec = sb("rec", [C, E, 4 * C + 4], F32)
    loaded = [sem(f"loaded{e}") for e in range(E)]
    turned, copied, product, biases = sem("turned"), sem("copied"), sem("product"), sem("biases")
    product_copied, biases_added, stored = sem("product_copied"), sem("biases_added"), sem("stored")

    def w1(e, k):
        return src[:, e, k * C:(k + 1) * C]

    def wgv(e, k):
        return src[:, e, W1_COLS + k * 4 * C:W1_COLS + (k + 1) * 4 * C]

    with nc.Block() as block:
        @block.sync
        def _(sp):
            sp.dma_start(w.all[:], weights_dram).then_inc(w.loaded, 16)
            for e in range(E):
                sp.dma_start(src[:, e], fold_dram[e]).then_inc(loaded[e], 16)
            for b in range(B):
                sp.dma_start(X[:, b * T:(b + 1) * T], x_dram[b]).then_inc(w.x_loaded[b], 16)

        @block.tensor
        def _(pe):
            pe.wait_ge(w.loaded, 16)

            def turn(e):
                pe.wait_ge(loaded[e], 16)
                if e >= 2:
                    pe.wait_ge(copied, e - 1)
                for k in range(2):
                    ins = pe.transpose(bank[:, e % 2, k * C:(k + 1) * C], w1(e, k), w["ident"])
                ins.then_inc(turned, 1)

            turn(0)
            for e in range(E):
                if e + 1 < E:
                    turn(e + 1)
                if e >= 2:
                    pe.wait_ge(biases_added, e - 1)
                for f in range(4):
                    for k in range(2):
                        ins = pe.matmul(bank[:, 4 + e % 2, f:f + 1], wgv(e, k)[:, f * C:(f + 1) * C],
                                        src[:, e, W1_COLS + WGV_COLS + k:W1_COLS + WGV_COLS + k + 1],
                                        start=(k == 0), stop=(k == 1))
                ins.then_inc(biases, 1)
                pe.wait_ge(copied, e + 1)
                for k in range(2):
                    ins = pe.matmul(bank[:, 2 + e % 2, :], w1t[:, e % 2, k, :], wgv(e, k), start=(k == 0), stop=(k == 1))
                ins.then_inc(product, 1)

        @block.vector
        def _(dve):
            dve.memset(w.ones, 1.0)
            dve.wait_ge(w.loaded, 16)
            dve.tensor_copy(w.before, w["before_f"]).then_inc(w.cast, 1)

            def copy_turned(e):
                dve.wait_ge(turned, e + 1)
                if e >= 2:
                    dve.wait_ge(product, e - 1)
                dve.tensor_copy(w1t[:, e % 2].rearrange("h k d -> h (k d)"), bank[:, e % 2, 0:2 * C]).then_inc(copied, 1)

            copy_turned(0)
            for e in range(E):
                if e + 1 < E:
                    copy_turned(e + 1)
                dve.wait_ge(product, e + 1)
                dve.tensor_copy(rec[:, e, 0:4 * C], bank[:, 2 + e % 2, :]).then_inc(product_copied, 1)
                dve.wait_ge(biases, e + 1)
                dve.tensor_tensor(rec[:, e, 4 * C:4 * C + 4], bank[:, 4 + e % 2, 0:4],
                                  src[:, e, W1_COLS + WGV_COLS + 2:W1_COLS + WGV_COLS + 6], ALU.add).then_inc(biases_added, 1)
            dve.wait_ge(w.cast, 1)

        @block.scalar
        def _(act):
            load_tables(nc, act, LN_EXP_TABLES)
            for e in range(E):
                act.wait_ge(product_copied, e + 1)
                act.wait_ge(biases_added, e + 1)
                act.dma_start(folded[e], rec[:, e]).then_inc(stored, 16)
            act.wait_ge(stored, E * 16)


SIDE = 32
TAPS = 5
PAD = TAPS // 2
WIDE = SIDE + 2 * PAD


def multiscale_attention(nc, sb, sem, bank, w, X):
    xc = sb("xc", [C, T], F32)
    sq = sb("sq", [C, T], F32)
    rs = sb("rs", [C, T], F32)
    xn = sb("xn", [C, T], F32)
    pads = [sb(f"pad_{s}", [C, WIDE, WIDE], F32) for s in "qkv"]
    dw = sb("dw", [C, 2, T], F32)
    av = sb("av", [C, T], F32)
    qr = sb("qr", [C, 2, T], F32)
    kT = sb("kT", [C, 2, TC, C], F32)
    vT = sb("vT", [C, 2, TC, C + 1], F32)
    vk = sb("vk", [C, 2, C + 1], F32)
    vkm = sb("vkm", [C, 2, C], F32)
    ksm = sb("ksm", [C, 2, C], F32)
    rd = sb("rd", [C, 4, HALF], F32)
    o = sb("o", [C, 4, HALF], F32)
    yb = sb("yb", [C, 2, HALF], F32)
    taps = sb("taps", [C, TAPS * TAPS, C], F32)
    inv = sb("inv", [C, 1], F32)
    shift = sb("shift", [C, 1], F32)
    bn_log = sb("bn_log", [C, 1], F32)
    fence = sem("fence")
    cleared, bn_step, taps_ready, bn_ready = sem("cleared"), sem("bn_step"), sem("taps_ready"), sem("bn_ready")
    centred, copied, squared, var_ready, logged = sem("centred"), sem("copied"), sem("squared"), sem("var_ready"), sem("logged")
    rstd_ready, xn_ready, qkv_ready, padded = sem("rstd_ready"), sem("xn_ready"), sem("qkv_ready"), sem("padded")
    kv_ready, kv_copied, dw_step, av_ready, av_copied = sem("kv_ready"), sem("kv_copied"), sem("dw_step"), sem("av_ready"), sem("av_copied")
    av_turned, vt_copied, qa_ready, qa_copied = sem("av_turned"), sem("vt_copied"), sem("qa_ready"), sem("qa_copied")
    ka_ready, ka_copied, vk_ready, vk_copied, masked = sem("ka_ready"), sem("ka_copied"), sem("vk_ready"), sem("vk_copied"), sem("masked")
    num_ready, den_logged, rden_ready, o_ready = sem("num_ready"), sem("den_logged"), sem("rden_ready"), sem("o_ready")
    proj_ready, y_ready, added = sem("proj_ready"), sem("y_ready"), sem("added")
    NT = TAPS * TAPS

    def window(pad, tap, n=None):
        dy, dx = tap // TAPS, tap % TAPS
        r0, r = (dy, SIDE) if n is None else (dy + n * SIDE // 2, SIDE // 2)
        return pad[:, r0:r0 + r, dx:dx + SIDE]

    with nc.Block() as block:
        @block.tensor
        def _(pe):
            with pe.Fori(0, B) as b:
                pe.wait_ge(added, 2 * b)
                for n in range(2):
                    pe.matmul(bank[:, n, :], w["centre"], X[:, bass.ds(b * T + n * HALF, HALF)],
                              start=True, stop=True).then_inc(centred, 1)
                for n in range(2):
                    pe.wait_ge(squared, b * 2 + n + 1)
                    pe.matmul(bank[:, 2 + n, :], w["mean"], sq[:, n * HALF:(n + 1) * HALF],
                              start=True, stop=True).then_inc(var_ready, 1)
                pe.wait_ge(xn_ready, b * 2 + 2)
                for s, slot in ((0, 4), (1, 6), (2, 0)):
                    for n in range(2):
                        pe.matmul(bank[:, slot + n, :], w["c_qkv"][:, s * C:(s + 1) * C], xn[:, n * HALF:(n + 1) * HALF],
                                  start=True, stop=True).then_inc(qkv_ready, 1)
                for u in range(4):
                    if u == 2:
                        pe.wait_ge(padded, b * 8 + 4)
                    for c in (2 * u, 2 * u + 1):
                        ins = pe.matmul(bank[:, 2 + u, c % 2 * 2 * C:(c % 2 + 1) * 2 * C], xn[:, c * C:(c + 1) * C],
                                        w["c_qkv"][:, C:3 * C], start=True, stop=True)
                    ins.then_inc(kv_ready, 1)
                pe.wait_ge(taps_ready, NT)
                pe.wait_ge(padded, b * 8 + 8)
                for tap in range(NT):
                    for n in range(2):
                        ins = pe.matmul(bank[:, 6 + n, :], taps[:, tap, :], window(pads[2], tap, n),
                                        start=(tap == 0), stop=(tap == NT - 1))
                ins.then_inc(av_ready, 1)
                pe.wait_ge(av_copied, b * 2 + 2)
                for n in range(2):
                    for q in range(4):
                        c = 4 * n + q
                        ins = pe.transpose(bank[:, n, q * C:(q + 1) * C], av[:, c * C:(c + 1) * C], w["ident"])
                    ins.then_inc(av_turned, 1)
                pe.wait_ge(kv_copied, b * 8 + 8)
                pe.wait_ge(dw_step, (b + 1) * 2 * NT)
                for n in range(2):
                    pe.matmul(bank[:, 2 + n, :], w["c_pw"][:, 0:C], dw[:, 0, n * HALF:(n + 1) * HALF],
                              start=True, stop=True).then_inc(qa_ready, 1)
                for n in range(2):
                    for q in range(4):
                        c = 4 * n + q
                        ins = pe.matmul(bank[:, 4 + n, q * C:(q + 1) * C], dw[:, 1, c * C:(c + 1) * C],
                                        w["c_pw"][:, C:2 * C], start=True, stop=True)
                    ins.then_inc(ka_ready, 1)
                for m in range(2):
                    if m == 1:
                        pe.wait_ge(vt_copied, b * 2 + 2)
                        pe.wait_ge(ka_copied, b * 2 + 2)
                    for c in range(TC):
                        ins = pe.matmul(bank[:, 6 + m, 0:C + 1], kT[:, m, c, :], vT[:, m, c, :],
                                        start=(c == 0), stop=(c == TC - 1))
                    ins.then_inc(vk_ready, 1)
                pe.wait_ge(qa_copied, b * 2 + 2)
                for m in range(2):
                    pe.wait_ge(masked, b * 2 + m + 1)
                    for n in range(2):
                        slot = 2 * (2 * m + n)
                        if slot == 6:
                            pe.wait_ge(masked, b * 2 + 2)
                        q = qr[:, m, n * HALF:(n + 1) * HALF]
                        pe.matmul(bank[:, slot, :], vkm[:, m, :], q, start=True, stop=True)
                        pe.matmul(bank[:, slot + 1, :], ksm[:, m, :], q, start=True, stop=True).then_inc(num_ready, 1)
                for n in range(2):
                    pe.wait_ge(o_ready, b * 4 + 3 + n)
                    for m in range(2):
                        ins = pe.matmul(bank[:, 1 + 2 * n, :], w["c_proj"][:, m * C:(m + 1) * C], o[:, 2 * m + n, :],
                                        start=(m == 0), stop=(m == 1))
                    ins.then_inc(proj_ready, 1)

        @block.scalar
        def _(act):
            load_tables(nc, act, LN_EXP_TABLES)
            act.wait_ge(bn_step, 1)
            act.activation(bn_log[:], w["bn"][:, 3:4], ACT.Ln, bias=w["eps"][:, 1:2]).then_inc(bn_step, 1)
            act.wait_ge(bn_step, 2)
            act.activation(bn_log[:], bn_log[:], ACT.Exp, scale=-0.5).then_inc(bn_step, 1)
            with act.Fori(0, B) as b:
                for n in range(2):
                    act.wait_ge(copied, b * 2 + n + 1)
                    act.activation(sq[:, n * HALF:(n + 1) * HALF], xc[:, n * HALF:(n + 1) * HALF], ACT.Square).then_inc(squared, 1)
                for n in range(2):
                    act.wait_ge(var_ready, b * 2 + n + 1)
                    act.activation(rs[:, n * HALF:(n + 1) * HALF], bank[:, 2 + n, :], ACT.Ln, bias=w["eps"][:, 0:1]).then_inc(logged, 1)
                for n in range(2):
                    act.wait_ge(logged, b * 2 + n + 1)
                    act.activation(rs[:, n * HALF:(n + 1) * HALF], rs[:, n * HALF:(n + 1) * HALF], ACT.Exp,
                                   scale=-0.5).then_inc(rstd_ready, 1)
                act.wait_ge(cleared, 4)
                for s, slot in ((0, 4), (1, 6), (2, 0)):
                    for n in range(2):
                        act.wait_ge(qkv_ready, b * 6 + 2 * s + n + 1)
                        rows = slice(PAD + n * SIDE // 2, PAD + (n + 1) * SIDE // 2)
                        act.activation(pads[s][:, rows, PAD:PAD + SIDE],
                                       bank[:, slot + n, :].rearrange("c (y x) -> c y x", x=SIDE), ACT.Copy).then_inc(padded, 1)
                        if s == 0:
                            act.activation(qr[:, 0, n * HALF:(n + 1) * HALF], bank[:, slot + n, :], ACT.Relu).then_inc(padded, 1)
                for u in range(4):
                    act.wait_ge(kv_ready, b * 4 + u + 1)
                    src = bank[:, 2 + u, :].rearrange("t (c s e) -> t c s e", c=2, s=2)
                    act.activation(kT[:, 0, 2 * u:2 * u + 2, :], src[:, :, 0, :], ACT.Relu).then_inc(kv_copied, 1)
                    act.activation(vT[:, 0, 2 * u:2 * u + 2, 0:C], src[:, :, 1, :], ACT.Copy).then_inc(kv_copied, 1)
                act.wait_ge(av_ready, b + 1)
                for n in range(2):
                    act.activation(av[:, n * HALF:(n + 1) * HALF], bank[:, 6 + n, :], ACT.Copy).then_inc(av_copied, 1)
                for n in range(2):
                    act.wait_ge(av_turned, b * 2 + n + 1)
                    act.activation(vT[:, 1, 4 * n:4 * n + 4, 0:C], bank[:, n, :].rearrange("t (c e) -> t c e", c=4),
                                   ACT.Copy).then_inc(vt_copied, 1)
                for n in range(2):
                    act.wait_ge(qa_ready, b * 2 + n + 1)
                    act.activation(qr[:, 1, n * HALF:(n + 1) * HALF], bank[:, 2 + n, :], ACT.Relu).then_inc(qa_copied, 1)
                for n in range(2):
                    act.wait_ge(ka_ready, b * 2 + n + 1)
                    act.activation(kT[:, 1, 4 * n:4 * n + 4, :].rearrange("t c e -> t (c e)"), bank[:, 4 + n, :],
                                   ACT.Relu).then_inc(ka_copied, 1)
                for m in range(4):
                    act.wait_ge(num_ready, b * 4 + m + 1)
                    act.activation(rd[:, m, :], bank[:, 2 * m + 1, :], ACT.Ln, bias=w["eps"][:, 3:4]).then_inc(den_logged, 1)
                    act.wait_ge(den_logged, b * 4 + m + 1)
                    act.activation(rd[:, m, :], rd[:, m, :], ACT.Exp, scale=-1.0).then_inc(rden_ready, 1)
                act.wait_ge(bn_ready, 1)
                for n in range(2):
                    act.wait_ge(proj_ready, b * 2 + n + 1)
                    act.activation(yb[:, n, :], bank[:, 1 + 2 * n, :], ACT.Identity, scale=inv[:, 0:1],
                                   bias=shift[:, 0:1]).then_inc(y_ready, 1)

        @block.vector
        def _(dve):
            dve.memset(vT[:], 1.0).then_inc(cleared, 1)
            dve.engine_nop().then_inc(bn_step, 1)
            dve.wait_ge(bn_step, 3)
            dve.tensor_tensor(inv[:], w["bn"][:, 0:1], bn_log[:], ALU.mult).then_inc(bn_step, 1)
            dve.wait_ge(bn_step, 4)
            dve.tensor_tensor(shift[:], w["bn"][:, 2:3], inv[:], ALU.mult).then_inc(bn_step, 1)
            dve.wait_ge(bn_step, 5)
            dve.tensor_tensor(shift[:], w["bn"][:, 1:2], shift[:], ALU.subtract).then_inc(bn_ready, 1)
            for tap in range(NT):
                dve.tensor_scalar(taps[:, tap, :], w["c_pw"][:, 2 * C:3 * C], w["c_dw"][:, 2 * NT + tap:2 * NT + tap + 1],
                                  None, ALU.mult).then_inc(taps_ready, 1)
            with dve.Fori(0, B) as b:
                for n in range(2):
                    dve.wait_ge(centred, b * 2 + n + 1)
                    dve.tensor_copy(xc[:, n * HALF:(n + 1) * HALF], bank[:, n, :]).then_inc(copied, 1)
                for n in range(2):
                    dve.wait_ge(rstd_ready, b * 2 + n + 1)
                    dve.tensor_tensor(xn[:, n * HALF:(n + 1) * HALF], xc[:, n * HALF:(n + 1) * HALF],
                                      rs[:, n * HALF:(n + 1) * HALF], ALU.mult).then_inc(xn_ready, 1)
                dve.wait_ge(padded, b * 8 + 6)
                for tap in range(NT):
                    for s in range(2):
                        plane = dw[:, s, :].rearrange("c (y x) -> c y x", x=SIDE)
                        weight = w["c_dw"][:, s * NT + tap:s * NT + tap + 1]
                        if tap == 0:
                            dve.tensor_scalar(plane, window(pads[s], tap), weight, None, ALU.mult).then_inc(dw_step, 1)
                        else:
                            dve.wait_ge(dw_step, b * 2 * NT + 2 * tap - 1 + s)
                            dve.scalar_tensor_tensor(out=plane, in0=window(pads[s], tap), scalar=weight, in1=plane,
                                                     op0=ALU.mult, op1=ALU.add).then_inc(dw_step, 1)
                for m in range(2):
                    dve.wait_ge(vk_ready, b * 2 + m + 1)
                    dve.tensor_copy(vk[:, m, :], bank[:, 6 + m, 0:C + 1]).then_inc(vk_copied, 1)
                    dve.wait_ge(vk_copied, b * 2 + m + 1)
                    dve.tensor_tensor(vkm[:, m, :], vk[:, m, 0:C], w["heads"], ALU.mult)
                    dve.tensor_scalar(ksm[:, m, :], w["heads"], vk[:, m, C:C + 1], None, ALU.mult).then_inc(masked, 1)
                for m in range(4):
                    dve.wait_ge(rden_ready, b * 4 + m + 1)
                    dve.tensor_tensor(o[:, m, :], bank[:, 2 * m, :], rd[:, m, :], ALU.mult).then_inc(o_ready, 1)
                for n in range(2):
                    dve.wait_ge(y_ready, b * 2 + n + 1)
                    cols = X[:, bass.ds(b * T + n * HALF, HALF)]
                    dve.tensor_tensor(cols, cols, yb[:, n, :], ALU.add).then_inc(added, 1)

        @block.gpsimd
        def _(pool):
            for pad in pads:
                pool.memset(pad[:], 0.0).then_inc(cleared, 1)




def metaformer(nc, x_in, columns, weights, to_fold, rest0, rec1, out):
    names = [0]

    def allocator(ctx, make):
        def allocate(name, *args):
            names[0] += 1
            return ctx.enter_context(make(f"{name}_{names[0]}", *args))
        return allocate

    def stage(run, *args):
        signals = []

        def own_sem(name):
            names[0] += 1
            signals.append(nc.alloc_semaphore(name=f"{name}_{names[0]}"))
            return signals[-1]

        with ExitStack() as own:
            run(nc, allocator(own, nc.sbuf_tensor), own_sem, bank, w, *args)
        nc.clear_and_free_semaphores(signals)
        nc.all_engine_barrier()

    parts_dram = nc.dram_tensor("qk_parts", (B, 2, 3, C, T), BF16).ap()
    v_dram = nc.dram_tensor("v_turned", (B, C, TC * HEADS * VH), F32).ap()
    folded = nc.dram_tensor("folded", (E, C, 4 * C + 4), F32).ap()
    xd_dram = [nc.dram_tensor(f"dispatched{n}", (UNITS_XD * TILE, ROW), F32).ap() for n in range(2)]
    yd_dram = [nc.dram_tensor(f"results{n}", (SPARE + BLANKS * TILE, C), F32).ap() for n in range(2)]

    with ExitStack() as ctx:
        sb, sem = allocator(ctx, nc.sbuf_tensor), allocator(ctx, nc.semaphore)
        bank = ctx.enter_context(nc.psum_tensor("bank", [C, 8, HALF], F32))
        w = Weights(nc, sb, sem, columns)
        X = sb("X", [C, TOKENS], F32)
        table = sb("table", [C, 2, TILES], mybir.dt.int32)
        stage(load_and_fold, weights, x_in, X, to_fold, folded)
        with ExitStack() as own:
            XF = allocator(own, nc.sbuf_tensor)("XF", [C, TOKENS], F32)
            stage(normalize_and_project, X, XF, parts_dram, v_dram)
            stage(attention, X, XF, parts_dram, v_dram)
        stage(route, X, 0, xd_dram[0], table)
        stage(experts, 0, xd_dram[0], yd_dram[0], table, [folded, rest0])
        stage(combine, X, yd_dram[0], None)
        stage(multiscale_attention, X)
        stage(route, X, 1, xd_dram[1], table)
        stage(experts, 1, xd_dram[1], yd_dram[1], table, [rec1])
        stage(combine, X, yd_dram[1], out)


def small_tensors(I):
    f4 = np.float32
    eye = np.eye(C, dtype=f4)
    lane = np.arange(C)
    qkv, qkv_b, proj = I["L0_conv_qkv_w"], I["L0_conv_qkv_b"], I["L0_conv_proj_w"]
    wv = np.zeros((C, HEADS, VH), f4)
    wv[:, :, :CH] = qkv[2 * C:].T.reshape(C, HEADS, CH)
    bv = np.ones((C, 2, HEADS, VH), f4)
    bv[:, :, :, :CH] = qkv_b[2 * C:].reshape(1, 1, HEADS, CH)
    proj_heads = np.zeros((2, HEADS // 2, VH, C), f4)
    proj_heads[:, :, :CH] = proj.T.reshape(2, HEADS // 2, CH, C)
    row_ids = np.zeros((C, 2, Q, 2), f4)
    row_ids[:] = (lane[:, None, None, None] + TILE * np.arange(2)[:, None, None] + C * np.arange(Q)[:, None]
                  + TOKENS * np.arange(2))
    blank_rows = SPARE + TILE * np.arange(BLANKS)[:, None] + Q * lane[:, None, None] + np.arange(Q)
    chunks = np.arange(3 * C).reshape(HEADS, 3, CH).transpose(1, 0, 2).reshape(-1)
    pw = I["L1_conv_w_pw"][:, :, 0, 0][chunks].reshape(3, C // 8, 8, 8)
    c_pw = np.zeros((3, C // 8, 8, C // 8, 8), f4)
    for g in range(C // 8):
        c_pw[:, g, :, g, :] = pw[:, g].transpose(0, 2, 1)
    w = dict(
        ident=eye, centre=eye - f4(1 / C), mean=np.full((C, C), 1 / C), before_f=np.triu(np.ones((C, C)), 1),
        group=np.kron(np.eye(C // 4), np.full((4, 4), 0.25)), eps=np.tile([1e-6, 1e-5, 1e-10, 1e-15], (C, 1)),
        wqk=qkv[:2 * C].T, wv=wv.reshape(C, -1), bqk=qkv_b[:2 * C].reshape(2, C).T, bv=bv.reshape(C, -1),
        gn=np.stack([I["L0_conv_gn_w"], I["L0_conv_gn_b"]], 1), wproj=proj.T,
        wproj_heads=proj_heads.reshape(2, C, C).transpose(1, 0, 2).reshape(C, -1), bproj=I["L0_conv_proj_b"].reshape(C, 1),
        moe0_router=I["L0_ffn_router_w"], moe0_router_bias=np.tile(I["L0_ffn_router_b"], (C, Q)),
        moe1_router=I["L1_ffn_gate_w"], moe1_router_bias=np.zeros((C, Q * E)),
        ln=np.stack([I["L1_ffn_ln_g"], I["L1_ffn_ln_b"]], 1), firstness=np.tile(np.arange(E, 0, -1), (C, Q)),
        region=np.tile(np.arange(E) * REGION * TILE, (C, 1)), row_ids=row_ids.reshape(C, -1),
        k_tile=np.tile(np.arange(TOKENS // TILE) * TILE, (C, E)), tile_no=np.tile(np.arange(TILES), (C, 1)),
        zeros=np.zeros((C, E)), blank_rows=blank_rows.reshape(C, -1),
        c_qkv=I["L1_conv_w_qkv"][:, :, 0, 0][chunks].T,
        c_dw=I["L1_conv_w_dw"].reshape(3 * C, -1)[chunks].reshape(3, C, -1).transpose(1, 0, 2).reshape(C, -1),
        c_pw=c_pw.reshape(3, C, C).transpose(1, 0, 2).reshape(C, -1),
        c_proj=I["L1_conv_w_proj"][:, :, 0, 0].T.reshape(2, C, C).transpose(1, 0, 2).reshape(C, -1),
        bn=np.stack([I["L1_conv_bn_" + n] for n in ("gamma", "beta", "mean", "var")], 1),
        heads=np.kron(np.eye(HEADS), np.ones((CH, CH))))
    return {k: np.ascontiguousarray(v, f4) for k, v in w.items()}


def expert_tensors(I):
    def interleaved(g, v):
        g, v = (a.reshape(a.shape[:-1] + (2, 1, C)) for a in (g, v))
        return np.concatenate([g, v], -2).reshape(g.shape[:-3] + (4, C))

    def down(w2, b2, n):
        blocks = w2.reshape(E, n, C, C).transpose(0, 2, 1, 3).reshape(E, C, n * C)
        return np.concatenate([blocks, np.broadcast_to(b2[:, None, :], (E, C, C))], 2)

    b = np.concatenate([I["L0_ffn_b1"].reshape(E, 2, C), interleaved(I["L0_ffn_bg"], I["L0_ffn_bv"])], 1)
    wgv = interleaved(I["L0_ffn_wg"], I["L0_ffn_wv"]).reshape(E, 2, C, 4 * C).transpose(0, 2, 1, 3).reshape(E, C, -1)
    big = dict(
        to_fold=np.concatenate([I["L0_ffn_w1"], wgv, b.transpose(0, 2, 1)], 2), rest0=down(I["L0_ffn_w2"], I["L0_ffn_b2"], 2),
        rec1=np.concatenate([I["L1_ffn_w1"], I["L1_ffn_b1"].reshape(E, 4, C).transpose(0, 2, 1),
                             down(I["L1_ffn_w2"], I["L1_ffn_b2"], 4)], 2))
    return {k: np.ascontiguousarray(v, np.float32) for k, v in big.items()}


def kernel(**inputs):
    import concourse.bacc as bacc
    from concourse.bass_utils import run_bass_kernel_spmd

    I = {k: np.asarray(v) for k, v in inputs.items()}
    nc = bacc.Bacc("TRN2", target_bir_lowering=False, num_devices=1)
    arrays = {}

    def declare(name, a):
        arrays[name] = a
        return nc.dram_tensor(name, a.shape, F32, kind="ExternalInput").ap()

    x_in = declare("x", np.ascontiguousarray(I["x"].reshape(B, C, T)))
    small = small_tensors(I)
    columns = {k: v.shape[1] for k, v in small.items()}
    weights = declare("weights", np.concatenate(list(small.values()), 1))
    big = {k: declare("e_" + k, v) for k, v in expert_tensors(I).items()}
    out = nc.dram_tensor("out", (B, C, T), F32, kind="ExternalOutput").ap()
    metaformer(nc, x_in, columns, weights, big["to_fold"], big["rest0"], big["rec1"], out)
    r = run_bass_kernel_spmd(nc, [arrays], core_ids=[0])
    return r.results[0]["out"].reshape(I["x"].shape)
```

```python
from contextlib import ExitStack

import numpy as np
import concourse.bass as bass
from concourse import mybir

F32 = mybir.dt.float32
BF16 = mybir.dt.bfloat16
ALU = mybir.AluOpType
ACT = mybir.ActivationFunctionType
AX = mybir.AxisListType

C = 128
B = 8
T = 1024
HALF = 512
HEADS = 8
CH = C // HEADS
VH = 2 * CH
TC = T // C
QK_SCALE = 0.5
Q_PARTS = (0, 0, 0, 1, 1, 2)
K_PARTS = (0, 1, 2, 0, 1, 0)
KB = len(Q_PARTS) * CH
KM = KB + 3


LN_EXP_TABLES = 6


def load_tables(nc, act, tables):
    act.add_instruction(mybir.InstLoadActFuncSet(name=nc.get_next_instruction_name(), ins=[], outs=[],
                                                 engine=mybir.EngineType.Activation, act_func_set_id=tables))


def split_in_three(eng, value, rest, parts, done, b, held=None):
    if held is not None:
        eng.sem_inc(held, 1)
    eng.tensor_copy(parts[:, 0], value).then_inc(done, 1)
    eng.wait_ge(done, b * 4 + 1)
    eng.tensor_tensor(rest, value, parts[:, 0], ALU.subtract).then_inc(done, 1)
    eng.wait_ge(done, b * 4 + 2)
    if held is not None:
        eng.sem_inc(held, 1)
    eng.tensor_copy(parts[:, 1], rest).then_inc(done, 1)
    eng.wait_ge(done, b * 4 + 3)
    eng.tensor_tensor(parts[:, 2], rest, parts[:, 1], ALU.subtract).then_inc(done, 1)


def normalize_and_project(nc, sb, sem, bank, w, X, XF, parts_dram, v_dram):
    xc = sb("xc", [C, T], F32)
    sq = sb("sq", [C, T], F32)
    rstd = sb("rstd", [C, T], F32)
    normed = sb("normed", [C, 2, T], F32)
    qk = sb("qk", [C, 2, T], F32)
    rest = sb("rest", [C, 2, T], F32)
    parts = sb("parts", [C, 2, 2, 3, T], BF16)
    vt = sb("vt", [C, 2, TC * HEADS * VH], F32)
    bqk = sb("bqk", [C, 2], F32)
    bn = sb("bn", [C, 2, 6], F32)
    mv = sb("mv", [C, 3], F32)
    gmean = sb("gmean", [C, 1], F32)
    gvar = sb("gvar", [C, 1], F32)
    gmean2 = sb("gmean2", [C, 1], F32)
    glog = sb("glog", [C, 1], F32)
    grs = sb("grs", [C, 1], F32)
    ga = sb("ga", [C, 1], F32)
    gma = sb("gma", [C, 1], F32)
    gb = sb("gb", [C, 1], F32)
    bias_scaled = sem("bias_scaled")
    centred, xc_copied, squared, var_ready = sem("centred"), sem("xc_copied"), sem("squared"), sem("var_ready")
    ln_logged, rstd_ready, xf_ready = sem("ln_logged"), sem("rstd_ready"), sem("xf_ready")
    stats_part, stats_ready, group_ready = sem("stats_part"), sem("stats_ready"), sem("group_ready")
    gmean_ready, gvar_ready, g_logged, grs_ready = sem("gmean_ready"), sem("gvar_ready"), sem("g_logged"), sem("grs_ready")
    gab_ready, normed_ready, qk_ready, qk_biased = sem("gab_ready"), sem("normed_ready"), sem("qk_ready"), sem("qk_biased")
    first_parts, second_parts = sem("first_parts"), sem("second_parts")
    q_rest, k_rest, q_split, k_split = sem("q_rest"), sem("k_rest"), sem("q_split"), sem("k_split")
    v_ready, v_copied, stats_held = sem("v_ready"), sem("v_copied"), sem("stats_held")
    parts_stored, v_stored = sem("parts_stored"), sem("v_stored")

    def half(n):
        return slice(n * HALF, (n + 1) * HALF)

    def over_images(eng, step):
        step(None, None, 0, 0)
        with eng.Fori(0, B // 2 - 1) as i:
            step(2 * i, 0, 2 * i + 1, 1)
            step(2 * i + 1, 1, 2 * i + 2, 0)
        step(B - 2, 0, B - 1, 1)
        step(B - 1, 1, None, None)

    with nc.Block() as block:
        @block.sync
        def _(sp):
            def store(b, p):
                sp.wait_ge(v_copied, b * 4 + 4)
                sp.dma_start(v_dram[bass.ds(b, 1)].rearrange("o c n -> c (o n)"), vt[:, p]).then_inc(v_stored, 16)
                sp.wait_ge(q_split, b + 1)
                sp.dma_start(parts_dram[bass.ds(b, 1), 0].rearrange("o w c t -> c (o w) t"), parts[:, p, 0]).then_inc(parts_stored, 16)
                sp.wait_ge(k_split, b + 1)
                sp.dma_start(parts_dram[bass.ds(b, 1), 1].rearrange("o w c t -> c (o w) t"), parts[:, p, 1]).then_inc(parts_stored, 16)

            with sp.Fori(0, B // 2) as i:
                store(2 * i, 0)
                store(2 * i + 1, 1)
            sp.wait_ge(v_stored, 16 * B)
            sp.wait_ge(parts_stored, 32 * B)

        @block.tensor
        def _(pe):
            for b in range(B):
                pe.wait_ge(w.x_loaded[b], 16)

            def step(b, p, nb, np_):
                if nb is not None:
                    pe.wait_ge(xc_copied, nb * 2)
                    for n in range(2):
                        pe.matmul(bank[:, n, :], w["centre"], X[:, bass.ds(nb * T + n * HALF, HALF)],
                                  start=True, stop=True).then_inc(centred, 1)
                if b is not None:
                    pe.wait_ge(v_copied, b * 4)
                    pe.wait_ge(normed_ready, b + 1)
                for s in range(2):
                    if s == 1 and nb is not None:
                        pe.wait_ge(gvar_ready, nb)
                        for n in range(2):
                            pe.wait_ge(squared, nb * 2 + n + 1)
                            pe.matmul(bank[:, 2 + n, :], w["mean"], sq[:, half(n)], start=True, stop=True).then_inc(var_ready, 1)
                    for n in range(2) if b is not None else ():
                        pe.matmul(bank[:, 4 + 2 * s + n, :], w["wqk"][:, s * C:(s + 1) * C],
                                  normed[:, p, half(n)], start=True, stop=True).then_inc(qk_ready, 1)
                for v in range(4) if b is not None else ():
                    pe.wait_ge(qk_biased, b * 4 + v + 1)
                    for u in range(2):
                        c = 2 * v + u
                        ins = pe.matmul(bank[:, 4 + v, 256 * u:256 * u + 256], normed[:, p, c * C:(c + 1) * C],
                                        w["wv"], start=True, stop=True)
                    ins.then_inc(v_ready, 1)
                if nb is not None:
                    pe.wait_ge(stats_ready, nb + 1)
                    pe.matmul(bank[:, 2, 0:3], w["group"], mv[:], start=True, stop=True).then_inc(group_ready, 1)

            over_images(pe, step)

        @block.scalar
        def _(act):
            act.activation(bqk[:], w["bqk"], ACT.Copy, scale=QK_SCALE).then_inc(bias_scaled, 1)
            act.wait_ge(bias_scaled, 1)

            def project(b, s):
                if s == 0:
                    act.wait_ge(q_rest, b)
                    act.wait_ge(k_rest, b)
                for n in range(2):
                    act.wait_ge(qk_ready, b * 4 + 2 * s + n + 1)
                    act.activation(qk[:, s, half(n)], bank[:, 4 + 2 * s + n, :], ACT.Identity,
                                   bias=bqk[:, s:s + 1], scale=QK_SCALE).then_inc(qk_biased, 1)

            def step(b, p, nb, np_):
                if nb is not None:
                    act.wait_ge(var_ready, nb * 2)
                    for n in range(2):
                        act.wait_ge(xc_copied, nb * 2 + n + 1)
                        act.activation(sq[:, half(n)], xc[:, half(n)], ACT.Square).then_inc(squared, 1)
                if b is not None:
                    project(b, 0)
                if nb is not None:
                    act.wait_ge(xf_ready, nb * 2)
                    for n in range(2):
                        act.wait_ge(var_ready, nb * 2 + n + 1)
                        act.activation(rstd[:, half(n)], bank[:, 2 + n, :], ACT.Ln, bias=w["eps"][:, 0:1]).then_inc(ln_logged, 1)
                    for n in range(2):
                        act.wait_ge(ln_logged, nb * 2 + n + 1)
                        act.activation(rstd[:, half(n)], rstd[:, half(n)], ACT.Exp, scale=-0.5).then_inc(rstd_ready, 1)
                if b is not None:
                    project(b, 1)
                    for s in range(2):
                        act.wait_ge(parts_stored, (b - p) * 32)
                        act.wait_ge(qk_biased, b * 4 + 2 * s + 2)
                        act.activation(parts[:, p, s, 0], qk[:, s], ACT.Copy).then_inc(first_parts, 1)
                if nb is not None:
                    act.wait_ge(gvar_ready, nb + 1)
                    act.activation(glog[:], gvar[:], ACT.Ln, bias=w["eps"][:, 1:2]).then_inc(g_logged, 1)
                    act.wait_ge(g_logged, nb + 1)
                    act.activation(grs[:], glog[:], ACT.Exp, scale=-0.5).then_inc(grs_ready, 1)
                if b is not None:
                    for s, rest_ready in enumerate((q_rest, k_rest)):
                        act.wait_ge(rest_ready, b + 1)
                        act.activation(parts[:, p, s, 1], rest[:, s], ACT.Copy).then_inc(second_parts, 1)

            over_images(act, step)

        def split_rest(eng, s, b, p, rest_ready):
            eng.wait_ge(q_split if s == 0 else k_split, b)
            eng.wait_ge(first_parts, b * 2 + s + 1)
            eng.tensor_tensor(rest[:, s], qk[:, s], parts[:, p, s, 0], ALU.subtract).then_inc(rest_ready, 1)

        def split_last(eng, s, b, p, split):
            eng.wait_ge(second_parts, b * 2 + s + 1)
            eng.tensor_tensor(parts[:, p, s, 2], rest[:, s], parts[:, p, s, 1], ALU.subtract).then_inc(split, 1)

        @block.vector
        def _(dve):
            def copy_v(b, p, v):
                dve.wait_ge(v_ready, b * 4 + v + 1)
                dve.tensor_tensor(vt[:, p, half(v)], bank[:, 4 + v, :], w["bv"], ALU.add).then_inc(v_copied, 1)

            def step(b, p, nb, np_):
                if nb is not None:
                    for n in range(2):
                        dve.wait_ge(centred, nb * 2 + n + 1)
                        dve.tensor_copy(xc[:, half(n)], bank[:, n, :]).then_inc(xc_copied, 1)
                    for n in range(2):
                        dve.wait_ge(xc_copied, nb * 2 + n + 1)
                        dve.wait_ge(rstd_ready, nb * 2 + n + 1)
                        dve.tensor_tensor(XF[:, bass.ds(nb * T + n * HALF, HALF)], xc[:, half(n)], rstd[:, half(n)],
                                          ALU.mult).then_inc(xf_ready, 1)
                    for n in range(2):
                        dve.wait_ge(xf_ready, nb * 2 + n + 1)
                        dve.sem_inc(stats_held, 1)
                        dve.bn_stats(bn[:, n, :], XF[:, bass.ds(nb * T + n * HALF, HALF)]).then_inc(stats_part, 1)
                    dve.wait_ge(stats_part, nb * 3 + 2)
                    dve.sem_inc(stats_held, 1)
                    dve.bn_aggr(mv[:, 0:2], bn[:]).then_inc(stats_part, 1)
                    dve.wait_ge(stats_part, nb * 3 + 3)
                    dve.scalar_tensor_tensor(out=mv[:, 2:3], in0=mv[:, 0:1], scalar=mv[:, 0:1], in1=mv[:, 1:2],
                                             op0=ALU.mult, op1=ALU.add).then_inc(stats_ready, 1)
                if b is not None:
                    dve.wait_ge(v_stored, (b - p) * 16)
                    copy_v(b, p, 0)
                    copy_v(b, p, 1)
                if nb is not None:
                    dve.wait_ge(group_ready, nb + 1)
                    dve.tensor_copy(gmean[:], bank[:, 2, 0:1]).then_inc(gmean_ready, 1)
                    dve.wait_ge(gmean_ready, nb * 2 + 1)
                    dve.tensor_tensor(gmean2[:], gmean[:], gmean[:], ALU.mult).then_inc(gmean_ready, 1)
                    dve.wait_ge(gmean_ready, nb * 2 + 2)
                    dve.tensor_tensor(gvar[:], bank[:, 2, 2:3], gmean2[:], ALU.subtract).then_inc(gvar_ready, 1)
                if b is not None:
                    copy_v(b, p, 2)
                    copy_v(b, p, 3)
                    split_rest(dve, 0, b, p, q_rest)
                if nb is not None:
                    dve.wait_ge(grs_ready, nb + 1)
                    dve.tensor_tensor(ga[:], grs[:], w["gn"][:, 0:1], ALU.mult).then_inc(gab_ready, 1)
                    dve.wait_ge(gab_ready, nb * 3 + 1)
                    dve.tensor_tensor(gma[:], gmean[:], ga[:], ALU.mult).then_inc(gab_ready, 1)
                    dve.wait_ge(gab_ready, nb * 3 + 2)
                    dve.tensor_tensor(gb[:], w["gn"][:, 1:2], gma[:], ALU.subtract).then_inc(gab_ready, 1)
                    dve.wait_ge(gab_ready, nb * 3 + 3)
                    if b is not None:
                        dve.wait_ge(v_ready, b * 4)
                    dve.tensor_scalar(normed[:, np_], XF[:, bass.ds(nb * T, T)], ga[:, 0:1], gb[:, 0:1],
                                      ALU.mult, ALU.add).then_inc(normed_ready, 1)
                if b is not None:
                    split_last(dve, 0, b, p, q_split)

            over_images(dve, step)

        @block.gpsimd
        def _(pool):
            def step(b, p, nb, np_):
                if b is not None:
                    split_rest(pool, 1, b, p, k_rest)
                    split_last(pool, 1, b, p, k_split)

            over_images(pool, step)


STEPS = 32
SLOTS = 4
FIRST, OWN = 129, 130


def units_of(prev, more):
    units = [("max", k) for k in range(2 * HEADS * TC)] if more else []
    units.insert(3, ("rows", 1))
    if more:
        units.insert(68, ("rows", 0))
    if prev:
        at = 30 if more else 1
        units[at:at] = [("proj", 0), ("proj", 1)]
    return units


FIRST_UNITS = [unit for unit in units_of(False, True) if unit != ("rows", 1)]


def units_before(b):
    return (OWN + 2) * b + FIRST + OWN - (OWN + 2)


def attention(nc, sb, sem, bank, w, X, XF, parts_dram, v_dram):
    qs = sb("qs", [KM, 2, HEADS, T], BF16)
    ks = sb("ks", [KM, 2, HEADS, T], BF16)
    vt = sb("vt", [C, 2, TC, HEADS * VH], F32)
    P = sb("P", [C, SLOTS, 2 * HALF], F32)
    mx = sb("mx", [C, 64, 2], F32)
    nm = sb("nm", [C, 64], F32)
    nmT = sb("nmT", [32, C], F32)
    nm_rest = sb("nm_rest", [32, C], F32)
    nm_parts = sb("nm_parts", [32, 3, C], BF16)
    o = sb("o", [C, HALF], F32)
    den = sb("den", [C, HALF], F32)
    rden = sb("rden", [C, HALF], F32)
    a = sb("a", [C, 2, T], F32)
    ones_set, rows_loaded, v_loaded = sem("ones_set"), sem("rows_loaded"), sem("v_loaded")
    qk_loaded = [sem("qk0_loaded"), sem("qk1_loaded")]
    unit_filled, unit_freed, negated, rows_split = sem("unit_filled"), sem("unit_freed"), sem("negated"), sem("rows_split")
    scores_ready, probs_ready, pv_done = sem("scores_ready"), sem("probs_ready"), sem("pv_done")
    o_copied, den_ready, den_logged, rden_ready, a_ready = (
        sem("o_copied"), sem("den_ready"), sem("den_logged"), sem("rden_ready"), sem("a_ready"))
    held, split_held = sem("held"), sem("split_held")
    LOADS = 16 * (len(Q_PARTS) + len(K_PARTS))

    def over_images(eng, first, body, last):
        first()
        body(0, None, 0, FIRST, False, True)
        with eng.Fori(0, B // 2 - 1) as i:
            body(2 * i + 1, 2 * i, 1, units_before(2 * i + 1), True, True)
            body(2 * i + 2, 2 * i + 1, 0, units_before(2 * i + 2), True, True)
        body(B - 1, B - 2, 1, units_before(B - 1), True, False)
        last()

    LAST = units_before(B - 1) + len(units_of(True, False))

    def units_at(e, units):
        if len(units) < STEPS:
            return [(index, unit) for index, unit in enumerate(units) if e == (0 if unit[0] == "rows" else 6)]
        return list(enumerate(units))[e * len(units) // STEPS:(e + 1) * len(units) // STEPS]

    with nc.Block() as block:
        @block.sync
        def _(sp):
            def load_qk(b, par, g):
                for r, (qp, kp) in enumerate(zip(Q_PARTS, K_PARTS)):
                    for s, part, stack in ((0, qp, qs), (1, kp, ks)):
                        src = parts_dram[bass.ds(b, 1), s, part, g * C // 2:(g + 1) * C // 2].rearrange("o (h i) t -> i (o h) t", i=CH)
                        sp.dma_start(stack[r * CH:(r + 1) * CH, par, 4 * g:4 * g + 4], src).then_inc(qk_loaded[g], 16)

            def load_v(b, par):
                sp.dma_start(vt[:, par].rearrange("c s n -> c (s n)"),
                             v_dram[bass.ds(b, 1)].rearrange("o c n -> c (o n)")).then_inc(v_loaded, 16)

            def max_rows(b, par, g):
                sp.wait_ge(rows_split, b * 8 + 4 * g + 4)
                for part in range(3):
                    sp.dma_start(qs[KB + part:KB + part + 1, par, 4 * g:4 * g + 4, :]
                                 .rearrange("p h (c t) -> p (h c) t", t=C),
                                 nm_parts[:, part, :]).then_inc(rows_loaded, 16)

            def first():
                load_qk(0, 0, 0)
                load_qk(0, 0, 1)
                load_v(0, 0)
                max_rows(0, 0, 0)
                load_qk(1, 1, 0)

            def body(b, par, prev, more, ahead):
                if more:
                    if prev:
                        sp.wait_ge(pv_done, b * STEPS)
                    load_qk(b + 1, 1 - par, 1)
                    load_v(b + 1, 1 - par)
                max_rows(b, par, 1)
                if ahead:
                    sp.wait_ge(pv_done, b * STEPS + STEPS // 2)
                    load_qk(b + 2, par, 0)
                if more:
                    max_rows(b + 1, 1 - par, 0)

            first()
            body(0, 0, False, True, True)
            with sp.Fori(0, B // 2 - 2) as i:
                body(2 * i + 1, 1, True, True, True)
                body(2 * i + 2, 0, True, True, True)
            body(B - 3, 1, True, True, True)
            body(B - 2, 0, True, True, False)
            body(B - 1, 1, True, False, False)
            sp.wait_ge(rows_loaded, B * 96)

        @block.tensor
        def _(pe):
            def rows(b, g, slot):
                pe.wait_ge(negated, b * 2 + g + 1)
                pe.transpose(bank[0:32, slot, 0:C], nm[:, 32 * g:32 * g + 32], w["ident"]).then_inc(unit_filled, 1)

            def take_max(b, par, k, slot):
                h, c, half = k // 16, k // 2 % TC, k % 2
                if k % 64 == 0:
                    pe.wait_ge(qk_loaded[k // 64], (b + 1) * LOADS)
                pe.matmul(bank[:, slot, :], qs[0:KB, par, h, c * C:(c + 1) * C],
                          ks[0:KB, par, h, half * HALF:(half + 1) * HALF], start=True, stop=True).then_inc(unit_filled, 1)

            def project(b, n, slot):
                if n == 0:
                    pe.wait_ge(a_ready, b * 4 + 4)
                pe.matmul(bank[:, slot, :], w["wproj"], XF[:, bass.ds(b * T + n * HALF, HALF)], start=True, stop=False)
                for g in range(2):
                    ins = pe.matmul(bank[:, slot, :], w["wproj_heads"][:, g * C:(g + 1) * C],
                                    a[:, g, n * HALF:(n + 1) * HALF], start=False, stop=(g == 1))
                ins.then_inc(unit_filled, 1)

            def first():
                for index, (kind, k) in enumerate(FIRST_UNITS):
                    if index >= 3:
                        pe.wait_ge(unit_freed, index - 2)
                    if kind == "max":
                        take_max(0, 0, k, 5 + index % 3)
                    else:
                        rows(0, 0, 5 + index % 3)

            def weigh(b, par, e):
                g, n, s = e // 16, e // 8 % 2, e % 8
                pe.wait_ge(probs_ready, b * 2 * STEPS + 2 * e + 2)
                if e == 0:
                    pe.wait_ge(v_loaded, (b + 1) * 16)
                if s == 0:
                    pe.wait_ge(o_copied, b * 4 + 2 * g + n)
                for j in range(4):
                    head = 4 * g + j
                    ins = pe.matmul(bank[32 * j:32 * j + 32, 4, :], vt[:, par, s, head * VH:(head + 1) * VH],
                                    P[:, (2 * e + j // 2) % SLOTS, j % 2 * HALF:(j % 2 + 1) * HALF],
                                    start=(s == 0), stop=(s == 7))
                ins.then_inc(pv_done, 1)

            def body(b, before, par, base, prev, more):
                units = units_of(prev, more)
                for e in range(STEPS):
                    g, n, s = e // 16, e // 8 % 2, e % 8
                    now = units_at(e, units)
                    for pair in range(2):
                        x = 2 * e + pair
                        if e == 0 and pair == 0 and not prev:
                            pe.wait_ge(ones_set, 1)
                        if e % 16 == 0 and pair == 0:
                            pe.wait_ge(rows_loaded, b * 96 + 48 * g + 48)
                        pe.wait_ge(probs_ready, b * 2 * STEPS + (x - 1 if prev else max(x - 1, 0)))
                        for u in range(2):
                            head = 4 * g + 2 * pair + u
                            ins = pe.matmul(bank[:, 2 * pair + u, :], ks[:, par, head, s * C:(s + 1) * C],
                                            qs[:, par, head, n * HALF:(n + 1) * HALF], start=True, stop=True)
                        ins.then_inc(scores_ready, 1)
                        for index, (kind, k) in now[:2] if pair == 0 else now[2:]:
                            slot = 5 + index % 3
                            pe.wait_ge(unit_freed, base + max(index - 2, 0))
                            if kind == "max":
                                take_max(b + 1, 1 - par, k, slot)
                            elif kind == "rows":
                                rows(b if k else b + 1, k, slot)
                            else:
                                project(before, k, slot)
                    if e:
                        weigh(b, par, e - 1)
                    elif prev:
                        weigh(before, 1 - par, STEPS - 1)

            def last():
                weigh(B - 1, (B - 1) % 2, STEPS - 1)
                pe.wait_ge(unit_freed, LAST)
                for n in range(2):
                    project(B - 1, n, 5 + n)

            over_images(pe, first, body, last)

        @block.scalar
        def _(act):
            def numerators(b, q):
                act.wait_ge(pv_done, b * STEPS + 8 * q + 8)
                act.wait_ge(a_ready, b * 4 + q)
                act.activation(o[:], bank[:, 4, :], ACT.Copy).then_inc(o_copied, 1)

            def reciprocal(b, q):
                act.wait_ge(den_ready, b * 4 + q + 1)
                act.wait_ge(a_ready, b * 4 + q)
                act.activation(rden[:], den[:], ACT.Ln).then_inc(den_logged, 1)
                act.wait_ge(den_logged, b * 4 + q + 1)
                act.activation(rden[:], rden[:], ACT.Exp, scale=-1.0).then_inc(rden_ready, 1)

            def body(b, before, par, base, prev, more):
                for e in range(STEPS):
                    image, q = (b, e // 8 - 1) if e >= 8 else (before, 3)
                    act.wait_ge(pv_done, b * STEPS + (e - 1 if prev else max(e - 1, 0)))
                    if e % 8 == 1 and (prev or e >= 8):
                        numerators(image, q)
                    for pair in range(2):
                        x = 2 * e + pair
                        act.wait_ge(scores_ready, b * 2 * STEPS + x + 1)
                        act.activation(P[:, x % SLOTS, :], bank[:, 2 * pair:2 * pair + 2, :]
                                       .rearrange("p a t -> p (a t)"), ACT.Exp).then_inc(probs_ready, 1)
                    if e % 8 == 2 and (prev or e >= 8):
                        reciprocal(image, q)

            def last():
                numerators(B - 1, 3)
                reciprocal(B - 1, 3)

            over_images(act, lambda: None, body, last)

        @block.vector
        def _(dve):
            def reduce(k, slot, filled):
                dve.wait_ge(unit_filled, filled)
                dve.tensor_reduce(mx[:, k // 2, k % 2:k % 2 + 1], bank[:, slot, :], AX.X, ALU.max).then_inc(unit_freed, 1)
                if k % 64 == 63:
                    g = k // 64
                    dve.wait_ge(unit_freed, filled)
                    dve.tensor_reduce(nm[:, 32 * g:32 * g + 32], mx[:, 32 * g:32 * g + 32, :], AX.X, ALU.max,
                                      negate=True).then_inc(negated, 1)

            def rows(b, g, slot, filled):
                dve.wait_ge(unit_filled, filled)
                dve.wait_ge(rows_split, b * 8 + 4 * g)
                dve.tensor_copy(nmT[:], bank[0:32, slot, 0:C]).then_inc(unit_freed, 1)

            def add(b, n, slot, filled):
                cols = X[:, bass.ds(b * T + n * HALF, HALF)]
                dve.wait_ge(unit_filled, filled)
                dve.scalar_tensor_tensor(out=cols, in0=bank[:, slot, :], scalar=w["bproj"], in1=cols,
                                         op0=ALU.add, op1=ALU.add).then_inc(unit_freed, 1)

            def sums(b, q):
                dve.wait_ge(o_copied, b * 4 + q + 1)
                dve.wait_ge(den_logged, b * 4 + q)
                dve.sem_inc(held, 1)
                dve.stream_shuffle(den[:], o[:], [CH + i % CH for i in range(32)]).then_inc(den_ready, 1)

            def first():
                for unit, (kind, k) in enumerate(FIRST_UNITS):
                    if kind == "max":
                        reduce(k, 5 + unit % 3, unit + 1)
                    else:
                        rows(0, 0, 5 + unit % 3, unit + 1)

            def body(b, before, par, base, prev, more):
                units = units_of(prev, more)
                for e in range(STEPS):
                    for index, (kind, k) in units_at(e, units):
                        slot, filled = 5 + index % 3, base + index + 1
                        if kind == "max":
                            reduce(k, slot, filled)
                        elif kind == "rows":
                            rows(b if k else b + 1, k, slot, filled)
                        else:
                            add(before, k, slot, filled)
                    if e % 8 == 1 and (prev or e >= 8):
                        sums(*((b, e // 8 - 1) if e >= 8 else (before, 3)))

            def last():
                sums(B - 1, 3)
                for n in range(2):
                    add(B - 1, n, 5 + n, LAST + n + 1)
                dve.wait_ge(unit_freed, LAST + 2)

            over_images(dve, first, body, last)

        @block.gpsimd
        def _(pool):
            def split_rows(b, g, freed):
                pool.wait_ge(unit_freed, freed)
                pool.wait_ge(rows_loaded, b * 96 + 48 * g)
                split_in_three(pool, nmT[:], nm_rest[:], nm_parts[:], rows_split, b * 2 + g, split_held)

            def divide(b, q, used=None):
                pool.wait_ge(rden_ready, b * 4 + q + 1)
                if used is not None:
                    pool.wait_ge(unit_filled, used)
                g, n = q // 2, q % 2
                pool.tensor_tensor(a[:, g, n * HALF:(n + 1) * HALF], o[:], rden[:], ALU.mult).then_inc(a_ready, 1)

            def first():
                pool.memset(ks[KB:KM, :, :, :], 1.0).then_inc(ones_set, 1)
                split_rows(0, 0, FIRST_UNITS.index(("rows", 0)) + 1)

            def body(b, before, par, base, prev, more):
                units = units_of(prev, more)
                split_rows(b, 1, base + units.index(("rows", 1)) + 1)
                if prev:
                    divide(before, 3)
                divide(b, 0, base + units.index(("proj", 1)) + 1 if prev else None)
                if more:
                    row_unit = units.index(("rows", 0))
                    divide(b, 1)
                    split_rows(b + 1, 0, base + row_unit + 1)
                else:
                    divide(b, 1)
                divide(b, 2)

            over_images(pool, first, body, lambda: divide(B - 1, 3))


class Weights:

    def __init__(self, nc, sb, sem, columns):
        self.loaded, self.x_loaded = sem("weights_loaded"), [sem(f"x{b}_loaded") for b in range(B)]
        self.all = sb("weights", [C, sum(columns.values())], F32)
        self.at, first = {}, 0
        for name, n in columns.items():
            self.at[name] = (first, first + n)
            first += n
        ones, before = sb("ones", [C, C], BF16), sb("before", [C, C], BF16)
        self.ones, self.before = ones[:], before[:]
        self.cast = sem("constants_cast")

    def __getitem__(self, name):
        first, end = self.at[name]
        return self.all[:, first:end]


E = 8
TOKENS = B * T
TILE = 512
Q = TILE // C
ROW = C + 2
G = T // C
REGION = TOKENS // TILE + 1
TILES = 40
RING = 8
IDLE = TILES - 2 * TOKENS // TILE
UNITS_XD = E * REGION + IDLE
BLANKS = E + IDLE
SPARE = 2 * TOKENS


def route(nc, sb, sem, bank, w, X, layer, xd_dram, table):
    second = layer == 1
    k = f"moe{layer}_"
    xc = sb("xc", [C, 2, TILE], F32)
    sq = sb("sq", [C, 2, TILE], F32)
    rs = sb("rs", [C, 2, TILE], F32)
    rs2 = sb("rs2", [C, 2, TILE], F32)
    xl = sb("xl", [C, 2, TILE], F32)
    xn = sb("xn", [C, 2, TILE], F32)
    rows = sb("rows", [C, 2, G, 2, ROW], F32)
    places = sb("places", [C, 2, G, 2], mybir.dt.uint32)
    small = {n: sb(n, [C, G, E], F32) for n in
             ("logits", "shifted", "e", "p", "eq", "key", "best", "p2", "eq2", "key2", "second", "slot", "at")}
    per = {n: sb(n, [C, G], F32) for n in ("lmax", "esum", "rsum", "g1", "k1", "g2", "k2")}
    per["place"] = sb("place", [C, G, 2], F32)
    ids = sb("ids", [C, G, 2], F32)
    count = sb("count", [C, E], F32)
    blank = sb("blank", [C, BLANKS, Q * ROW], F32)
    mask = sb("mask", [C, G, E], BF16)
    base = sb("base", [C, E], F32)
    count16 = sb("count16", [C, E, 16], F32)
    tiles = sb("tiles", [C, E], F32)
    ends = sb("ends", [C, E], F32)
    pad = sb("pad", [C, E], F32)
    passed = sb("passed", [C, TILES, E], F32)
    skip = sb("skip", [C, TILES, E], F32)
    ex = sb("ex", [C, TILES], F32)
    un = sb("un", [C, TILES], F32)
    base_i = sb("base_i", [C, E], mybir.dt.int32)
    centred, copied, squared, var_ready = sem("centred"), sem("copied"), sem("squared"), sem("var_ready")
    logged, rstd_ready, xn_ready, router_ready = sem("logged"), sem("rstd_ready"), sem("xn_ready"), sem("router_ready")
    turned, rows_ready, exp_ready, mask_ready = sem("turned"), sem("rows_ready"), sem("exp_ready"), sem("mask_ready")
    ranked, step_done, gates_ready = sem("ranked"), sem("step_done"), sem("gates_ready")
    sent = [sem("sent0"), sem("sent1")]
    planned, blanks_sent, base_set, blank_ready = sem("planned"), sem("blanks_sent"), sem("base_set"), sem("blank_ready")
    held, normed_once, logits_ready = sem("held"), sem("normed_once"), sem("logits_ready")
    CHAIN = 22
    GROUPS = TOKENS // T
    SENDS = 16 * 2 * G

    def over_groups(eng, step):
        step(None, None, 0, 0)
        with eng.Fori(0, GROUPS // 2 - 1) as i:
            step(2 * i, 0, 2 * i + 1, 1)
            step(2 * i + 1, 1, 2 * i + 2, 0)
        step(GROUPS - 2, 0, GROUPS - 1, 1)
        step(GROUPS - 1, 1, None, None)

    with nc.Block() as block:
        @block.tensor
        def _(pe):
            def step(g, p, ng, np_):
                if ng is not None:
                    pe.wait_ge(copied, 2 * ng)
                    for n in range(2):
                        pe.matmul(bank[:, n, :], w["centre"], X[:, bass.ds(ng * T + n * TILE, TILE)],
                                  start=True, stop=True).then_inc(centred, 1)
                    for n in range(2):
                        pe.wait_ge(squared, 2 * ng + n + 1)
                        pe.matmul(bank[:, 2 + n, :], w["mean"], sq[:, n, :], start=True, stop=True).then_inc(var_ready, 1)
                if g is not None:
                    pe.wait_ge(mask_ready, g + 1)
                    for q in range(G + 1):
                        out = bank[:, 7, q * E:(q + 1) * E]
                        for q2 in range(q):
                            ins = pe.matmul(out, w.ones, mask[:, q2, :], start=(q2 == 0), stop=(q == G and q2 == q - 1))
                        if q < G:
                            ins = pe.matmul(out, w.before, mask[:, q, :], start=(q == 0), stop=True)
                    ins.then_inc(ranked, 1)
                if ng is not None:
                    pe.wait_ge(logits_ready, ng)
                    for n in range(2):
                        pe.wait_ge(xn_ready, 2 * ng + n + 1)
                        for q in range(Q):
                            ins = pe.matmul(bank[:, 6, (n * Q + q) * E:(n * Q + q + 1) * E], xn[:, n, q * C:(q + 1) * C],
                                            w[k + "router"], start=True, stop=True)
                    ins.then_inc(router_ready, 1)
                    for n in range(2):
                        pe.wait_ge(rows_ready, 2 * ng)
                        for q in range(Q):
                            ins = pe.transpose(bank[:, 4 + n, q * C:(q + 1) * C], xn[:, n, q * C:(q + 1) * C], w["ident"])
                        ins.then_inc(turned, 1)

            over_groups(pe, step)

        @block.scalar
        def _(act):
            load_tables(nc, act, LN_EXP_TABLES)

            def step(g, p, ng, np_):
                if ng is not None:
                    for n in range(2):
                        act.wait_ge(copied, 2 * ng + n + 1)
                        act.wait_ge(var_ready, 2 * ng)
                        act.activation(sq[:, n, :], xc[:, n, :], ACT.Square).then_inc(squared, 1)
                if g is not None:
                    act.wait_ge(step_done, g * CHAIN + 2)
                    act.activation(small["e"][:], small["shifted"][:], ACT.Exp).then_inc(exp_ready, 1)
                if ng is not None:
                    m = 2 if second else 1
                    for n in range(2):
                        act.wait_ge(var_ready, 2 * ng + n + 1)
                        act.wait_ge(xn_ready, 2 * ng)
                        act.activation(rs[:, n, :], bank[:, 2 + n, :], ACT.Ln, bias=w["eps"][:, 1:2]).then_inc(logged, 1)
                        if second:
                            act.activation(rs2[:, n, :], bank[:, 2 + n, :], ACT.Ln, bias=w["eps"][:, 2:3],
                                           scale=1.0 + 1e-5).then_inc(logged, 1)
                    for n in range(2):
                        act.wait_ge(logged, (2 * ng + n + 1) * m)
                        act.activation(rs[:, n, :], rs[:, n, :], ACT.Exp, scale=-0.5).then_inc(rstd_ready, 1)
                        if second:
                            act.activation(rs2[:, n, :], rs2[:, n, :], ACT.Exp, scale=-0.5).then_inc(rstd_ready, 1)
                    act.wait_ge(sent[np_], (ng - np_) * (SENDS // 2))
                    for n in range(2):
                        act.wait_ge(turned, 2 * ng + n + 1)
                        act.activation(rows[:, np_, n * Q:(n + 1) * Q, :, 0:C],
                                       bank[:, 4 + n, :].rearrange("t (q c) -> t q c", q=Q)
                                       .unsqueeze(2).to_broadcast([C, Q, 2, C]), ACT.Copy).then_inc(rows_ready, 1)

            over_groups(act, step)

        @block.vector
        def _(dve):
            dve.tensor_copy(base[:], w["region"])
            dve.tensor_copy(ids[:].rearrange("t q c -> t (q c)"), w["row_ids"]).then_inc(base_set, 1)
            dve.wait_ge(base_set, 1)
            s, v = small, per

            def wide(a):
                return a[:].unsqueeze(2).to_broadcast([C, G, E])

            def normalize(ng):
                for n in range(2):
                    t = 2 * ng + n
                    if not second:
                        dve.wait_ge(rstd_ready, t + 1)
                        dve.wait_ge(turned, 2 * ng)
                        dve.tensor_tensor(xn[:, n, :], xc[:, n, :], rs[:, n, :], ALU.mult).then_inc(xn_ready, 1)
                        continue
                    dve.wait_ge(rstd_ready, 2 * t + 2)
                    dve.wait_ge(turned, 2 * ng)
                    dve.tensor_tensor(rs2[:, n, :], xc[:, n, :], rs2[:, n, :], ALU.mult).then_inc(normed_once, 1)
                    dve.tensor_tensor(xl[:, n, :], xc[:, n, :], rs[:, n, :], ALU.mult).then_inc(normed_once, 1)
                    dve.wait_ge(normed_once, 2 * t + 1)
                    dve.tensor_scalar(xn[:, n, :], rs2[:, n, :], w["ln"][:, 0:1], w["ln"][:, 1:2],
                                      ALU.mult, ALU.add).then_inc(xn_ready, 1)
                    dve.wait_ge(normed_once, 2 * t + 2)
                    tokens = X[:, bass.ds(t * TILE, TILE)]
                    dve.tensor_tensor(tokens, tokens, xl[:, n, :], ALU.add)

            def step(g, p, ng, np_):
                done = [0]

                def then(ins):
                    ins.then_inc(step_done, 1)
                    done[0] += 1
                    dve.wait_ge(step_done, g * CHAIN + done[0])

                if g is not None:
                    then(dve.tensor_reduce(v["lmax"][:], s["logits"][:], AX.X, ALU.max))
                    then(dve.tensor_tensor(s["shifted"][:], s["logits"][:], wide(v["lmax"]), ALU.subtract))
                if ng is not None:
                    for n in range(2):
                        dve.wait_ge(centred, 2 * ng + n + 1)
                        dve.tensor_copy(xc[:, n, :], bank[:, n, :]).then_inc(copied, 1)
                if g is not None:
                    dve.wait_ge(exp_ready, g + 1)
                    then(dve.tensor_reduce(v["esum"][:], s["e"][:], AX.X, ALU.add))
                    then(dve.reciprocal(v["rsum"][:], v["esum"][:]))
                    then(dve.tensor_tensor(s["p"][:], s["e"][:], wide(v["rsum"]), ALU.mult))
                    for probs, gate, eq, key, kmax, hot in (("p", "g1", "eq", "key", "k1", "best"),
                                                            ("p2", "g2", "eq2", "key2", "k2", "second")):
                        if hot == "second":
                            then(dve.scalar_tensor_tensor(out=s["p2"][:], in0=s["best"][:], scalar=-2.0, in1=s["p"][:],
                                                          op0=ALU.mult, op1=ALU.add))
                        then(dve.tensor_reduce(v[gate][:], s[probs][:], AX.X, ALU.max))
                        then(dve.tensor_tensor(s[eq][:], s[probs][:], wide(v[gate]), ALU.is_equal))
                        then(dve.tensor_tensor(s[key][:].rearrange("t q e -> t (q e)"),
                                               s[eq][:].rearrange("t q e -> t (q e)"), w["firstness"], ALU.mult))
                        then(dve.tensor_reduce(v[kmax][:], s[key][:], AX.X, ALU.max))
                        then(dve.tensor_tensor(s[hot][:], s[key][:], wide(v[kmax]), ALU.is_equal))
                    dve.wait_ge(ranked, g)
                    dve.tensor_tensor(mask[:], s["best"][:], s["second"][:], ALU.add).then_inc(mask_ready, 1)
                    dve.wait_ge(rows_ready, 2 * g + 2)
                    dve.tensor_copy(rows[:, p, :, 0, C:C + 1], v["g1"][:].unsqueeze(2))
                    dve.tensor_copy(rows[:, p, :, 1, C:C + 1], v["g2"][:].unsqueeze(2))
                    dve.tensor_copy(rows[:, p, :, :, C + 1:C + 2], ids[:].unsqueeze(3))
                    then(dve.tensor_scalar(ids[:], ids[:], float(T), None, ALU.add))
                    dve.wait_ge(ranked, g + 1)
                    then(dve.tensor_tensor(s["slot"][:], bank[:, 7, 0:G * E].rearrange("t (q e) -> t q e", q=G),
                                           base[:].unsqueeze(1).to_broadcast([C, G, E]), ALU.add))
                    dve.tensor_tensor(base[:], base[:], bank[:, 7, G * E:(G + 1) * E], ALU.add)
                    for c, hot in enumerate(("best", "second")):
                        then(dve.tensor_tensor(s["at"][:], s["slot"][:], s[hot][:], ALU.mult))
                        then(dve.tensor_reduce(v["place"][:, :, c:c + 1], s["at"][:], AX.X, ALU.add))
                    dve.tensor_copy(places[:, p], v["place"][:]).then_inc(gates_ready, 1)
                    assert done[0] == CHAIN
                if ng is not None:
                    normalize(ng)
                    dve.wait_ge(router_ready, ng + 1)
                    dve.tensor_tensor(s["logits"][:].rearrange("t q e -> t (q e)"), bank[:, 6, 0:G * E],
                                      w[k + "router_bias"], ALU.add).then_inc(logits_ready, 1)
                    dve.wait_ge(logits_ready, ng + 1)

            over_groups(dve, step)
            done = [0]

            def plan(ins):
                ins.then_inc(planned, 1)
                done[0] += 1
                dve.wait_ge(planned, done[0])

            dve.wait_ge(gates_ready, GROUPS)
            plan(dve.tensor_copy(base_i[:], base[:]))
            plan(dve.tensor_tensor(count[:], base[:], w["region"], ALU.subtract))
            plan(dve.tensor_tensor(count16[:], count[:].unsqueeze(2).to_broadcast([C, E, 16]),
                                   w["k_tile"].rearrange("t (e k) -> t e k", e=E), ALU.is_gt))
            plan(dve.tensor_reduce(tiles[:], count16[:], AX.X, ALU.add))
            plan(dve.tensor_tensor_scan(ends[:], tiles[:], w["zeros"][:, 0:E], 0.0, ALU.add, ALU.add))
            plan(dve.tensor_scalar(pad[:], tiles[:], -1.0, float(REGION), ALU.mult, ALU.add))
            plan(dve.tensor_tensor(passed[:], ends[:].unsqueeze(1).to_broadcast([C, TILES, E]),
                                   w["tile_no"].unsqueeze(2).to_broadcast([C, TILES, E]), ALU.is_le))
            plan(dve.tensor_reduce(ex[:], passed[:], AX.X, ALU.add))
            plan(dve.tensor_tensor(skip[:], passed[:], pad[:].unsqueeze(1).to_broadcast([C, TILES, E]), ALU.mult))
            plan(dve.tensor_reduce(un[:], skip[:], AX.X, ALU.add))
            plan(dve.tensor_tensor(un[:], un[:], w["tile_no"], ALU.add))
            plan(dve.tensor_scalar(table[:, 0, :], ex[:], float(E - 1), None, ALU.min))
            plan(dve.tensor_scalar(table[:, 1, :], un[:], 1.0, None, ALU.mult))

        @block.gpsimd
        def _(pool):
            pool.memset(blank[:], 0.0).then_inc(blank_ready, 1)
            pool.wait_ge(blank_ready, 1)
            pool.tensor_copy(blank[:].rearrange("t n (q r) -> t (n q) r", q=Q)[:, :, ROW - 1:ROW],
                             w["blank_rows"].unsqueeze(2)).then_inc(blank_ready, 1)
            with pool.Fori(0, GROUPS // 2) as i:
                for p in range(2):
                    pool.wait_ge(gates_ready, 2 * i + p + 1)
                    pool.sem_inc(held, 1)
                    for q in range(G):
                        for c in range(2):
                            pool.indirect_dma_start(xd_dram, bass.IndirectOffsetOnAxis(places[:, p, q, c:c + 1], 0),
                                                    rows[:, p, q, c, :], None).then_inc(sent[p], 16)
            for p in range(2):
                pool.wait_ge(sent[p], GROUPS // 2 * SENDS)

        @block.sync
        def _(sp):
            sp.wait_ge(blank_ready, 2)
            for n in range(IDLE):
                sp.dma_start(xd_dram[(E * REGION + n) * TILE:(E * REGION + n + 1) * TILE, :]
                             .rearrange("(t q) r -> t (q r)", q=Q), blank[:, E + n]).then_inc(blanks_sent, 16)
            sp.wait_ge(planned, 1)
            for e in range(E):
                first = sp.value_load(base_i[0:1, e:e + 1], min_val=0, max_val=E * REGION * TILE)
                sp.dma_start(xd_dram[bass.ds(first, TILE), :].rearrange("(t q) r -> t (q r)", q=Q),
                             blank[:, e]).then_inc(blanks_sent, 16)
            sp.wait_ge(blanks_sent, 16 * BLANKS)


def experts(nc, sb, sem, bank, w, layer, xd_dram, yd_dram, table, records):
    second = layer == 1
    FB = 4 * C
    NH = 4 if second else 2
    W2 = FB + 4
    B2 = W2 + NH * C
    REC = B2 + C
    rec = sb("rec", [C, RING, REC], F32)
    xr = sb("xr", [C, RING, Q, ROW], F32)
    xt = sb("xt", [C, 2, TILE], F32)
    hidden = sb("hidden", [C, 2, NH, TILE], F32)
    gate = sb("gate", [C, 2, TILE], F32)
    y1 = sb("y1", [C, 2, Q, C], F32)
    yo = sb("yo", [C, 2, Q, C], F32)
    places = sb("places", [C, 2, Q], mybir.dt.uint32)
    loaded = [sem(f"loaded{r}") for r in range(RING)]
    turned, xt_copied, g_ready, v_ready, gated = sem("turned"), sem("xt_copied"), sem("g_ready"), sem("v_ready"), sem("gated")
    h_ready, y_ready, y_copied, yo_ready, fence = sem("h_ready"), sem("y_ready"), sem("y_copied"), sem("yo_ready"), sem("fence")
    sent = [sem("sent0"), sem("sent1")]
    LOADS = 16 * (len(records) + 1)

    def over_tiles(eng, turn, first, finish):
        def at(step, group, r):
            group, r = group + r // RING, r % RING
            step(RING * group + r, r, r % 2, RING // 2 * group + r // 2, group)

        at(turn, 0, 0)
        at(first, 0, 0)
        at(turn, 0, 1)
        with eng.Fori(0, TILES // RING - 1) as group:
            for r in range(RING):
                at(first, group, r + 1)
                at(turn, group, r + 2)
                at(finish, group, r)
        last = TILES // RING - 1
        for r in range(RING):
            if r + 1 < RING:
                at(first, last, r + 1)
            if r + 2 < RING:
                at(turn, last, r + 2)
            at(finish, last, r)

    def nothing(*_):
        pass

    with nc.Block() as block:
        @block.sync
        def _(sp):
            def load(j, r):
                e = sp.value_load(table[0:1, 0, bass.ds(j, 1)], min_val=0, max_val=E - 1)
                u = sp.value_load(table[0:1, 1, bass.ds(j, 1)], min_val=0, max_val=UNITS_XD - 1)
                at = 0
                for record in records:
                    n = record.shape[2]
                    sp.dma_start(rec[:, r, at:at + n],
                                 record[bass.ds(e, 1)].rearrange("o c n -> c (o n)")).then_inc(loaded[r], 16)
                    at += n
                sp.dma_start(xr[:, r].rearrange("t q r -> t (q r)"),
                             xd_dram[bass.ds(u * TILE, TILE), :].rearrange("(t q) r -> t (q r)", q=Q)).then_inc(loaded[r], 16)

            for r in range(RING):
                load(r, r)
            with sp.Fori(0, TILES // RING - 1) as i:
                for r in range(RING):
                    sp.wait_ge(yo_ready, RING * i + r + 1)
                    load(RING * (i + 1) + r, r)

        @block.tensor
        def _(pe):
            def turn(j, r, p, h, i):
                pe.wait_ge(loaded[r], (i + 1) * LOADS)
                pe.wait_ge(xt_copied, 2 * h)
                for q in range(Q):
                    ins = pe.transpose(bank[:, p, q * C:(q + 1) * C], xr[:, r, q, 0:C], w["ident"])
                ins.then_inc(turned, 1)

            def first(j, r, p, h, i):
                pe.wait_ge(xt_copied, j + 1)
                for f in range(4):
                    if not (isinstance(j, int) and j == 0):
                        if second:
                            pe.wait_ge(h_ready, (j - 1) * 4 + f + 1)
                        elif f % 2:
                            pe.wait_ge(h_ready, (j - 1) * 2 + f // 2 + 1)
                        else:
                            pe.wait_ge(gated, (j - 1) * 2 + f // 2 + 1)
                    ins = pe.matmul(bank[:, 2 + f, :], rec[:, r, f * C:(f + 1) * C], xt[:, p, :], start=True, stop=True)
                    ins.then_inc(g_ready if second or f % 2 == 0 else v_ready, 1)

            def finish(j, r, p, h, i):
                pe.wait_ge(h_ready, (j + 1) * NH)
                pe.wait_ge(y_copied, 2 * h)
                for q in range(Q):
                    for f in range(NH):
                        ins = pe.matmul(bank[:, 6 + p, q * C:(q + 1) * C], hidden[:, p, f, q * C:(q + 1) * C],
                                        rec[:, r, W2 + f * C:W2 + (f + 1) * C], start=(f == 0), stop=(f == NH - 1))
                ins.then_inc(y_ready, 1)

            over_tiles(pe, turn, first, finish)

        @block.scalar
        def _(act):
            def first(j, r, p, h, i):
                if not (isinstance(j, int) and j == 0):
                    act.wait_ge(y_ready, j - 1)
                for f in range(NH):
                    act.wait_ge(g_ready, j * NH + f + 1)
                    if second:
                        act.activation(hidden[:, p, f, :], bank[:, 2 + f, :], ACT.Gelu,
                                       bias=rec[:, r, FB + f:FB + f + 1]).then_inc(h_ready, 1)
                    else:
                        if f == 0:
                            act.wait_ge(h_ready, j * 2)
                        act.activation(gate[:, f, :], bank[:, 2 + 2 * f, :], ACT.Silu,
                                       bias=rec[:, r, FB + 2 * f:FB + 2 * f + 1]).then_inc(gated, 1)

            over_tiles(act, nothing, first, nothing)

        @block.vector
        def _(dve):
            def turn(j, r, p, h, i):
                dve.wait_ge(turned, j + 1)
                dve.tensor_copy(xt[:, p, :], bank[:, p, :]).then_inc(xt_copied, 1)

            def first(j, r, p, h, i):
                if not second:
                    if not (isinstance(j, int) and j == 0):
                        dve.wait_ge(y_ready, j - 1)
                    for f in range(2):
                        dve.wait_ge(gated, j * 2 + f + 1)
                        dve.wait_ge(v_ready, j * 2 + f + 1)
                        dve.scalar_tensor_tensor(out=hidden[:, p, f, :], in0=bank[:, 3 + 2 * f, :],
                                                 scalar=rec[:, r, FB + 2 * f + 1:FB + 2 * f + 2], in1=gate[:, f, :],
                                                 op0=ALU.add, op1=ALU.mult).then_inc(h_ready, 1)

            def finish(j, r, p, h, i):
                dve.wait_ge(y_ready, j + 1)
                dve.tensor_tensor(y1[:, p], bank[:, 6 + p, :].rearrange("t (q c) -> t q c", q=Q),
                                  rec[:, r, B2:B2 + C].unsqueeze(1).to_broadcast([C, Q, C]), ALU.add).then_inc(y_copied, 1)
                dve.wait_ge(sent[p], h * (16 * Q))
                dve.tensor_scalar(places[:, p], xr[:, r, :, C + 1], 0.0, None, ALU.add)
                dve.wait_ge(y_copied, j + 1)
                dve.tensor_tensor(yo[:, p], y1[:, p], xr[:, r, :, C:C + 1].to_broadcast([C, Q, C]), ALU.mult).then_inc(yo_ready, 1)

            over_tiles(dve, turn, first, finish)

        @block.gpsimd
        def _(pool):
            with pool.Fori(0, TILES // 2) as i:
                for p in range(2):
                    pool.wait_ge(yo_ready, 2 * i + p + 1)
                    pool.sem_inc(fence, 1)
                    for q in range(Q):
                        pool.indirect_dma_start(yd_dram, bass.IndirectOffsetOnAxis(places[:, p, q:q + 1], 0),
                                                yo[:, p, q, :], None).then_inc(sent[p], 16)
            for p in range(2):
                pool.wait_ge(sent[p], TILES // 2 * 16 * Q)


def combine(nc, sb, sem, bank, w, X, yd_dram, out):
    DEPTH = 4
    y = sb("y", [C, DEPTH, 2, Q * C], F32)
    total = sb("total", [C, 2, Q * C], F32)
    loaded = [sem(f"loaded{r}") for r in range(DEPTH)]
    summed, turned, added, stored = sem("summed"), sem("turned"), sem("added"), sem("stored")
    ROUNDS = TOKENS // TILE // DEPTH

    with nc.Block() as block:
        @block.sync
        def _(sp):
            def load(t, r):
                for c in range(2):
                    src = yd_dram[bass.ds(t * TILE + c * TOKENS, TILE), :].rearrange("(t q) c -> t (q c)", q=Q)
                    sp.dma_start(y[:, r, c, :], src).then_inc(loaded[r], 16)

            for r in range(DEPTH):
                load(r, r)
            with sp.Fori(0, ROUNDS - 1) as i:
                for r in range(DEPTH):
                    sp.wait_ge(summed, DEPTH * i + r + 1)
                    load(DEPTH * (i + 1) + r, r)

        @block.vector
        def _(dve):
            def add_up(t, r, i):
                dve.wait_ge(loaded[r], (i + 1) * 32)
                dve.wait_ge(turned, t - r % 2)
                dve.tensor_tensor(total[:, r % 2, :], y[:, r, 0, :], y[:, r, 1, :], ALU.add).then_inc(summed, 1)

            def add(t, r):
                dve.wait_ge(turned, t + 1)
                tokens = X[:, bass.ds(t * TILE, TILE)].rearrange("c (t q) -> c q t", q=Q)
                dve.tensor_tensor(tokens, tokens, bank[:, r, :].rearrange("c (q t) -> c q t", q=Q),
                                  ALU.add).then_inc(added, 1)

            with dve.Fori(0, ROUNDS) as i:
                for r in range(0, DEPTH, 2):
                    for u in (r, r + 1):
                        add_up(DEPTH * i + u, u, i)
                    for u in (r, r + 1):
                        add(DEPTH * i + u, u)

        @block.tensor
        def _(pe):
            with pe.Fori(0, ROUNDS) as i:
                for r in range(DEPTH):
                    pe.wait_ge(summed, DEPTH * i + r + 1)
                    pe.wait_ge(added, DEPTH * i)
                    for q in range(Q):
                        ins = pe.transpose(bank[:, r, q * C:(q + 1) * C], total[:, r % 2, q * C:(q + 1) * C], w["ident"])
                    ins.then_inc(turned, 1)

        @block.gpsimd
        def _(pool):
            if out is None:
                return
            for b in range(B):
                pool.wait_ge(added, 2 * b + 2)
                pool.dma_start(out[b], X[:, b * T:(b + 1) * T]).then_inc(stored, 16)
            pool.wait_ge(stored, 16 * B)


W1_COLS, WGV_COLS = 2 * C, 2 * 4 * C


def load_and_fold(nc, sb, sem, bank, w, weights_dram, x_dram, X, fold_dram, folded):
    src = sb("src", [C, E, W1_COLS + WGV_COLS + 6], F32)
    w1t = sb("w1t", [C, 2, 2, C], F32)
    rec = sb("rec", [C, E, 4 * C + 4], F32)
    loaded = [sem(f"loaded{e}") for e in range(E)]
    turned, copied, product, biases = sem("turned"), sem("copied"), sem("product"), sem("biases")
    product_copied, biases_added, stored = sem("product_copied"), sem("biases_added"), sem("stored")

    def w1(e, k):
        return src[:, e, k * C:(k + 1) * C]

    def wgv(e, k):
        return src[:, e, W1_COLS + k * 4 * C:W1_COLS + (k + 1) * 4 * C]

    with nc.Block() as block:
        @block.sync
        def _(sp):
            sp.dma_start(w.all[:], weights_dram).then_inc(w.loaded, 16)
            for e in range(E):
                sp.dma_start(src[:, e], fold_dram[e]).then_inc(loaded[e], 16)
            for b in range(B):
                sp.dma_start(X[:, b * T:(b + 1) * T], x_dram[b]).then_inc(w.x_loaded[b], 16)

        @block.tensor
        def _(pe):
            pe.wait_ge(w.loaded, 16)

            def turn(e):
                pe.wait_ge(loaded[e], 16)
                if e >= 2:
                    pe.wait_ge(copied, e - 1)
                for k in range(2):
                    ins = pe.transpose(bank[:, e % 2, k * C:(k + 1) * C], w1(e, k), w["ident"])
                ins.then_inc(turned, 1)

            turn(0)
            for e in range(E):
                if e + 1 < E:
                    turn(e + 1)
                if e >= 2:
                    pe.wait_ge(biases_added, e - 1)
                for f in range(4):
                    for k in range(2):
                        ins = pe.matmul(bank[:, 4 + e % 2, f:f + 1], wgv(e, k)[:, f * C:(f + 1) * C],
                                        src[:, e, W1_COLS + WGV_COLS + k:W1_COLS + WGV_COLS + k + 1],
                                        start=(k == 0), stop=(k == 1))
                ins.then_inc(biases, 1)
                pe.wait_ge(copied, e + 1)
                for k in range(2):
                    ins = pe.matmul(bank[:, 2 + e % 2, :], w1t[:, e % 2, k, :], wgv(e, k), start=(k == 0), stop=(k == 1))
                ins.then_inc(product, 1)

        @block.vector
        def _(dve):
            dve.memset(w.ones, 1.0)
            dve.wait_ge(w.loaded, 16)
            dve.tensor_copy(w.before, w["before_f"]).then_inc(w.cast, 1)

            def copy_turned(e):
                dve.wait_ge(turned, e + 1)
                if e >= 2:
                    dve.wait_ge(product, e - 1)
                dve.tensor_copy(w1t[:, e % 2].rearrange("h k d -> h (k d)"), bank[:, e % 2, 0:2 * C]).then_inc(copied, 1)

            copy_turned(0)
            for e in range(E):
                if e + 1 < E:
                    copy_turned(e + 1)
                dve.wait_ge(product, e + 1)
                dve.tensor_copy(rec[:, e, 0:4 * C], bank[:, 2 + e % 2, :]).then_inc(product_copied, 1)
                dve.wait_ge(biases, e + 1)
                dve.tensor_tensor(rec[:, e, 4 * C:4 * C + 4], bank[:, 4 + e % 2, 0:4],
                                  src[:, e, W1_COLS + WGV_COLS + 2:W1_COLS + WGV_COLS + 6], ALU.add).then_inc(biases_added, 1)
            dve.wait_ge(w.cast, 1)

        @block.scalar
        def _(act):
            load_tables(nc, act, LN_EXP_TABLES)
            for e in range(E):
                act.wait_ge(product_copied, e + 1)
                act.wait_ge(biases_added, e + 1)
                act.dma_start(folded[e], rec[:, e]).then_inc(stored, 16)
            act.wait_ge(stored, E * 16)


SIDE = 32
TAPS = 5
PAD = TAPS // 2
WIDE = SIDE + 2 * PAD


def multiscale_attention(nc, sb, sem, bank, w, X):
    xc = sb("xc", [C, T], F32)
    sq = sb("sq", [C, T], F32)
    rs = sb("rs", [C, T], F32)
    xn = sb("xn", [C, T], F32)
    pads = [sb(f"pad_{s}", [C, 2, WIDE, WIDE], F32) for s in "qkv"]
    dw = sb("dw", [C, 2, 2, T], F32)
    av = sb("av", [C, T], F32)
    qr = sb("qr", [C, 2, T], F32)
    kT = sb("kT", [C, 2, TC, C], F32)
    vT = sb("vT", [C, 2, TC, C + 1], F32)
    vk = sb("vk", [C, 2, C + 1], F32)
    vkm = sb("vkm", [C, 2, C], F32)
    ksm = sb("ksm", [C, 2, C], F32)
    rd = sb("rd", [C, 4, HALF], F32)
    o = sb("o", [C, 4, HALF], F32)
    yb = sb("yb", [C, 2, HALF], F32)
    taps = sb("taps", [C, TAPS * TAPS, C], F32)
    inv = sb("inv", [C, 1], F32)
    shift = sb("shift", [C, 1], F32)
    bn_log = sb("bn_log", [C, 1], F32)
    cleared, bn_step, taps_ready, bn_ready = sem("cleared"), sem("bn_step"), sem("taps_ready"), sem("bn_ready")
    centred, copied, squared, var_ready, logged = sem("centred"), sem("copied"), sem("squared"), sem("var_ready"), sem("logged")
    rstd_ready, xn_ready, qkv_ready, padded = sem("rstd_ready"), sem("xn_ready"), sem("qkv_ready"), sem("padded")
    kv_ready, kv_copied, dw_step, av_ready, av_copied = sem("kv_ready"), sem("kv_copied"), sem("dw_step"), sem("av_ready"), sem("av_copied")
    av_turned, vt_copied, qa_ready, qa_copied = sem("av_turned"), sem("vt_copied"), sem("qa_ready"), sem("qa_copied")
    ka_ready, ka_copied, vk_ready, vk_copied, masked = sem("ka_ready"), sem("ka_copied"), sem("vk_ready"), sem("vk_copied"), sem("masked")
    num_ready, den_logged, rden_ready, o_ready = sem("num_ready"), sem("den_logged"), sem("rden_ready"), sem("o_ready")
    q0_ready, proj_ready, y_ready, added = sem("q0_ready"), sem("proj_ready"), sem("y_ready"), sem("added")
    NT = TAPS * TAPS
    VK = (0, 1)
    NUM = ((0, 1), (2, 3), (4, 5), (0, 1))
    PROJ = (2, 3)

    def half(n):
        return slice(n * HALF, (n + 1) * HALF)

    def window(s, p, tap, n=None):
        dy, dx = tap // TAPS, tap % TAPS
        r0, r = (dy, SIDE) if n is None else (dy + n * SIDE // 2, SIDE // 2)
        return pads[s][:, p, r0:r0 + r, dx:dx + SIDE]

    def over_images(eng, step):
        step(None, None, 0, 1)
        step(0, None, 1, 0)
        with eng.Fori(0, B // 2 - 1) as i:
            step(2 * i + 1, 2 * i, 2 * i + 2, 1)
            step(2 * i + 2, 2 * i + 1, 2 * i + 3, 0)
        step(B - 1, B - 2, None, 1)
        step(None, B - 1, None, 0)

    with nc.Block() as block:
        @block.tensor
        def _(pe):
            def step(b, pb, nb, p):
                tapped = [0]

                def take(count):
                    if b is None:
                        return
                    for tap in range(tapped[0], tapped[0] + count):
                        for n in range(2):
                            ins = pe.matmul(bank[:, 6 + n, :], taps[:, tap, :], window(2, p, tap, n),
                                            start=(tap == 0), stop=(tap == NT - 1))
                    tapped[0] += count
                    if tapped[0] == NT:
                        ins.then_inc(av_ready, 1)

                if pb is not None:
                    pe.wait_ge(padded, (pb + 1 if b is None else pb + 2) * 6)
                    pe.wait_ge(dw_step, (pb + 1) * 2 * NT)
                    for n in range(2):
                        pe.matmul(bank[:, 2 + n, :], w["c_pw"][:, 0:C], dw[:, 1 - p, 0, half(n)],
                                  start=True, stop=True).then_inc(qa_ready, 1)
                    for n in range(2):
                        for q in range(4):
                            c = 4 * n + q
                            ins = pe.matmul(bank[:, 4 + n, q * C:(q + 1) * C], dw[:, 1 - p, 1, c * C:(c + 1) * C],
                                            w["c_pw"][:, C:2 * C], start=True, stop=True)
                        ins.then_inc(ka_ready, 1)
                    pe.wait_ge(av_copied, pb * 2 + 2)
                    for n in range(2):
                        for q in range(4):
                            c = 4 * n + q
                            ins = pe.transpose(bank[:, n, q * C:(q + 1) * C], av[:, c * C:(c + 1) * C], w["ident"])
                        ins.then_inc(av_turned, 1)
                if b is not None:
                    if pb is None:
                        pe.wait_ge(taps_ready, NT)
                    pe.wait_ge(padded, b * 6 + 6)
                take(3)
                if pb is not None:
                    pe.wait_ge(kv_copied, pb * 8 + 8)
                    pe.wait_ge(vt_copied, pb * 2 + 2)
                    pe.wait_ge(ka_copied, pb * 2 + 2)
                    for m in range(2):
                        for c in range(TC):
                            ins = pe.matmul(bank[:, VK[m], 0:C + 1], kT[:, m, c, :], vT[:, m, c, :],
                                            start=(c == 0), stop=(c == TC - 1))
                        ins.then_inc(vk_ready, 1)
                if b is not None:
                    if pb is not None:
                        pe.wait_ge(qa_copied, pb * 2 + 2)
                    for u in range(4):
                        for c in (2 * u, 2 * u + 1):
                            ins = pe.matmul(bank[:, 2 + u, c % 2 * 2 * C:(c % 2 + 1) * 2 * C], xn[:, c * C:(c + 1) * C],
                                            w["c_qkv"][:, C:3 * C], start=True, stop=True)
                        ins.then_inc(kv_ready, 1)
                take(2)
                for m in range(2):
                    if pb is not None:
                        pe.wait_ge(masked, pb * 2 + 2)
                        if m == 0:
                            pe.wait_ge(q0_ready, pb + 1)
                        if b is not None:
                            pe.wait_ge(kv_copied, b * 8 + 4 + 4 * m)
                        for n in range(2):
                            if (m, n) == (1, 1):
                                pe.wait_ge(o_ready, pb * 4 + 1)
                            num, den = NUM[2 * m + n]
                            q = qr[:, m, half(n)]
                            pe.matmul(bank[:, num, :], vkm[:, m, :], q, start=True, stop=True)
                            pe.matmul(bank[:, den, :], ksm[:, m, :], q, start=True, stop=True).then_inc(num_ready, 1)
                    take((2, 3)[m])
                if pb is not None:
                    for n in range(2):
                        pe.wait_ge(o_ready, pb * 4 + 3 + n)
                        for m in range(2):
                            ins = pe.matmul(bank[:, PROJ[n], :], w["c_proj"][:, m * C:(m + 1) * C], o[:, 2 * m + n, :],
                                            start=(m == 0), stop=(m == 1))
                        ins.then_inc(proj_ready, 1)
                if nb is not None:
                    if b is not None:
                        pe.wait_ge(kv_copied, b * 8 + 8)
                    for n in range(2):
                        pe.matmul(bank[:, 4 + n, :], w["centre"], X[:, bass.ds(nb * T + n * HALF, HALF)],
                                  start=True, stop=True).then_inc(centred, 1)
                take(3)
                if nb is not None:
                    for n in range(2):
                        pe.wait_ge(squared, nb * 2 + n + 1)
                        pe.matmul(bank[:, n, :], w["mean"], sq[:, half(n)], start=True, stop=True).then_inc(var_ready, 1)
                take(4)
                if nb is not None:
                    pe.wait_ge(xn_ready, nb * 2 + 2)
                    if pb is not None:
                        pe.wait_ge(y_ready, pb * 2 + 2)
                    for s, slot in enumerate((2, 4, 0)):
                        for n in range(2):
                            pe.matmul(bank[:, slot + n, :], w["c_qkv"][:, s * C:(s + 1) * C], xn[:, half(n)],
                                      start=True, stop=True).then_inc(qkv_ready, 1)
                take(NT - tapped[0])

            over_images(pe, step)

        @block.scalar
        def _(act):
            load_tables(nc, act, LN_EXP_TABLES)
            act.wait_ge(bn_step, 1)
            act.activation(bn_log[:], w["bn"][:, 3:4], ACT.Ln, bias=w["eps"][:, 1:2]).then_inc(bn_step, 1)
            act.wait_ge(bn_step, 2)
            act.activation(bn_log[:], bn_log[:], ACT.Exp, scale=-0.5).then_inc(bn_step, 1)

            def step(b, pb, nb, p):
                if pb is not None:
                    act.wait_ge(av_ready, pb + 1)
                    act.wait_ge(av_turned, pb * 2)
                    for n in range(2):
                        act.activation(av[:, half(n)], bank[:, 6 + n, :], ACT.Copy).then_inc(av_copied, 1)
                    act.wait_ge(vk_ready, pb * 2)
                    for n in range(2):
                        act.wait_ge(qa_ready, pb * 2 + n + 1)
                        act.activation(qr[:, 1, half(n)], bank[:, 2 + n, :], ACT.Relu).then_inc(qa_copied, 1)
                    for n in range(2):
                        act.wait_ge(ka_ready, pb * 2 + n + 1)
                        act.activation(kT[:, 1, 4 * n:4 * n + 4, :].rearrange("t c e -> t (c e)"), bank[:, 4 + n, :],
                                       ACT.Relu).then_inc(ka_copied, 1)
                    for n in range(2):
                        act.wait_ge(av_turned, pb * 2 + n + 1)
                        act.activation(vT[:, 1, 4 * n:4 * n + 4, 0:C], bank[:, n, :].rearrange("t (c e) -> t c e", c=4),
                                       ACT.Copy).then_inc(vt_copied, 1)
                if b is not None:
                    if pb is not None:
                        act.wait_ge(vk_ready, pb * 2 + 1)
                    for u in range(4):
                        act.wait_ge(kv_ready, b * 4 + u + 1)
                        src = bank[:, 2 + u, :].rearrange("t (c s e) -> t c s e", c=2, s=2)
                        act.activation(kT[:, 0, 2 * u:2 * u + 2, :], src[:, :, 0, :], ACT.Relu).then_inc(kv_copied, 1)
                        act.activation(vT[:, 0, 2 * u:2 * u + 2, 0:C], src[:, :, 1, :], ACT.Copy).then_inc(kv_copied, 1)
                if pb is not None:
                    act.wait_ge(o_ready, pb * 4)
                    for m in range(4):
                        act.wait_ge(num_ready, pb * 4 + m + 1)
                        act.activation(rd[:, m, :], bank[:, NUM[m][1], :], ACT.Ln, bias=w["eps"][:, 3:4]).then_inc(den_logged, 1)
                        act.wait_ge(den_logged, pb * 4 + m + 1)
                        act.activation(rd[:, m, :], rd[:, m, :], ACT.Exp, scale=-1.0).then_inc(rden_ready, 1)
                if b is not None:
                    act.wait_ge(padded, b * 6 + 2)
                    act.activation(qr[:, 0, :].rearrange("c (y x) -> c y x", x=SIDE),
                                   pads[0][:, p, PAD:PAD + SIDE, PAD:PAD + SIDE], ACT.Relu).then_inc(q0_ready, 1)
                if pb is not None:
                    act.wait_ge(bn_ready, 1)
                    act.wait_ge(added, pb * 2)
                    for n in range(2):
                        act.wait_ge(proj_ready, pb * 2 + n + 1)
                        act.activation(yb[:, n, :], bank[:, PROJ[n], :], ACT.Identity, scale=inv[:, 0:1],
                                       bias=shift[:, 0:1]).then_inc(y_ready, 1)
                if nb is not None:
                    act.wait_ge(var_ready, nb * 2)
                    for n in range(2):
                        act.wait_ge(copied, nb * 2 + n + 1)
                        act.activation(sq[:, half(n)], xc[:, half(n)], ACT.Square).then_inc(squared, 1)
                    for n in range(2):
                        act.wait_ge(var_ready, nb * 2 + n + 1)
                        act.activation(rs[:, half(n)], bank[:, n, :], ACT.Ln, bias=w["eps"][:, 0:1]).then_inc(logged, 1)
                    for n in range(2):
                        act.wait_ge(logged, nb * 2 + n + 1)
                        act.activation(rs[:, half(n)], rs[:, half(n)], ACT.Exp, scale=-0.5).then_inc(rstd_ready, 1)
                    if b is None:
                        act.wait_ge(cleared, 4)
                    if pb is not None:
                        act.wait_ge(dw_step, (pb + 1) * 2 * NT)
                    for s, slot in enumerate((2, 4, 0)):
                        for n in range(2):
                            act.wait_ge(qkv_ready, nb * 6 + 2 * s + n + 1)
                            rows = slice(PAD + n * SIDE // 2, PAD + (n + 1) * SIDE // 2)
                            act.activation(pads[s][:, 1 - p, rows, PAD:PAD + SIDE],
                                           bank[:, slot + n, :].rearrange("c (y x) -> c y x", x=SIDE), ACT.Copy).then_inc(padded, 1)

            over_images(act, step)

        @block.vector
        def _(dve):
            dve.memset(vT[:], 1.0).then_inc(cleared, 1)
            dve.engine_nop().then_inc(bn_step, 1)
            dve.wait_ge(bn_step, 3)
            dve.tensor_tensor(inv[:], w["bn"][:, 0:1], bn_log[:], ALU.mult).then_inc(bn_step, 1)
            dve.wait_ge(bn_step, 4)
            dve.tensor_tensor(shift[:], w["bn"][:, 2:3], inv[:], ALU.mult).then_inc(bn_step, 1)
            dve.wait_ge(bn_step, 5)
            dve.tensor_tensor(shift[:], w["bn"][:, 1:2], shift[:], ALU.subtract).then_inc(bn_ready, 1)

            def step(b, pb, nb, p):
                tapped = [0]

                def take(until):
                    if b is None:
                        return
                    for product in range(tapped[0], until):
                        tap, s = product // 2, product % 2
                        plane = dw[:, p, s, :].rearrange("c (y x) -> c y x", x=SIDE)
                        weight = w["c_dw"][:, s * NT + tap:s * NT + tap + 1]
                        if tap == 0:
                            dve.tensor_scalar(plane, window(s, p, tap), weight, None, ALU.mult).then_inc(dw_step, 1)
                        else:
                            dve.wait_ge(dw_step, b * 2 * NT + product - 1)
                            dve.scalar_tensor_tensor(out=plane, in0=window(s, p, tap), scalar=weight, in1=plane,
                                                     op0=ALU.mult, op1=ALU.add).then_inc(dw_step, 1)
                    tapped[0] = until

                if b is not None:
                    dve.wait_ge(padded, b * 6 + 4)
                    if pb is not None:
                        dve.wait_ge(ka_ready, pb * 2)
                take(13)
                if pb is not None:
                    dve.wait_ge(num_ready, pb * 4)
                    for m in range(2):
                        dve.wait_ge(vk_ready, pb * 2 + m + 1)
                        dve.tensor_copy(vk[:, m, :], bank[:, VK[m], 0:C + 1]).then_inc(vk_copied, 1)
                    for m in range(2):
                        dve.wait_ge(vk_copied, pb * 2 + m + 1)
                        dve.tensor_tensor(vkm[:, m, :], vk[:, m, 0:C], w["heads"], ALU.mult)
                        dve.tensor_scalar(ksm[:, m, :], w["heads"], vk[:, m, C:C + 1], None, ALU.mult).then_inc(masked, 1)
                for m in range(4):
                    if m == 0:
                        take(21)
                    if m == 2:
                        take(27)
                    if pb is not None:
                        if m == 0:
                            dve.wait_ge(proj_ready, pb * 2)
                        dve.wait_ge(rden_ready, pb * 4 + m + 1)
                        dve.tensor_tensor(o[:, m, :], bank[:, NUM[m][0], :], rd[:, m, :], ALU.mult).then_inc(o_ready, 1)
                take(32)
                if pb is not None:
                    for n in range(2):
                        dve.wait_ge(y_ready, pb * 2 + n + 1)
                        cols = X[:, bass.ds(pb * T + n * HALF, HALF)]
                        dve.tensor_tensor(cols, cols, yb[:, n, :], ALU.add).then_inc(added, 1)
                if nb is not None:
                    for n in range(2):
                        dve.wait_ge(centred, nb * 2 + n + 1)
                        dve.tensor_copy(xc[:, half(n)], bank[:, 4 + n, :]).then_inc(copied, 1)
                take(38)
                if nb is not None:
                    if b is not None:
                        dve.wait_ge(kv_ready, b * 4 + 4)
                    for n in range(2):
                        dve.wait_ge(rstd_ready, nb * 2 + n + 1)
                        dve.tensor_tensor(xn[:, half(n)], xc[:, half(n)], rs[:, half(n)], ALU.mult).then_inc(xn_ready, 1)
                if b is None and nb is not None:
                    for tap in range(NT):
                        dve.tensor_scalar(taps[:, tap, :], w["c_pw"][:, 2 * C:3 * C], w["c_dw"][:, 2 * NT + tap:2 * NT + tap + 1],
                                          None, ALU.mult).then_inc(taps_ready, 1)
                take(2 * NT)

            over_images(dve, step)

        @block.gpsimd
        def _(pool):
            for pad in pads:
                pool.memset(pad[:], 0.0).then_inc(cleared, 1)




def metaformer(nc, x_in, columns, weights, to_fold, rest0, rec1, out):
    names = [0]

    def allocator(ctx, make):
        def allocate(name, *args):
            names[0] += 1
            return ctx.enter_context(make(f"{name}_{names[0]}", *args))
        return allocate

    def stage(run, *args):
        signals = []

        def own_sem(name):
            names[0] += 1
            signals.append(nc.alloc_semaphore(name=f"{name}_{names[0]}"))
            return signals[-1]

        with ExitStack() as own:
            run(nc, allocator(own, nc.sbuf_tensor), own_sem, bank, w, *args)
        nc.clear_and_free_semaphores(signals)
        nc.all_engine_barrier()

    parts_dram = nc.dram_tensor("qk_parts", (B, 2, 3, C, T), BF16).ap()
    v_dram = nc.dram_tensor("v_turned", (B, C, TC * HEADS * VH), F32).ap()
    folded = nc.dram_tensor("folded", (E, C, 4 * C + 4), F32).ap()
    xd_dram = [nc.dram_tensor(f"dispatched{n}", (UNITS_XD * TILE, ROW), F32).ap() for n in range(2)]
    yd_dram = [nc.dram_tensor(f"results{n}", (SPARE + BLANKS * TILE, C), F32).ap() for n in range(2)]

    with ExitStack() as ctx:
        sb, sem = allocator(ctx, nc.sbuf_tensor), allocator(ctx, nc.semaphore)
        bank = ctx.enter_context(nc.psum_tensor("bank", [C, 8, HALF], F32))
        w = Weights(nc, sb, sem, columns)
        X = sb("X", [C, TOKENS], F32)
        table = sb("table", [C, 2, TILES], mybir.dt.int32)
        stage(load_and_fold, weights, x_in, X, to_fold, folded)
        with ExitStack() as own:
            XF = allocator(own, nc.sbuf_tensor)("XF", [C, TOKENS], F32)
            stage(normalize_and_project, X, XF, parts_dram, v_dram)
            stage(attention, X, XF, parts_dram, v_dram)
        stage(route, X, 0, xd_dram[0], table)
        stage(experts, 0, xd_dram[0], yd_dram[0], table, [folded, rest0])
        stage(combine, X, yd_dram[0], None)
        stage(multiscale_attention, X)
        stage(route, X, 1, xd_dram[1], table)
        stage(experts, 1, xd_dram[1], yd_dram[1], table, [rec1])
        stage(combine, X, yd_dram[1], out)


def small_tensors(I):
    f4 = np.float32
    eye = np.eye(C, dtype=f4)
    lane = np.arange(C)
    qkv, qkv_b, proj = I["L0_conv_qkv_w"], I["L0_conv_qkv_b"], I["L0_conv_proj_w"]
    wv = np.zeros((C, HEADS, VH), f4)
    wv[:, :, :CH] = qkv[2 * C:].T.reshape(C, HEADS, CH)
    bv = np.ones((C, 2, HEADS, VH), f4)
    bv[:, :, :, :CH] = qkv_b[2 * C:].reshape(1, 1, HEADS, CH)
    proj_heads = np.zeros((2, HEADS // 2, VH, C), f4)
    proj_heads[:, :, :CH] = proj.T.reshape(2, HEADS // 2, CH, C)
    row_ids = np.zeros((C, G, 2), f4)
    row_ids[:] = lane[:, None, None] + C * np.arange(G)[:, None] + TOKENS * np.arange(2)
    blank_rows = SPARE + TILE * np.arange(BLANKS)[:, None] + Q * lane[:, None, None] + np.arange(Q)
    chunks = np.arange(3 * C).reshape(HEADS, 3, CH).transpose(1, 0, 2).reshape(-1)
    pw = I["L1_conv_w_pw"][:, :, 0, 0][chunks].reshape(3, C // 8, 8, 8)
    c_pw = np.zeros((3, C // 8, 8, C // 8, 8), f4)
    for g in range(C // 8):
        c_pw[:, g, :, g, :] = pw[:, g].transpose(0, 2, 1)
    w = dict(
        ident=eye, centre=eye - f4(1 / C), mean=np.full((C, C), 1 / C), before_f=np.triu(np.ones((C, C)), 1),
        group=np.kron(np.eye(C // 4), np.full((4, 4), 0.25)), eps=np.tile([1e-6, 1e-5, 1e-10, 1e-15], (C, 1)),
        wqk=qkv[:2 * C].T, wv=wv.reshape(C, -1), bqk=qkv_b[:2 * C].reshape(2, C).T, bv=bv.reshape(C, -1),
        gn=np.stack([I["L0_conv_gn_w"], I["L0_conv_gn_b"]], 1), wproj=proj.T,
        wproj_heads=proj_heads.reshape(2, C, C).transpose(1, 0, 2).reshape(C, -1), bproj=I["L0_conv_proj_b"].reshape(C, 1),
        moe0_router=I["L0_ffn_router_w"], moe0_router_bias=np.tile(I["L0_ffn_router_b"], (C, G)),
        moe1_router=I["L1_ffn_gate_w"], moe1_router_bias=np.zeros((C, G * E)),
        ln=np.stack([I["L1_ffn_ln_g"], I["L1_ffn_ln_b"]], 1), firstness=np.tile(np.arange(E, 0, -1), (C, G)),
        region=np.tile(np.arange(E) * REGION * TILE, (C, 1)), row_ids=row_ids.reshape(C, -1),
        k_tile=np.tile(np.arange(TOKENS // TILE) * TILE, (C, E)), tile_no=np.tile(np.arange(TILES), (C, 1)),
        zeros=np.zeros((C, E)), blank_rows=blank_rows.reshape(C, -1),
        c_qkv=I["L1_conv_w_qkv"][:, :, 0, 0][chunks].T,
        c_dw=I["L1_conv_w_dw"].reshape(3 * C, -1)[chunks].reshape(3, C, -1).transpose(1, 0, 2).reshape(C, -1),
        c_pw=c_pw.reshape(3, C, C).transpose(1, 0, 2).reshape(C, -1),
        c_proj=I["L1_conv_w_proj"][:, :, 0, 0].T.reshape(2, C, C).transpose(1, 0, 2).reshape(C, -1),
        bn=np.stack([I["L1_conv_bn_" + n] for n in ("gamma", "beta", "mean", "var")], 1),
        heads=np.kron(np.eye(HEADS), np.ones((CH, CH))))
    return {k: np.ascontiguousarray(v, f4) for k, v in w.items()}


def expert_tensors(I):
    def interleaved(g, v):
        g, v = (a.reshape(a.shape[:-1] + (2, 1, C)) for a in (g, v))
        return np.concatenate([g, v], -2).reshape(g.shape[:-3] + (4, C))

    def down(w2, b2, n):
        blocks = w2.reshape(E, n, C, C).transpose(0, 2, 1, 3).reshape(E, C, n * C)
        return np.concatenate([blocks, np.broadcast_to(b2[:, None, :], (E, C, C))], 2)

    b = np.concatenate([I["L0_ffn_b1"].reshape(E, 2, C), interleaved(I["L0_ffn_bg"], I["L0_ffn_bv"])], 1)
    wgv = interleaved(I["L0_ffn_wg"], I["L0_ffn_wv"]).reshape(E, 2, C, 4 * C).transpose(0, 2, 1, 3).reshape(E, C, -1)
    big = dict(
        to_fold=np.concatenate([I["L0_ffn_w1"], wgv, b.transpose(0, 2, 1)], 2), rest0=down(I["L0_ffn_w2"], I["L0_ffn_b2"], 2),
        rec1=np.concatenate([I["L1_ffn_w1"], I["L1_ffn_b1"].reshape(E, 4, C).transpose(0, 2, 1),
                             down(I["L1_ffn_w2"], I["L1_ffn_b2"], 4)], 2))
    return {k: np.ascontiguousarray(v, np.float32) for k, v in big.items()}


def kernel(**inputs):
    import concourse.bacc as bacc
    from concourse.bass_utils import run_bass_kernel_spmd

    I = {k: np.asarray(v) for k, v in inputs.items()}
    nc = bacc.Bacc("TRN2", target_bir_lowering=False, num_devices=1)
    arrays = {}

    def declare(name, a):
        arrays[name] = a
        return nc.dram_tensor(name, a.shape, F32, kind="ExternalInput").ap()

    x_in = declare("x", np.ascontiguousarray(I["x"].reshape(B, C, T)))
    small = small_tensors(I)
    columns = {k: v.shape[1] for k, v in small.items()}
    weights = declare("weights", np.concatenate(list(small.values()), 1))
    big = {k: declare("e_" + k, v) for k, v in expert_tensors(I).items()}
    out = nc.dram_tensor("out", (B, C, T), F32, kind="ExternalOutput").ap()
    metaformer(nc, x_in, columns, weights, big["to_fold"], big["rest0"], big["rec1"], out)
    r = run_bass_kernel_spmd(nc, [arrays], core_ids=[0])
    return r.results[0]["out"].reshape(I["x"].shape)
```
